# Optimizing a Trainium2 kernel written in Bass

```python
import numpy as np
import jax
import jax.numpy as jnp

def _softmax(x, axis=-1):
    return jax.nn.softmax(x, axis=axis)

def _gelu(x):
    return jax.nn.gelu(x, approximate=True)

def _silu(x):
    return jax.nn.silu(x)

def _sigmoid(x):
    return jax.nn.sigmoid(x)

def _layernorm(x, axis=-1, eps=1e-05):
    m = jnp.mean(x, axis=axis, keepdims=True)
    v = jnp.var(x, axis=axis, keepdims=True)
    return (x - m) / jnp.sqrt(v + eps)

def _scatter_add(tgt, idx, src, axis=0):
    return tgt.at[idx].add(src)

def _segment_sum(src, seg, n):
    return jax.ops.segment_sum(src, seg, n)
kernel_name = 'mk_gnn_ffn_d2_gnn_r32_685603'

def setup_inputs(seed: int=0):
    np.random.seed(seed)
    _w = jnp.asarray

    def _rec_inputs():
        import jax
        import jax.numpy as jnp
        _gk = jax.random.key(seed)
        x = -0.0003713 + 1 * jax.random.normal(jax.random.fold_in(_gk, 1), (3125, 256), jnp.float32)
        src = jax.random.randint(jax.random.fold_in(_gk, 2), (50000,), 0, 3125, jnp.int32)
        dst = jax.random.randint(jax.random.fold_in(_gk, 3), (50000,), 0, 3125, jnp.int32)
        _o = jnp.argsort(dst, stable=True)
        src = src[_o]
        dst = dst[_o]
        edge_weight = jax.random.uniform(jax.random.fold_in(_gk, 13), (50000,), jnp.float32, 0.0, 1)
        return (x, src, dst, edge_weight)
    x, src, dst, edge_weight = _rec_inputs()

    def _L0_gnn_setup():
        import jax, jax.numpy as jnp
        import numpy as np
        N = 50000
        E = 25000
        D = 256
        H = 4
        F = D // H

        def gat_layer(x, src, dst, W, att_src, att_dst, bias):
            n = x.shape[0]
            h = (x @ W).reshape(n, H, F)
            a_src = jnp.sum(h * att_src[None], axis=-1)
            a_dst = jnp.sum(h * att_dst[None], axis=-1)
            e = jax.nn.leaky_relu(a_src[src] + a_dst[dst], 0.2)
            m = jax.ops.segment_max(e, dst, num_segments=n)
            m = jnp.where(jnp.isfinite(m), m, 0.0)
            ex = jnp.exp(e - m[dst])
            denom = jax.ops.segment_sum(ex, dst, num_segments=n)
            alpha = ex / (denom[dst] + 1e-16)
            msg = h[src] * alpha[..., None]
            out = jax.ops.segment_sum(msg, dst, num_segments=n)
            return out.reshape(n, H * F) + bias
        key = jax.random.key(seed)
        ks = jax.random.split(key, 8)
        x = jax.random.normal(ks[0], (N, D), dtype=jnp.float32)
        edge_index = jax.random.randint(ks[1], (2, E), 0, N, dtype=jnp.int32)
        W = jax.random.normal(ks[2], (D, H * F), dtype=jnp.float32) * (1.0 / np.sqrt(D))
        att_src = jax.random.normal(ks[3], (H, F), dtype=jnp.float32) * (1.0 / np.sqrt(F))
        att_dst = jax.random.normal(ks[4], (H, F), dtype=jnp.float32) * (1.0 / np.sqrt(F))
        bias = jnp.zeros((D,), dtype=jnp.float32)
        ln_gamma = jnp.ones((D,), dtype=jnp.float32)
        ln_beta = jnp.zeros((D,), dtype=jnp.float32)
        return {'x': x, 'edge_index': edge_index, 'W': W, 'att_src': att_src, 'att_dst': att_dst, 'bias': bias, 'ln_gamma': ln_gamma, 'ln_beta': ln_beta}
    _L0_gnn_all = _L0_gnn_setup()
    _L0_gnn_in = {k: v for k, v in _L0_gnn_all.items() if k in ('W', 'att_src', 'att_dst', 'bias', 'ln_gamma', 'ln_beta')}
    del _L0_gnn_all

    def _L0_ffn_setup():
        import jax, jax.numpy as jnp
        import numpy as np
        B, S, D = (8, 128, 256)
        H = 4 * D
        CAPACITY = 0.5
        key = jax.random.key(seed)
        ks = jax.random.split(key, 6)
        x = jax.random.normal(ks[0], (B, S, D), dtype=jnp.float32)
        attention_mask = jnp.zeros((B, 1, 1, S), dtype=jnp.float32)
        wr = jax.random.normal(ks[1], (D, 1), dtype=jnp.float32) * 0.02
        br = jnp.zeros((1,), dtype=jnp.float32)
        w1 = jax.random.normal(ks[2], (D, H), dtype=jnp.float32) * 0.02
        b1 = jnp.zeros((H,), dtype=jnp.float32)
        w2 = jax.random.normal(ks[3], (H, D), dtype=jnp.float32) * 0.02
        b2 = jnp.zeros((D,), dtype=jnp.float32)
        return {'x': x, 'attention_mask': attention_mask, 'wr': wr, 'br': br, 'w1': w1, 'b1': b1, 'w2': w2, 'b2': b2}
    _L0_ffn_all = _L0_ffn_setup()
    _L0_ffn_in = {k: v for k, v in _L0_ffn_all.items() if k in ('attention_mask', 'wr', 'br', 'w1', 'b1', 'w2', 'b2')}
    del _L0_ffn_all

    def _L1_gnn_setup():
        import jax, jax.numpy as jnp
        import numpy as np
        N = 3125
        E = 100000
        DI = 256
        DO = 256
        BN_EPS = 1e-05

        def _bn_relu(h, gamma, beta):
            mean = jnp.mean(h, axis=0)
            var = jnp.var(h, axis=0)
            hn = (h - mean) * jax.lax.rsqrt(var + BN_EPS)
            return jax.nn.relu(hn * gamma + beta)
        key = jax.random.key(seed)
        ks = jax.random.split(key, 6)
        x = jax.random.normal(ks[0], (N, DI), dtype=jnp.float32)
        edge_row = jax.random.randint(ks[1], (E,), 0, N, dtype=jnp.int32)
        edge_col = jax.random.randint(ks[2], (E,), 0, N, dtype=jnp.int32)
        edge_vals = jnp.ones((E,), dtype=jnp.float32)
        eps = jnp.zeros((1,), dtype=jnp.float32)
        W1 = jax.random.normal(ks[3], (DI, DO), dtype=jnp.float32) * 0.05
        b1 = jnp.zeros((DO,), dtype=jnp.float32)
        g1 = jnp.ones((DO,), dtype=jnp.float32)
        be1 = jnp.zeros((DO,), dtype=jnp.float32)
        W2 = jax.random.normal(ks[4], (DO, DO), dtype=jnp.float32) * 0.05
        b2 = jnp.zeros((DO,), dtype=jnp.float32)
        g2 = jnp.ones((DO,), dtype=jnp.float32)
        be2 = jnp.zeros((DO,), dtype=jnp.float32)
        return {'x': x, 'edge_row': edge_row, 'edge_col': edge_col, 'edge_vals': edge_vals, 'eps': eps, 'W1': W1, 'b1': b1, 'g1': g1, 'be1': be1, 'W2': W2, 'b2': b2, 'g2': g2, 'be2': be2}
    _L1_gnn_all = _L1_gnn_setup()
    _L1_gnn_in = {k: v for k, v in _L1_gnn_all.items() if k in ('eps', 'W1', 'b1', 'g1', 'be1', 'W2', 'b2', 'g2', 'be2')}
    del _L1_gnn_all

    def _L1_ffn_setup():
        import math
        import jax, jax.numpy as jnp
        import numpy as np
        CAPACITY_FACTOR = 1.25
        TOP_K = 2
        LN_EPS = 1e-05

        def _layer_norm(x, gamma, beta):
            mu = jnp.mean(x, axis=-1, keepdims=True)
            var = jnp.var(x, axis=-1, keepdims=True)
            return (x - mu) * jax.lax.rsqrt(var + LN_EPS) * gamma + beta
        key = jax.random.key(seed)
        ks = jax.random.split(key, 4)
        B, S, D, F, E = (8, 128, 256, 512, 8)
        x = jax.random.normal(ks[0], (B, S, D), dtype=jnp.float32)
        Wr = jax.random.normal(ks[1], (D, E), dtype=jnp.float32) / np.sqrt(D)
        br = jnp.zeros((E,), jnp.float32)
        W1 = jax.random.normal(ks[2], (E, D, F), dtype=jnp.float32) / np.sqrt(D)
        b1 = jnp.zeros((E, F), jnp.float32)
        W2 = jax.random.normal(ks[3], (E, F, D), dtype=jnp.float32) / np.sqrt(F)
        b2 = jnp.zeros((E, D), jnp.float32)
        gamma = jnp.ones((D,), jnp.float32)
        beta = jnp.zeros((D,), jnp.float32)
        return {'x': x, 'Wr': Wr, 'br': br, 'W1': W1, 'b1': b1, 'W2': W2, 'b2': b2, 'gamma': gamma, 'beta': beta}
    _L1_ffn_all = _L1_ffn_setup()
    _L1_ffn_in = {k: v for k, v in _L1_ffn_all.items() if k in ('Wr', 'br', 'W1', 'b1', 'W2', 'b2', 'gamma', 'beta')}
    del _L1_ffn_all
    return {'x': x, 'src': src, 'dst': dst, 'edge_weight': edge_weight, 'L0_gnn_W': _L0_gnn_in['W'], 'L0_gnn_att_src': _L0_gnn_in['att_src'], 'L0_gnn_att_dst': _L0_gnn_in['att_dst'], 'L0_gnn_bias': _L0_gnn_in['bias'], 'L0_gnn_ln_gamma': _L0_gnn_in['ln_gamma'], 'L0_gnn_ln_beta': _L0_gnn_in['ln_beta'], 'L0_ffn_attention_mask': _L0_ffn_in['attention_mask'], 'L0_ffn_wr': _L0_ffn_in['wr'], 'L0_ffn_br': _L0_ffn_in['br'], 'L0_ffn_w1': _L0_ffn_in['w1'], 'L0_ffn_b1': _L0_ffn_in['b1'], 'L0_ffn_w2': _L0_ffn_in['w2'], 'L0_ffn_b2': _L0_ffn_in['b2'], 'L1_gnn_eps': _L1_gnn_in['eps'], 'L1_gnn_W1': _L1_gnn_in['W1'], 'L1_gnn_b1': _L1_gnn_in['b1'], 'L1_gnn_g1': _L1_gnn_in['g1'], 'L1_gnn_be1': _L1_gnn_in['be1'], 'L1_gnn_W2': _L1_gnn_in['W2'], 'L1_gnn_b2': _L1_gnn_in['b2'], 'L1_gnn_g2': _L1_gnn_in['g2'], 'L1_gnn_be2': _L1_gnn_in['be2'], 'L1_ffn_Wr': _L1_ffn_in['Wr'], 'L1_ffn_br': _L1_ffn_in['br'], 'L1_ffn_W1': _L1_ffn_in['W1'], 'L1_ffn_b1': _L1_ffn_in['b1'], 'L1_ffn_W2': _L1_ffn_in['W2'], 'L1_ffn_b2': _L1_ffn_in['b2'], 'L1_ffn_gamma': _L1_ffn_in['gamma'], 'L1_ffn_beta': _L1_ffn_in['beta']}

def reference(x, src, dst, edge_weight, L0_gnn_W, L0_gnn_att_src, L0_gnn_att_dst, L0_gnn_bias, L0_gnn_ln_gamma, L0_gnn_ln_beta, L0_ffn_attention_mask, L0_ffn_wr, L0_ffn_br, L0_ffn_w1, L0_ffn_b1, L0_ffn_w2, L0_ffn_b2, L1_gnn_eps, L1_gnn_W1, L1_gnn_b1, L1_gnn_g1, L1_gnn_be1, L1_gnn_W2, L1_gnn_b2, L1_gnn_g2, L1_gnn_be2, L1_ffn_Wr, L1_ffn_br, L1_ffn_W1, L1_ffn_b1, L1_ffn_W2, L1_ffn_b2, L1_ffn_gamma, L1_ffn_beta):
    import jax
    import jax.numpy as jnp

    def _L0_gnn_ref(x, edge_index, W, att_src, att_dst, bias, ln_gamma, ln_beta):
        import jax, jax.numpy as jnp
        import numpy as np
        N = 50000
        E = 25000
        D = 256
        H = 4
        F = D // H

        def gat_layer(x, src, dst, W, att_src, att_dst, bias):
            n = x.shape[0]
            h = (x @ W).reshape(n, H, F)
            a_src = jnp.sum(h * att_src[None], axis=-1)
            a_dst = jnp.sum(h * att_dst[None], axis=-1)
            e = jax.nn.leaky_relu(a_src[src] + a_dst[dst], 0.2)
            m = jax.ops.segment_max(e, dst, num_segments=n)
            m = jnp.where(jnp.isfinite(m), m, 0.0)
            ex = jnp.exp(e - m[dst])
            denom = jax.ops.segment_sum(ex, dst, num_segments=n)
            alpha = ex / (denom[dst] + 1e-16)
            msg = h[src] * alpha[..., None]
            out = jax.ops.segment_sum(msg, dst, num_segments=n)
            return out.reshape(n, H * F) + bias
        n = x.shape[0]
        loops = jnp.arange(n, dtype=edge_index.dtype)
        src = jnp.concatenate([edge_index[0], loops])
        dst = jnp.concatenate([edge_index[1], loops])
        h = gat_layer(x, src, dst, W, att_src, att_dst, bias)
        y = h + x
        mu = jnp.mean(y, axis=-1, keepdims=True)
        var = jnp.mean((y - mu) ** 2, axis=-1, keepdims=True)
        y = (y - mu) / jnp.sqrt(var + 1e-05) * ln_gamma + ln_beta
        return jax.nn.relu(y)

    def _L0_ffn_ref(x, attention_mask, wr, br, w1, b1, w2, b2):
        import jax, jax.numpy as jnp
        import numpy as np
        B, S, D = (8, 128, 256)
        H = 4 * D
        CAPACITY = 0.5
        b, s, d = x.shape
        weights = (jnp.einsum('bsd,do->bso', x, wr) + br)[..., 0]
        k = max(1, int(CAPACITY * s))
        kk = k - 1 if k > 1 else 1
        _, idx = jax.lax.top_k(weights, k)
        sel_idx = idx[:, :kk]
        sel = jnp.take_along_axis(x, sel_idx[:, :, None], axis=1)
        h = jax.nn.gelu(jnp.einsum('bkd,dh->bkh', sel, w1) + b1)
        y = jnp.einsum('bkh,hd->bkd', h, w2) + b2
        w_sel = jnp.take_along_axis(weights, sel_idx, axis=1)
        y = y * w_sel[..., None]
        batch_idx = jnp.arange(b)[:, None]
        processed = jnp.zeros_like(x).at[batch_idx, sel_idx].set(y)
        return processed + x

    def _L1_gnn_ref(x, edge_row, edge_col, edge_vals, eps, W1, b1, g1, be1, W2, b2, g2, be2):
        import jax, jax.numpy as jnp
        import numpy as np
        N = 3125
        E = 100000
        DI = 256
        DO = 256
        BN_EPS = 1e-05

        def _bn_relu(h, gamma, beta):
            mean = jnp.mean(h, axis=0)
            var = jnp.var(h, axis=0)
            hn = (h - mean) * jax.lax.rsqrt(var + BN_EPS)
            return jax.nn.relu(hn * gamma + beta)
        n = x.shape[0]
        msgs = edge_vals[:, None] * x[edge_col]
        agg = jax.ops.segment_sum(msgs, edge_row, num_segments=n)
        h = (1.0 + eps[0]) * x + agg
        h = _bn_relu(h @ W1 + b1, g1, be1)
        h = _bn_relu(h @ W2 + b2, g2, be2)
        return h

    def _L1_ffn_ref(x, Wr, br, W1, b1, W2, b2, gamma, beta):
        import math
        import jax, jax.numpy as jnp
        import numpy as np
        CAPACITY_FACTOR = 1.25
        TOP_K = 2
        LN_EPS = 1e-05

        def _layer_norm(x, gamma, beta):
            mu = jnp.mean(x, axis=-1, keepdims=True)
            var = jnp.var(x, axis=-1, keepdims=True)
            return (x - mu) * jax.lax.rsqrt(var + LN_EPS) * gamma + beta
        B, S, D = x.shape
        E = Wr.shape[1]
        N = B * S
        K = TOP_K
        logits = jnp.mean(x, axis=1) @ Wr + br
        routing_weights = jax.nn.softmax(logits, axis=-1)
        capacity = float(math.ceil(N * CAPACITY_FACTOR / E))
        expected_loads = routing_weights.sum(axis=0) * (N / B)
        scale = jnp.where(expected_loads > capacity, capacity / expected_loads, 1.0)
        routing_weights = jax.nn.softmax(routing_weights * scale, axis=-1)
        rw_tok = jnp.broadcast_to(routing_weights[:, None, :], (B, S, E)).reshape(N, E)
        top_w, top_i = jax.lax.top_k(rw_tok, K)
        top_w = jax.nn.softmax(top_w, axis=-1)
        xf = x.reshape(N, D)
        h = jax.nn.gelu(jnp.einsum('nd,edf->enf', xf, W1) + b1[:, None, :], approximate=False)
        y = jnp.einsum('enf,efd->end', h, W2) + b2[:, None, :]
        w_dense = jnp.zeros((N, E), x.dtype).at[jnp.arange(N)[:, None], top_i].add(top_w)
        out = jnp.einsum('ne,end->nd', w_dense, y).reshape(B, S, D)
        out = _layer_norm(out + x, gamma, beta)
        return out
    edge_index = jnp.stack([src, dst])
    x = x + _L0_gnn_ref(_layernorm(x, axis=-1), edge_index, L0_gnn_W, L0_gnn_att_src, L0_gnn_att_dst, L0_gnn_bias, L0_gnn_ln_gamma, L0_gnn_ln_beta)
    x = x + _L0_ffn_ref(_layernorm(x, axis=-1)[None], L0_ffn_attention_mask, L0_ffn_wr, L0_ffn_br, L0_ffn_w1, L0_ffn_b1, L0_ffn_w2, L0_ffn_b2)[0]
    x = x + _L1_gnn_ref(_layernorm(x, axis=-1), src, dst, edge_weight, L1_gnn_eps, L1_gnn_W1, L1_gnn_b1, L1_gnn_g1, L1_gnn_be1, L1_gnn_W2, L1_gnn_b2, L1_gnn_g2, L1_gnn_be2)
    x = x + _L1_ffn_ref(_layernorm(x, axis=-1)[None], L1_ffn_Wr, L1_ffn_br, L1_ffn_W1, L1_ffn_b1, L1_ffn_W2, L1_ffn_b2, L1_ffn_gamma, L1_ffn_beta)[0]
    return x

_drawn_inputs = setup_inputs


def setup_inputs(seed=0):
    import zlib

    import numpy as np

    out = dict(_drawn_inputs(seed))
    spreads = {'L0_gnn_bias': (0.0, 0.1),
     'L0_gnn_ln_gamma': (1.0, 0.2),
     'L0_gnn_ln_beta': (0.0, 0.1),
     'L0_ffn_b1': (0.0, 0.8),
     'L0_ffn_b2': (0.0, 0.8),
     'L1_gnn_b1': (0.0, 2.0),
     'L1_gnn_g1': (1.0, 0.567),
     'L1_gnn_be1': (0.0, 0.38),
     'L1_gnn_b2': (0.0, 2.0),
     'L1_gnn_g2': (1.0, 0.559),
     'L1_gnn_be2': (0.0, 0.299),
     'L1_ffn_br': (0.0, 0.8),
     'L1_ffn_b1': (0.0, 0.646),
     'L1_ffn_b2': (0.0, 0.446),
     'L1_ffn_gamma': (1.0, 0.553),
     'L1_ffn_beta': (0.0, 0.304)}
    factors = {'L0_ffn_wr': 4.793, 'L0_ffn_w1': 5.969, 'L0_ffn_w2': 5.609}
    for name, (base, spread) in spreads.items():
        noise = np.random.default_rng([zlib.crc32(name.encode()), seed]).standard_normal(out[name].shape)
        drawn = base * np.exp(spread * noise) if base else spread * noise
        out[name] = jnp.asarray(drawn.astype(out[name].dtype))
    for name, factor in factors.items():
        out[name] = (out[name] * factor).astype(out[name].dtype)
    return out
```

```python
import concourse.bass as bass
from concourse import mybir
from contextlib import ExitStack

F32 = mybir.dt.float32
I32 = mybir.dt.int32
U32 = mybir.dt.uint32
ALU = mybir.AluOpType
ACT = mybir.ActivationFunctionType
AX = mybir.AxisListType
ds = bass.ds

P = 128
N = 3125
D = 256
KD = D // P
E = 50000
NT = -(-N // P)
NPAD = NT * P
TAIL = N - (NT - 1) * P
TC = 5
NC = NT // TC
CW = TC * P
HALF = CW // 2
HEADS = 4
FH = D // HEADS
HID = 1024
MH = HID // P
EXPERTS = 8
FE = 512
SLOPE = 0.2
EPS = 1e-5
KEPT = int(0.5 * N) - 1
CAPACITY = float(-(-N * 5 // (4 * EXPERTS)))
HEADROOM = 60.0

COLS = -(-E // P)
LAST = E - (P - 1) * COLS
BATCH = 4
NBATCH = 98
COLPAD = (NBATCH + 1) * BATCH
MSG = D + HEADS
SPARE = NPAD - 1
ROWS = NPAD + P
TABLES = BATCH
assert COLS <= NBATCH * BATCH and NBATCH % 2 == 0 and NT == NC * TC


class Steps:

    def __init__(self, eng, sem):
        self.eng, self.sem, self.n, self.base = eng, sem, 0, None

    def value(self):
        return self.n if self.base is None else self.base + self.n

    def __call__(self, ins):
        ins.then_inc(self.sem, 1)
        self.n += 1

    def wait(self):
        self.eng.wait_ge(self.sem, self.value())

    def begin(self, i, per):
        self.before, self.per, self.base, self.n = self.n, per, i * per + self.n, 0

    def end(self, trips):
        assert self.n == self.per, (self.n, self.per)
        self.n, self.base = self.before + trips * self.per, None


def build(nc, x, src, dst, edge_weight, g0_W, g0_as, g0_ad, g0_bias, g0_gamma, g0_beta, f0_wr, f0_br,
          f0_w1, f0_b1, f0_w2, f0_b2, g1_eps, g1_W1, g1_b1, g1_g1, g1_be1, g1_W2, g1_b2, g1_g2, g1_be2,
          f1_Wr, f1_br, f1_W1, f1_b1, f1_W2, f1_b2, f1_gamma, f1_beta, out):
    ctx = ExitStack()
    with ctx:
        def sb(name, shape, dt=F32):
            return ctx.enter_context(nc.sbuf_tensor(name, shape, dt))

        def sem(name):
            return ctx.enter_context(nc.semaphore(name))

        htab = nc.dram_tensor("htab", [NPAD, MSG], F32).ap()
        qtab = nc.dram_tensor("qtab", [NPAD, 2 * HEADS], F32).ap()
        xtab = nc.dram_tensor("xtab", [NPAD, D], F32).ap()
        sum0 = nc.dram_tensor("sum0", [TABLES * ROWS, MSG], F32).ap()
        sum1 = nc.dram_tensor("sum1", [TABLES * ROWS, D], F32).ap()
        wtab = nc.dram_tensor("wtab", [NPAD], F32).ap()

        X = sb("X", [P, NT, D])
        XN = sb("XN", [P, NT, D])
        R1 = sb("R1", [P, NT * (MSG + HEADS)])
        R2 = sb("R2", [P, (NT + 1) * MSG])
        R3 = sb("R3", [P, NT * MSG])
        HN = R1[:, :].rearrange("p (t c) -> p t c", t=NT)
        A = R2[:, 0:NT * MSG].rearrange("p (t c) -> p t c", t=NT)
        B = R3[:, :].rearrange("p (t c) -> p t c", t=NT)
        H1 = R1[:, 0:KD * NPAD].rearrange("p (k n) -> p k n", k=KD)
        H2 = R3[:, 0:KD * NPAD].rearrange("p (k n) -> p k n", k=KD)
        Z = R2[:, 0:NT * D].rearrange("p (t c) -> p t c", t=NT)
        xc = sb("xc", [P, TC, D])
        xt = sb("xt", [P, KD, CW])
        ht = sb("ht", [P, MH * CW])
        w1s = sb("w1s", [P, KD, HID])
        w2s = sb("w2s", [P, MH, D])
        b1s = sb("b1s", [P, MH])
        wext = sb("wext", [P, KD, MSG + HEADS])
        gw = sb("gw", [P, 2, KD, D])
        gcol = sb("gcol", [P, 6, KD])
        wr1 = sb("wr1", [P, KD, EXPERTS])
        rows = sb("rows", [P, 8, D])
        ATS, ATD, BIAS, GAM, BET, WRR, B2R, B2B = range(8)
        small = sb("small", [P, 4])
        ident = sb("ident", [P, P])
        ones = sb("ones", [P, P])
        lower = sb("lower", [P, P])
        spare_row = sb("spare_row", [P, 1])
        table_of = sb("table_of", [P, BATCH])
        st = sb("st", [P, NT, 6])
        mean = sb("mean", [P, NT])
        var = sb("var", [P, NT])
        rstd = sb("rstd", [P, NT])
        t1 = sb("t1", [P, NT])
        t2 = sb("t2", [P, NT])
        zs = sb("zs", [P, NT, HEADS])
        zb = sb("zb", [P, NT, HEADS])
        qn = sb("qn", [P, NT, 2 * HEADS])
        exs = sb("exs", [P, NT, HEADS])
        amax = sb("amax", [P, HEADS])
        gmax = sb("gmax", [P, HEADS])
        wl = sb("wl", [P, NT])
        wm = sb("wm", [P, NT])
        wlT = sb("wlT", [NT, P])
        cnt = sb("cnt", [P, 3, NT])
        ftmp = sb("ftmp", [P, 2, D])
        bst = sb("bst", [P, KD, 7, 6])
        bmv = sb("bmv", [P, KD, 2])
        bsc = sb("bsc", [P, 3, KD])
        rt = sb("rt", [1, 12, EXPERTS])
        ri = sb("ri", [1, EXPERTS], U32)
        r1 = sb("r1", [1, 8])
        mrow = sb("mrow", [1, D])
        mcol = sb("mcol", [P, KD])
        wexp = sb("wexp", [P, 2])
        bre = sb("bre", [1, EXPERTS])

        srcI = sb("srcI", [P, COLPAD], I32)
        dstI = sb("dstI", [P, COLPAD], I32)
        srcF = sb("srcF", [P, COLPAD])
        dstF = sb("dstF", [P, COLPAD])
        ew = sb("ew", [P, COLPAD])
        o = [0]

        def part(n):
            o[0] += n
            assert o[0] <= MH * CW
            return ht[:, o[0] - n:o[0]]

        G = [part(BATCH * MSG).rearrange("p (u c) -> p u c", u=BATCH) for _ in range(2)]
        M = [part(BATCH * MSG).rearrange("p (u c) -> p u c", u=BATCH) for _ in range(2)]
        Q = [part(BATCH * 2 * HEADS).rearrange("p (u c) -> p u c", u=BATCH) for _ in range(2)]
        xcf = xc[:, :, :].rearrange("p t c -> p (t c)")
        same, earlier = (xcf[:, j * BATCH * P:(j + 1) * BATCH * P].rearrange("p (u e) -> p u e", u=BATCH)
                         for j in range(2))
        ez = [sb(f"ez{h}", [P, BATCH, HEADS]) for h in range(2)]
        gat = [sb(f"gat{h}", [P, 2, BATCH], I32) for h in range(2)]
        key = [sb(f"key{h}", [P, BATCH]) for h in range(2)]
        ewb = [sb(f"ewb{h}", [P, BATCH]) for h in range(2)]
        rowid = [sb(f"rowid{h}", [P, BATCH], I32) for h in range(2)]
        es = sb("es", [P, 4, BATCH])

        PS = ctx.enter_context(nc.psum_tensor("PS", [P, 8, 512], F32))
        PSF = PS[:, :, :].rearrange("p b c -> p (b c)")

        names = """x_in idx_in ew_in watt_in vec_in f0w_in gw_in r1_in idx_clear zero_set zeroed ones_set ident_set
            const_set dve stat var_ready std_ready norm_done xc_ready xt_read xt_ready wext_ready
            proj_done proj_kept amax_ready gmax_ready shift_ready exs_ready q_stored h_stored
            idx_float sums0_in sums1_in table_added wlog_ready wlT_done wlT_ready wrow_stored wrow_in xn_stored
            hid_done hid_kept y_done y_kept x_added h1_done h1_kept h2_done h2_kept h1n_ready h2n_ready
            bnv_ready bnstd_ready bn_ready a_ready back_done back_added mean_done mrow_ready mcol_done
            mcol_ready logit_done rexp_in rexp_out pair_ready pairw_ready wb_done expert_w1_in
            expert_w2_in expert_b2_in w2_scaled out_ready stored pool_held""".split()
        s = {n: sem(n) for n in names}
        edge_names = "staged rowed row_ready ex_in ex_out msg_ready merged merged_kept chain_passed"
        es_ = [{n: sem(f"{n}{k}") for n in edge_names.split()} for k in range(2)]
        for k in range(2):
            es_[k]["gathered"] = [sem(f"gathered{k}_{h}") for h in range(2)]
            es_[k]["added"] = [sem(f"added{k}_{u}") for u in range(TABLES)]
        block = ctx.enter_context(nc.Block())

        def nodes(ap):
            return ap.rearrange("(t p) c -> p t c", p=P)

        def on_all(ap):
            return ap.rearrange("(o c) -> o c", o=1).to_broadcast([P, ap.shape[0]])

        width = [MSG, D]
        sums = [sum0, sum1]

        @block.sync
        def _(sp):
            sp.wait_ge(s["dve"], 1)
            sp.dma_start(X[:, 0:NT - 1, :], nodes(x[0:(NT - 1) * P, :])).then_inc(s["x_in"], 16)
            sp.dma_start(X[0:TAIL, NT - 1, :], x[(NT - 1) * P:N, :]).then_inc(s["x_in"], 16)
            sp.dma_start(wext[:, :, 0:D], g0_W.rearrange("(k p) n -> p k n", p=P)).then_inc(s["watt_in"], 16)
            sp.dma_start(rows[:, ATS, :], on_all(g0_as.rearrange("h f -> (h f)"))).then_inc(s["watt_in"], 16)
            sp.dma_start(rows[:, ATD, :], on_all(g0_ad.rearrange("h f -> (h f)"))).then_inc(s["watt_in"], 16)
            sp.wait_ge(s["idx_clear"], 3)
            n112 = 112
            for a, t in ((src, srcI), (dst, dstI), (edge_weight, ew)):
                q = s["ew_in"] if t is ew else s["idx_in"]
                sp.dma_start(t[0:n112, 0:COLS],
                             a[0:n112 * COLS].rearrange("(p c) -> p c", c=COLS)).then_inc(q, 16)
                sp.dma_start(t[n112:P - 1, 0:COLS],
                             a[n112 * COLS:(P - 1) * COLS].rearrange("(p c) -> p c", c=COLS)).then_inc(q, 16)
                sp.dma_start(t[P - 1:P, 0:LAST],
                             a[(P - 1) * COLS:E].rearrange("(p c) -> p c", p=1)).then_inc(q, 16)
            for j, v in ((BIAS, g0_bias), (GAM, g0_gamma), (BET, g0_beta), (B2R, f0_b2)):
                sp.dma_start(rows[:, j, :], on_all(v)).then_inc(s["vec_in"], 16)
            sp.dma_start(rows[:, WRR, :], on_all(f0_wr.rearrange("d o -> (d o)"))).then_inc(s["vec_in"], 16)
            sp.dma_start(small[:, 0:1], on_all(f0_br)).then_inc(s["vec_in"], 16)
            sp.dma_start(small[:, 1:2], on_all(g1_eps)).then_inc(s["vec_in"], 16)
            sp.wait_ge(s["zero_set"], 1)
            for k in range(2):
                rpp = TABLES * ROWS // P
                v = sums[k].rearrange("(p r) c -> p (r c)", p=P)
                step = NT + 1
                for r in range(0, rpp, step):
                    sp.dma_start(v[:, r * width[k]:(r + step) * width[k]],
                                 R2[:, 0:step * width[k]]).then_inc(s["zeroed"], 16)
            sp.dma_start(w1s[:, :, :], f0_w1.rearrange("(k p) n -> p k n", p=P)).then_inc(s["f0w_in"], 16)
            sp.dma_start(w2s[:, :, :], f0_w2.rearrange("(k p) n -> p k n", p=P)).then_inc(s["f0w_in"], 16)
            with nc.allow_non_contiguous_dma(reason="short vectors, one feature on a partition"):
                sp.dma_start(b1s[:, :], f0_b1.rearrange("(m p) -> p m", p=P)).then_inc(s["f0w_in"], 16)
                for j, v in enumerate((g1_b1, g1_g1, g1_be1, g1_b2, g1_g2, g1_be2)):
                    sp.dma_start(gcol[:, j, :], v.rearrange("(m p) -> p m", p=P)).then_inc(s["gw_in"], 16)
            for j, w in enumerate((g1_W1, g1_W2)):
                sp.dma_start(gw[:, j, :, :], w.rearrange("(k p) n -> p k n", p=P)).then_inc(s["gw_in"], 16)
            sp.dma_start(wr1[:, :, :], f1_Wr.rearrange("(k p) n -> p k n", p=P)).then_inc(s["r1_in"], 16)
            sp.dma_start(bre[:, :], f1_br.rearrange("(o c) -> o c", o=1)).then_inc(s["r1_in"], 16)

            sp.wait_ge(s["proj_kept"], NT)
            sp.dma_start(nodes(htab), HN[:, :, 0:MSG]).then_inc(s["h_stored"], 16)
            sp.wait_ge(s["shift_ready"], 1)
            sp.dma_start(nodes(qtab), qn[:, :, :]).then_inc(s["q_stored"], 16)

            def sums_in(k, regions):
                for u in range(TABLES):
                    sp.wait_ge(es_[k]["added"][u], 16 * NBATCH)
                for u in range(TABLES):
                    if u >= 2:
                        sp.wait_ge(s["table_added"], (TABLES - 1) * k + u - 1)
                    dest = regions[0] if u == 0 else regions[1]
                    sp.dma_start(dest, nodes(sums[k][u * ROWS:u * ROWS + NPAD, :])).then_inc(s[f"sums{k}_in"], 16)

            sums_in(0, (A, B))

            sp.wait_ge(s["wlT_ready"], 1)
            sp.dma_start(wtab.rearrange("(t p) -> t p", p=P), wlT[:, :]).then_inc(s["wrow_stored"], 16)
            sp.wait_ge(s["wrow_stored"], 16)
            sp.dma_start(R3[:, 0:NPAD], on_all(wtab)).then_inc(s["wrow_in"], 16)

            sp.wait_ge(s["norm_done"], 4 * NT)
            sp.dma_start(nodes(xtab), XN[:, :, :]).then_inc(s["xn_stored"], 16)
            sums_in(1, (Z, R3[:, 0:NT * D].rearrange("p (t c) -> p t c", t=NT)))

            sp.wait_ge(s["norm_done"], 5 * NT)
            sp.dma_start(rows[:, GAM, :], on_all(f1_gamma)).then_inc(s["expert_b2_in"], 16)
            sp.dma_start(rows[:, BET, :], on_all(f1_beta)).then_inc(s["expert_b2_in"], 16)
            sp.wait_ge(s["pair_ready"], 2)
            for j in range(2):
                e = sp.value_load(ri[0:1, j:j + 1], min_val=0, max_val=EXPERTS - 1)
                sp.dma_start(w1s[:, :, j * FE:(j + 1) * FE],
                             f1_W1.rearrange("e (k p) f -> p (e k) f", p=P)[:, ds(e * KD, KD), :]).then_inc(s["expert_w1_in"], 16)
                sp.dma_start(w2s[:, j * MH // 2:(j + 1) * MH // 2, :],
                             f1_W2.rearrange("e (k p) d -> p (e k) d", p=P)[:, ds(e * (FE // P), FE // P), :]).then_inc(s["expert_w2_in"], 16)
                with nc.allow_non_contiguous_dma(reason="a short vector, one feature on a partition"):
                    sp.dma_start(b1s[:, j * MH // 2:(j + 1) * MH // 2],
                                 f1_b1.rearrange("e (k p) -> p (e k)", p=P)[:, ds(e * (FE // P), FE // P)]).then_inc(s["expert_w1_in"], 16)
                sp.dma_start(rows[:, B2R + j, :], f1_b2[ds(e, 1), :].to_broadcast([P, D])).then_inc(s["expert_b2_in"], 16)
            sp.wait_ge(s["out_ready"], 1)
            sp.dma_start(nodes(out[0:(NT - 1) * P, :]), X[:, 0:NT - 1, :]).then_inc(s["stored"], 16)
            sp.dma_start(out[(NT - 1) * P:N, :], X[0:TAIL, NT - 1, :]).then_inc(s["stored"], 16)
            sp.wait_ge(s["stored"], 32)

        @block.gpsimd
        def _(pool):
            pool.memset(srcI[:, :], 0).then_inc(s["idx_clear"], 1)
            pool.memset(dstI[:, :], SPARE).then_inc(s["idx_clear"], 1)
            pool.memset(ew[:, :], 0.0).then_inc(s["idx_clear"], 1)
            pool.memset(ident[:, :], 1.0).then_inc(s["ones_set"], 1)
            pool.memset(lower[:, :], 1.0).then_inc(s["ones_set"], 1)
            pool.memset(ones[:, :], 1.0).then_inc(s["const_set"], 1)
            pool.wait_ge(s["ones_set"], 2)
            pool.affine_select(out=ident[:, :], in_=ident[:, :], compare_op=ALU.is_equal, fill=0.0, base=0,
                               pattern=[[-1, P]], channel_multiplier=1).then_inc(s["ident_set"], 1)
            pool.affine_select(out=lower[:, :], in_=lower[:, :], compare_op=ALU.is_gt, fill=0.0, base=0,
                               pattern=[[-1, P]], channel_multiplier=1).then_inc(s["const_set"], 1)
            pool.iota(spare_row[:, :], pattern=[[0, 1]], base=NPAD, channel_multiplier=1,
                      allow_small_or_imprecise_dtypes=True).then_inc(s["const_set"], 1)
            pool.iota(table_of[:, :], pattern=[[ROWS, BATCH]], base=0, channel_multiplier=0,
                      allow_small_or_imprecise_dtypes=True).then_inc(s["const_set"], 1)
            pool.memset(small[:, 2:3], EPS).then_inc(s["const_set"], 1)

            def chunks(stage, source, kept):
                with pool.Fori(0, NC) as i:
                    pool.wait_ge(s["xt_read"], NC * stage + i)
                    pool.wait_ge(*kept)
                    pool.tensor_copy(xc[:, :, :], source[:, ds(i * TC, TC), :]).then_inc(s["xc_ready"], 1)

            chunks(0, XN, (s["norm_done"], NT))
            pool.wait_ge(s["amax_ready"], 1)
            pool.partition_all_reduce(gmax[:, :], amax[:, :], P, bass.bass_isa.ReduceOp.max).then_inc(s["gmax_ready"], 1)

            def hold():
                pool.sem_inc(s["pool_held"], 1)

            def edges(k):
                z, w = es_[k], width[k]
                tables = (htab, qtab) if k == 0 else (xtab,)
                stored = s["q_stored"] if k == 0 else s["xn_stored"]

                def gather(h):
                    for u in range(BATCH):
                        pool.indirect_dma_start(G[h][:, u, 0:w], None, tables[0],
                                                bass.IndirectOffsetOnAxis(ap=gat[h][:, 0, u:u + 1], axis=0)
                                                ).then_inc(z["gathered"][h], 16)
                        if k == 0:
                            pool.indirect_dma_start(Q[h][:, u, :], None, tables[1],
                                                    bass.IndirectOffsetOnAxis(ap=gat[h][:, 1, u:u + 1], axis=0)
                                                    ).then_inc(z["gathered"][h], 16)

                if k == 0:
                    pool.wait_ge(s["h_stored"], 16)
                pool.wait_ge(s["zeroed"], 16 * 2 * TABLES)
                pool.wait_ge(stored, 16)
                pool.wait_ge(z["staged"], 3)
                gather(0)
                with pool.Fori(0, NBATCH // 2) as i:
                    for h in range(2):
                        b = i * 2 + h
                        pool.wait_ge(z["staged"], b * 3 + 6)
                        pool.wait_ge(z["merged"], b * BATCH)
                        hold()
                        gather(1 - h)
                        for u in range(BATCH):
                            pool.wait_ge(z["added"][u], b * 16)
                        pool.sem_inc(z["chain_passed"], 1)
                        for u in range(BATCH):
                            pool.wait_ge(z["merged_kept"], b * BATCH + u + 1)
                            pool.wait_ge(z["row_ready"], b + 1)
                            hold()
                            pool.indirect_dma_start(sums[k], bass.IndirectOffsetOnAxis(ap=rowid[h][:, u:u + 1], axis=0),
                                                    M[h][:, u, 0:w], None, compute_op=ALU.add).then_inc(z["added"][u], 16)
                pool.wait_ge(z["gathered"][0], 16 * BATCH * (2 - k) * (NBATCH // 2 + 1))

            edges(0)
            chunks(1, XN, (s["norm_done"], 3 * NT))
            edges(1)
            chunks(2, Z, (s["a_ready"], 1))
            chunks(3, XN, (s["norm_done"], 5 * NT))

        @block.scalar
        def _(act):
            stds = [0]
            HT = ht[:, :].rearrange("p (m c) -> p m c", m=MH)

            def apart():
                act.wait_ge(s["const_set"], 5)

            def std():
                stds[0] += 1
                act.wait_ge(s["const_set"], 5)
                act.wait_ge(s["var_ready"], stds[0])
                act.activation(rstd[:, :], var[:, :], ACT.Sqrt, bias=small[:, 2:3]).then_inc(s["std_ready"], 1)

            def turned(i, stage, used, before):
                act.wait_ge(s["xt_read"], i + (NC * stage + 1))
                act.wait_ge(s[used], before)
                act.activation(xt[:, :, :].rearrange("p k c -> p (k c)"), PSF[:, 0:KD * CW],
                               ACT.Copy).then_inc(s["xt_ready"], 1)

            std()
            with act.Fori(0, NC) as i:
                turned(i, 0, "proj_done", i * TC)
            act.preload_act_table(ACT.Exp)
            act.wait_ge(s["shift_ready"], 2)
            act.activation(exs[:, :, :], zb[:, :, :], ACT.Exp).then_inc(s["exs_ready"], 1)

            def edges(k):
                z, w = es_[k], width[k]

                def stage(h, b):
                    cols = ds(b * BATCH, BATCH)
                    if k == 0:
                        copies = ((gat[h][:, 0, :], srcF), (gat[h][:, 1, :], dstF), (key[h][:, :], dstF))
                    else:
                        copies = ((gat[h][:, 0, :], dstF), (ewb[h][:, :], ew), (key[h][:, :], srcF))
                    for to, of in copies:
                        act.activation(to, of[:, cols], ACT.Copy).then_inc(z["staged"], 1)

                act.wait_ge(s["ew_in"], 48)
                act.wait_ge(s["idx_float"], 2)
                stage(0, 0)
                with act.Fori(0, NBATCH // 2) as i:
                    for h in range(2):
                        b = i * 2 + h
                        act.wait_ge(z["msg_ready"], b)
                        act.wait_ge(s["idx_float"], 2)
                        stage(1 - h, b + 1)
                        if k == 0:
                            act.wait_ge(z["ex_in"], b + 1)
                            act.activation(G[h][:, :, D:MSG], ez[h][:, :, :], ACT.Exp).then_inc(z["ex_out"], 1)
                        act.wait_ge(z["chain_passed"], b)
                        for u in range(BATCH):
                            act.wait_ge(z["merged"], b * BATCH + u + 1)
                            act.activation(M[h][:, u, 0:w], PS[:, 2 + u, 0:w], ACT.Copy).then_inc(z["merged_kept"], 1)

            edges(0)
            std()
            std()

            def ffn(stage, j, func, loaded):
                act.preload_act_table(func)
                act.wait_ge(*loaded)
                groups = 2 * MH
                with act.Fori(0, NC) as i:
                    turned(i, stage, "hid_done", i * groups + j * NC * groups)
                    for g in range(groups):
                        m, half = g // 2, g % 2
                        act.wait_ge(s["hid_done"], i * groups + (j * NC * groups + g + 1))
                        act.activation(HT[:, m, half * HALF:(half + 1) * HALF], PS[:, 3 + g % 2, 0:HALF], func,
                                       bias=b1s[:, m:m + 1]).then_inc(s["hid_kept"], 1)

            ffn(1, 0, ACT.Gelu_apprx_tanh, (s["f0w_in"], 48))
            std()
            edges(1)

            act.wait_ge(s["gw_in"], 16 * 8)
            with act.Fori(0, NC) as i:
                turned(i, 2, "h1_done", i * 4)
                for g in range(4):
                    m, half = g // 2, g % 2
                    act.wait_ge(s["h1_done"], i * 4 + (g + 1))
                    apart()
                    act.activation(H1[:, m, ds(i * CW + half * HALF, HALF)], PS[:, 3 + g, 0:HALF], ACT.Identity,
                                   bias=gcol[:, 0, m:m + 1]).then_inc(s["h1_kept"], 1)

            def bn_std(n):
                act.wait_ge(s["bnv_ready"], KD * n)
                act.activation(bsc[:, 0, :], bmv[:, :, 1], ACT.Sqrt, bias=small[:, 2:3]).then_inc(s["bnstd_ready"], 1)

            def bn_relu(i, n, of, ready):
                for m in range(KD):
                    act.wait_ge(s["bn_ready"], n)
                    act.activation(xt[:, m, :], of[:, m, ds(i * CW, CW)], ACT.Relu, bias=bsc[:, 2, m:m + 1],
                                   scale=bsc[:, 1, m:m + 1]).then_inc(s[ready], 1)

            bn_std(1)
            with act.Fori(0, NC) as i:
                act.wait_ge(s["h2_done"], i * 4)
                bn_relu(i, 1, H1, "h1n_ready")
                for g in range(4):
                    m, half = g // 2, g % 2
                    act.wait_ge(s["h2_done"], i * 4 + (g + 1))
                    apart()
                    act.activation(H2[:, m, ds(i * CW + half * HALF, HALF)], PS[:, 3 + g, 0:HALF], ACT.Identity,
                                   bias=gcol[:, 3, m:m + 1]).then_inc(s["h2_kept"], 1)
            bn_std(2)
            with act.Fori(0, NC) as i:
                act.wait_ge(s["back_done"], i)
                bn_relu(i, 2, H2, "h2n_ready")
            std()

            act.wait_ge(s["rexp_in"], 1)
            act.activation(rt[:, 1, :], rt[:, 0, :], ACT.Exp, bias=r1[:, 1:2]).then_inc(s["rexp_out"], 1)
            act.wait_ge(s["rexp_in"], 2)
            act.activation(rt[:, 5, :], rt[:, 4, :], ACT.Exp, bias=r1[:, 1:2]).then_inc(s["rexp_out"], 1)
            act.wait_ge(s["rexp_in"], 3)
            act.activation(rt[:, 8, 0:2], rt[:, 7, 0:2], ACT.Exp, bias=r1[:, 1:2]).then_inc(s["rexp_out"], 1)
            ffn(3, 1, ACT.Gelu, (s["expert_w1_in"], 64))
            std()

        @block.tensor
        def _(pe):
            HT = ht[:, :].rearrange("p (m c) -> p m c", m=MH)

            def turn(i, stage):
                pe.wait_ge(s["xc_ready"], i + (NC * stage + 1))
                pe.wait_ge(s["xt_ready"], i + NC * stage)
                for k in range(KD):
                    for u in range(TC):
                        c = k * CW + u * P
                        mm = pe.transpose(PSF[:, c:c + P], xc[:, u, k * P:(k + 1) * P], ident[:, :])
                mm.then_inc(s["xt_read"], 1)
                pe.wait_ge(s["xt_ready"], i + (NC * stage + 1))

            pe.wait_ge(s["ident_set"], 1)
            pe.wait_ge(s["wext_ready"], 4)
            with pe.Fori(0, NC) as i:
                turn(i, 0)
                pe.wait_ge(s["proj_kept"], i * TC)
                for u in range(TC):
                    for k in range(KD):
                        mm = pe.matmul(PS[:, 3 + u, 0:MSG + HEADS], xt[:, k, u * P:(u + 1) * P], wext[:, k, :],
                                       start=(k == 0), stop=(k == KD - 1))
                    mm.then_inc(s["proj_done"], 1)

            def edges(k):
                z, w = es_[k], width[k]
                with pe.Fori(0, NBATCH // 2) as i:
                    for h in range(2):
                        b = i * 2 + h
                        pe.wait_ge(z["staged"], b * 3 + 3)
                        for u in range(BATCH):
                            mm = pe.matmul(PS[:, h, u * P:(u + 1) * P], key[h][:, u:u + 1].to_broadcast([P, P]),
                                           ident[:, :], start=True, stop=True)
                        mm.then_inc(z["rowed"], 1)
                        pe.wait_ge(z["msg_ready"], b + 1)
                        pe.wait_ge(z["merged_kept"], b * BATCH)
                        for u in range(BATCH):
                            pe.matmul(PS[:, 2 + u, 0:w], same[:, u, :], G[h][:, u, 0:w],
                                      start=True, stop=True).then_inc(z["merged"], 1)

            pe.wait_ge(s["proj_kept"], NT)
            edges(0)

            pe.wait_ge(s["wlog_ready"], 1)
            pe.transpose(PS[0:NT, 7, 0:P], wl[:, :], ident[:, :]).then_inc(s["wlT_done"], 1)

            def ffn(stage, j, loaded):
                for q in loaded:
                    pe.wait_ge(*q)
                groups = 2 * MH
                with pe.Fori(0, NC) as i:
                    turn(i, stage)
                    for g in range(groups):
                        m, half = g // 2, g % 2
                        if g >= 2:
                            pe.wait_ge(s["hid_kept"], i * groups + (j * NC * groups + g - 1))
                        for k in range(KD):
                            mm = pe.matmul(PS[:, 3 + g % 2, 0:HALF], w1s[:, k, m * P:(m + 1) * P],
                                           xt[:, k, half * HALF:(half + 1) * HALF], start=(k == 0), stop=(k == KD - 1))
                        mm.then_inc(s["hid_done"], 1)
                    pe.wait_ge(s["hid_kept"], i * groups + (j * NC * groups + groups))
                    for u in range(TC):
                        pe.wait_ge(s["y_kept"], i * TC + (j * NT + max(0, u - 2)))
                        for m in range(MH):
                            mm = pe.matmul(PS[:, 5 + u % 3, 0:D], HT[:, m, u * P:(u + 1) * P], w2s[:, m, :],
                                           start=(m == 0), stop=(m == MH - 1))
                        mm.then_inc(s["y_done"], 1)

            pe.wait_ge(s["wlT_ready"], 1)
            ffn(1, 0, ((s["f0w_in"], 48),))
            edges(1)

            def layer(i, j, done, kept):
                pe.wait_ge(s[kept], i * 4)
                for g in range(4):
                    m, half = g // 2, g % 2
                    for k in range(KD):
                        mm = pe.matmul(PS[:, 3 + g, 0:HALF], gw[:, j, k, m * P:(m + 1) * P],
                                       xt[:, k, half * HALF:(half + 1) * HALF], start=(k == 0), stop=(k == KD - 1))
                    mm.then_inc(s[done], 1)

            pe.wait_ge(s["gw_in"], 16 * 8)
            with pe.Fori(0, NC) as i:
                turn(i, 2)
                layer(i, 0, "h1_done", "h1_kept")
            with pe.Fori(0, NC) as i:
                pe.wait_ge(s["h1n_ready"], i * KD + KD)
                layer(i, 1, "h2_done", "h2_kept")
            with pe.Fori(0, NC) as i:
                pe.wait_ge(s["h2n_ready"], i * KD + KD)
                pe.wait_ge(s["back_added"], i)
                for u in range(TC):
                    for m in range(KD):
                        c = u * D + m * P
                        mm = pe.transpose(PSF[:, c:c + P], xt[:, m, u * P:(u + 1) * P], ident[:, :])
                mm.then_inc(s["back_done"], 1)

            pe.wait_ge(s["norm_done"], 5 * NT)
            pe.wait_ge(s["const_set"], 5)
            pe.matmul(PS[0:1, 7, 0:D], ones[:, 0:1], XN[:, 0, :], start=True, stop=False)
            with pe.Fori(1, NT - 1) as t:
                pe.matmul(PS[0:1, 7, 0:D], ones[:, 0:1], XN[:, ds(t, 1), :], start=False, stop=False)
            pe.matmul(PS[0:1, 7, 0:D], ones[0:TAIL, 0:1], XN[0:TAIL, NT - 1, :],
                      start=False, stop=True).then_inc(s["mean_done"], 1)
            pe.wait_ge(s["mrow_ready"], 1)
            for k in range(KD):
                mm = pe.matmul(PS[:, 6, k:k + 1], mrow[0:1, k * P:(k + 1) * P], ones[0:1, 0:1], start=True, stop=True)
            mm.then_inc(s["mcol_done"], 1)
            pe.wait_ge(s["mcol_ready"], 1)
            pe.wait_ge(s["r1_in"], 32)
            for k in range(KD):
                mm = pe.matmul(PS[0:1, 7, 0:EXPERTS], mcol[:, k:k + 1], wr1[:, k, :], start=(k == 0), stop=(k == KD - 1))
            mm.then_inc(s["logit_done"], 1)
            pe.wait_ge(s["pairw_ready"], 1)
            pe.matmul(PS[:, 6, 0:2], ones[0:1, :], rt[0:1, 9, 0:2], start=True, stop=True).then_inc(s["wb_done"], 1)
            ffn(3, 1, ((s["expert_w1_in"], 64), (s["w2_scaled"], 2)))

        @block.vector
        def _(v):
            step = Steps(v, s["dve"])
            norms, tables = [0], [0]

            def link(ins):
                step(ins)
                step.wait()

            def norm(of, to):
                n = norms[0]
                with v.Fori(0, NC) as i:
                    for u in range(TC):
                        t = i * TC + u
                        v.bn_stats(st[:, ds(t, 1), :], of(t)).then_inc(s["stat"], 1)
                v.wait_ge(s["stat"], NT * (n + 1))
                step(v.tensor_tensor(mean[:, :], st[:, :, 1], st[:, :, 4], ALU.add))
                step(v.tensor_tensor(t1[:, :], st[:, :, 1], st[:, :, 4], ALU.subtract))
                step(v.tensor_tensor(t2[:, :], st[:, :, 2], st[:, :, 5], ALU.add))
                step.wait()
                step(v.tensor_scalar(mean[:, :], mean[:, :], 0.5, None, ALU.mult))
                link(v.scalar_tensor_tensor(out=t1[:, :], in0=t1[:, :], scalar=0.25, in1=t1[:, :], op0=ALU.mult, op1=ALU.mult))
                v.scalar_tensor_tensor(out=var[:, :], in0=t2[:, :], scalar=1.0 / D, in1=t1[:, :], op0=ALU.mult,
                                       op1=ALU.add).then_inc(s["var_ready"], 1)
                v.wait_ge(s["std_ready"], n + 1)
                link(v.reciprocal(rstd[:, :], rstd[:, :]))
                with v.Fori(0, NC) as i:
                    for u in range(TC):
                        t = i * TC + u
                        v.tensor_scalar(to(t), of(t), mean[:, ds(t, 1)], rstd[:, ds(t, 1)], ALU.subtract,
                                        ALU.mult).then_inc(s["norm_done"], 1)
                norms[0] += 1
                v.wait_ge(s["norm_done"], NT * norms[0])

            def tile(a):
                return lambda t: a[:, ds(t, 1), 0:D]

            def row(j, n=NT):
                return rows[:, j:j + 1, :].to_broadcast([P, n, D])

            def add_tables(k, a, b):
                for u in range(1, TABLES):
                    v.wait_ge(s[f"sums{k}_in"], 16 * (u + 1))
                    v.tensor_tensor(a, a, b, ALU.add).then_inc(s["table_added"], 1)
                    tables[0] += 1
                v.wait_ge(s["table_added"], tables[0])

            step(v.memset(X[:, NT - 1, :], 0.0))
            v.memset(R2[:, :], 0.0).then_inc(s["zero_set"], 1)
            v.wait_ge(s["watt_in"], 48)
            for k in range(KD):
                for j, a in ((0, ATS), (1, ATD)):
                    link(v.tensor_tensor(ftmp[:, j, :], wext[:, k, 0:D], rows[:, a, :], ALU.mult))
                    v.tensor_reduce(wext[:, k, D + j * HEADS:D + (j + 1) * HEADS],
                                    ftmp[:, j, :].rearrange("p (h f) -> p h f", h=HEADS), AX.X,
                                    ALU.add).then_inc(s["wext_ready"], 1)
            v.wait_ge(s["x_in"], 32)
            norm(tile(X), tile(XN))

            v.wait_ge(s["idx_in"], 96)
            v.tensor_copy(srcF[:, :], srcI[:, :]).then_inc(s["idx_float"], 1)
            v.tensor_copy(dstF[:, :], dstI[:, :]).then_inc(s["idx_float"], 1)
            with v.Fori(0, NC) as i:
                for u in range(TC):
                    v.wait_ge(s["proj_done"], i * TC + (u + 1))
                    v.tensor_scalar(HN[:, ds(i * TC + u, 1), :], PS[:, 3 + u:4 + u, 0:MSG + HEADS], 0.0, None,
                                    ALU.add).then_inc(s["proj_kept"], 1)
            v.wait_ge(s["proj_kept"], NT)
            a_src, a_dst = HN[:, :, D:MSG], HN[:, :, MSG:MSG + HEADS]
            v.tensor_reduce(amax[:, :], a_src.rearrange("p t h -> p h t"), AX.X, ALU.max).then_inc(s["amax_ready"], 1)
            step(v.tensor_copy(qn[:, :, 0:HEADS], a_dst))
            link(v.tensor_tensor(zs[:, :, :], a_src, a_dst, ALU.add))
            step(v.scalar_tensor_tensor(out=zs[:, :, :], in0=zs[:, :, :], scalar=SLOPE, in1=zs[:, :, :], op0=ALU.mult, op1=ALU.max))
            v.wait_ge(s["gmax_ready"], 1)
            link(v.tensor_tensor(zb[:, :, :], a_dst, gmax[:, :].unsqueeze(1).to_broadcast([P, NT, HEADS]), ALU.add))
            link(v.scalar_tensor_tensor(out=zb[:, :, :], in0=zb[:, :, :], scalar=SLOPE, in1=zb[:, :, :], op0=ALU.mult, op1=ALU.max))
            v.scalar_tensor_tensor(out=qn[:, :, HEADS:2 * HEADS], in0=zb[:, :, :], scalar=-HEADROOM, in1=zs[:, :, :],
                                   op0=ALU.add, op1=ALU.max).then_inc(s["shift_ready"], 1)
            v.wait_ge(s["shift_ready"], 1)
            v.tensor_tensor(zb[:, :, :], zs[:, :, :], qn[:, :, HEADS:2 * HEADS], ALU.subtract).then_inc(s["shift_ready"], 1)

            def edges(k):
                z, w = es_[k], width[k]
                with v.Fori(0, NBATCH // 2) as i:
                    step.begin(i, 2 * (8 if k == 0 else 6))
                    for h in range(2):
                        b = i * 2 + h
                        v.wait_ge(z["merged"], b * BATCH)
                        v.wait_ge(z["rowed"], b + 1)
                        link(v.tensor_tensor(same[:, :, :], PS[:, h, :].rearrange("p (u e) -> p u e", u=BATCH),
                                             key[h][:, :].unsqueeze(2).to_broadcast([P, BATCH, P]), ALU.is_equal))
                        step(v.tensor_tensor(earlier[:, :, :], same[:, :, :],
                                             lower[:, :].unsqueeze(1).to_broadcast([P, BATCH, P]), ALU.mult))
                        step(v.tensor_scalar(es[:, 1, :], key[h][:, :], -1.0, spare_row[:, 0:1], ALU.mult, ALU.add))
                        link(v.tensor_tensor(es[:, 2, :], key[h][:, :], table_of[:, :], ALU.add))
                        link(v.tensor_reduce(es[:, 0, :], earlier[:, :, :], AX.X, ALU.max))
                        link(v.tensor_tensor(es[:, 1, :], es[:, 1, :], es[:, 0, :], ALU.mult))
                        v.wait_ge(z["chain_passed"], b)
                        v.tensor_tensor(rowid[h][:, :], es[:, 1, :], es[:, 2, :], ALU.add).then_inc(z["row_ready"], 1)
                        v.wait_ge(z["gathered"][h], i * (16 * BATCH * (2 - k)) + 16 * BATCH * (2 - k))
                        if k == 0:
                            link(v.tensor_tensor(ez[h][:, :, :], G[h][:, :, D:MSG], Q[h][:, :, 0:HEADS], ALU.add))
                            link(v.scalar_tensor_tensor(out=ez[h][:, :, :], in0=ez[h][:, :, :], scalar=SLOPE,
                                                        in1=ez[h][:, :, :], op0=ALU.mult, op1=ALU.max))
                            v.tensor_tensor(ez[h][:, :, :], ez[h][:, :, :], Q[h][:, :, HEADS:2 * HEADS],
                                            ALU.subtract).then_inc(z["ex_in"], 1)
                            v.wait_ge(z["ex_out"], b + 1)
                            m = G[h][:, :, 0:D].rearrange("p u (h f) -> p u h f", h=HEADS)
                            by = G[h][:, :, D:MSG].unsqueeze(3).to_broadcast([P, BATCH, HEADS, FH])
                        else:
                            m = G[h][:, :, 0:D]
                            by = ewb[h][:, :].unsqueeze(2).to_broadcast([P, BATCH, D])
                        v.tensor_tensor(m, m, by, ALU.mult).then_inc(z["msg_ready"], 1)
                    step.end(NBATCH // 2)

            v.wait_ge(s["const_set"], 5)
            edges(0)
            heads = lambda a: a[:, :, 0:D].rearrange("p t (h f) -> p t h f", h=HEADS)
            of_head = lambda a: a.unsqueeze(3).to_broadcast([P, NT, HEADS, FH])
            v.wait_ge(s["h_stored"], 16)
            v.wait_ge(s["exs_ready"], 1)
            link(v.tensor_tensor(heads(HN), heads(HN), of_head(exs[:, :, :]), ALU.mult))
            add_tables(0, A, B)
            den = A[:, :, D:MSG]
            step(v.tensor_tensor(A[:, :, 0:D], A[:, :, 0:D], HN[:, :, 0:D], ALU.add))
            link(v.scalar_tensor_tensor(out=den, in0=exs[:, :, :], scalar=1e-16, in1=den, op0=ALU.mult, op1=ALU.add))
            link(v.tensor_tensor(den, den, exs[:, :, :], ALU.add))
            link(v.reciprocal(den, den))
            link(v.tensor_tensor(heads(A), heads(A), of_head(den), ALU.mult))
            v.wait_ge(s["vec_in"], 16 * 7)
            link(v.tensor_tensor(A[:, :, 0:D], A[:, :, 0:D], row(BIAS), ALU.add))
            link(v.tensor_tensor(A[:, :, 0:D], A[:, :, 0:D], XN[:, :, :], ALU.add))
            norm(tile(A), tile(A))
            link(v.tensor_tensor(A[:, :, 0:D], A[:, :, 0:D], row(GAM), ALU.mult))
            link(v.tensor_tensor(A[:, :, 0:D], A[:, :, 0:D], row(BET), ALU.add))
            link(v.scalar_tensor_tensor(out=X[:, :, :], in0=A[:, :, 0:D], scalar=0.0, in1=X[:, :, :], op0=ALU.max, op1=ALU.add))

            norm(tile(X), tile(XN))
            link(v.tensor_tensor(Z, XN[:, :, :], row(WRR), ALU.mult))
            link(v.tensor_reduce(wl[:, :], Z, AX.X, ALU.add))
            v.tensor_scalar(wl[:, :], wl[:, :], small[:, 0:1], None, ALU.add).then_inc(s["wlog_ready"], 1)
            v.wait_ge(s["wlT_done"], 1)
            v.tensor_copy(wlT[:, :], PS[0:NT, 7, 0:P]).then_inc(s["wlT_ready"], 1)
            step(v.tensor_tensor(X[:, :, :], X[:, :, :], XN[:, :, :], ALU.add))
            link(v.memset(cnt[:, :, :], 0.0))
            v.wait_ge(s["wrow_in"], 16)
            wrow, scr = R3[:, 0:NPAD], R2[:, 0:NPAD]
            for t in range(NT):
                a, b = t * P, min(N, (t + 1) * P)
                w = wl[:, t:t + 1]
                if t:
                    link(v.tensor_scalar(scr[:, 0:a], wrow[:, 0:a], w, None, ALU.is_ge, ALU.add, accum_out=cnt[:, 0, t:t + 1]))
                link(v.tensor_scalar(scr[:, a:N], wrow[:, a:N], w, None, ALU.is_gt, ALU.add, accum_out=cnt[:, 1, t:t + 1]))
                link(v.scalar_tensor_tensor(out=scr[:, a:b], in0=wrow[:, a:b], scalar=w, in1=lower[:, 0:b - a],
                                            op0=ALU.is_equal, op1=ALU.mult, accum_out=cnt[:, 2, t:t + 1]))
            link(v.tensor_tensor(cnt[:, 0, :], cnt[:, 0, :], cnt[:, 1, :], ALU.add))
            link(v.tensor_tensor(cnt[:, 0, :], cnt[:, 0, :], cnt[:, 2, :], ALU.add))
            link(v.scalar_tensor_tensor(out=wm[:, :], in0=cnt[:, 0, :], scalar=float(KEPT), in1=wl[:, :],
                                        op0=ALU.is_lt, op1=ALU.mult))
            with v.Fori(0, NC) as i:
                for u in range(TC):
                    t = i * TC + u
                    v.wait_ge(s["y_done"], t + 1)
                    v.wait_ge(s["x_added"], t)
                    v.tensor_tensor(ftmp[:, u % 2, :], PS[:, 5 + u % 3, 0:D], rows[:, B2R, :], ALU.add).then_inc(s["y_kept"], 1)
                    v.wait_ge(s["y_kept"], t + 1)
                    v.scalar_tensor_tensor(out=X[:, ds(t, 1), :], in0=ftmp[:, u % 2:u % 2 + 1, :], scalar=wm[:, ds(t, 1)],
                                           in1=X[:, ds(t, 1), :], op0=ALU.mult, op1=ALU.add).then_inc(s["x_added"], 1)
            v.wait_ge(s["x_added"], NT)

            norm(tile(X), tile(XN))
            edges(1)
            link(v.tensor_scalar(small[:, 3:4], small[:, 1:2], 1.0, None, ALU.add))
            add_tables(1, Z, R3[:, 0:NT * D].rearrange("p (t c) -> p t c", t=NT))
            v.scalar_tensor_tensor(out=Z, in0=XN[:, :, :], scalar=small[:, 3:4], in1=Z, op0=ALU.mult,
                                   op1=ALU.add).then_inc(s["a_ready"], 1)

            def batch_norm(n, of, g, be):
                for m in range(KD):
                    for j in range(7):
                        step(v.bn_stats(bst[:, m, j, :], of[:, m, j * 512:min(N, (j + 1) * 512)]))
                step.wait()
                for m in range(KD):
                    v.bn_aggr(bmv[:, m, :], bst[:, m, :, :].rearrange("p j c -> p (j c)")).then_inc(s["bnv_ready"], 1)
                v.wait_ge(s["bnstd_ready"], n)
                v.wait_ge(s["bnv_ready"], KD * n)
                link(v.reciprocal(bsc[:, 0, :], bsc[:, 0, :]))
                link(v.tensor_tensor(bsc[:, 1, :], bsc[:, 0, :], gcol[:, g, :], ALU.mult))
                link(v.tensor_tensor(bsc[:, 2, :], bmv[:, :, 0], bsc[:, 1, :], ALU.mult))
                v.tensor_tensor(bsc[:, 2, :], gcol[:, be, :], bsc[:, 2, :], ALU.subtract).then_inc(s["bn_ready"], 1)

            v.wait_ge(s["gw_in"], 16 * 8)
            v.wait_ge(s["h1_kept"], 4 * NC)
            batch_norm(1, H1, 1, 2)
            v.wait_ge(s["h2_kept"], 4 * NC)
            batch_norm(2, H2, 4, 5)
            with v.Fori(0, NC) as i:
                xi = X[:, ds(i * TC, TC), :]
                v.wait_ge(s["back_done"], i + 1)
                v.tensor_tensor(xi, xi, PSF[:, 0:KD * CW].rearrange("p (t c) -> p t c", t=TC), ALU.add).then_inc(s["back_added"], 1)
            v.wait_ge(s["back_added"], NC)

            norm(tile(X), tile(XN))
            v.wait_ge(s["mean_done"], 1)
            v.tensor_scalar(mrow[:, :], PS[0:1, 7, 0:D], 1.0 / N, None, ALU.mult).then_inc(s["mrow_ready"], 1)
            v.wait_ge(s["mcol_done"], 1)
            v.tensor_copy(mcol[:, :], PS[:, 6, 0:KD]).then_inc(s["mcol_ready"], 1)
            v.wait_ge(s["logit_done"], 1)
            v.wait_ge(s["r1_in"], 32)
            link(v.tensor_tensor(rt[:, 0, :], PS[0:1, 7, 0:EXPERTS], bre[:, :], ALU.add))

            def softmax(n, of, ex, to, w):
                link(v.tensor_reduce(r1[:, 0:1], rt[:, of, 0:w], AX.X, ALU.max))
                v.tensor_scalar(r1[:, 1:2], r1[:, 0:1], -1.0, None, ALU.mult).then_inc(s["rexp_in"], 1)
                v.wait_ge(s["rexp_out"], n)
                link(v.tensor_reduce(r1[:, 2:3], rt[:, ex, 0:w], AX.X, ALU.add))
                link(v.reciprocal(r1[:, 3:4], r1[:, 2:3]))
                return v.tensor_scalar(rt[:, to, 0:w], rt[:, ex, 0:w], r1[:, 3:4], None, ALU.mult)

            link(softmax(1, 0, 1, 2, EXPERTS))
            link(v.tensor_scalar(rt[:, 3, :], rt[:, 2, :], float(N), 1e-30, ALU.mult, ALU.max))
            link(v.reciprocal(rt[:, 3, :], rt[:, 3, :]))
            link(v.tensor_scalar(rt[:, 3, :], rt[:, 3, :], CAPACITY, 1.0, ALU.mult, ALU.min))
            link(v.tensor_tensor(rt[:, 4, :], rt[:, 2, :], rt[:, 3, :], ALU.mult))
            link(softmax(2, 4, 5, 6, EXPERTS))
            v.max(rt[:, 7, :], rt[:, 6, :]).then_inc(s["pair_ready"], 1)
            v.wait_ge(s["pair_ready"], 1)
            v.max_index(ri[:, :], rt[:, 7, :], rt[:, 6, :]).then_inc(s["pair_ready"], 1)
            softmax(3, 7, 8, 9, 2).then_inc(s["pairw_ready"], 1)
            v.wait_ge(s["wb_done"], 1)
            link(v.tensor_copy(wexp[:, :], PS[:, 6, 0:2]))
            v.wait_ge(s["expert_b2_in"], 64)
            link(v.tensor_scalar(rows[:, B2R, :], rows[:, B2R, :], wexp[:, 0:1], None, ALU.mult))
            link(v.scalar_tensor_tensor(out=rows[:, B2R, :], in0=rows[:, B2B, :], scalar=wexp[:, 1:2], in1=rows[:, B2R, :],
                                        op0=ALU.mult, op1=ALU.add))
            v.wait_ge(s["expert_w2_in"], 32)
            for j in range(2):
                wj = w2s[:, j * MH // 2:(j + 1) * MH // 2, :]
                v.tensor_scalar(wj, wj, wexp[:, j:j + 1], None, ALU.mult).then_inc(s["w2_scaled"], 1)
            link(v.tensor_tensor(Z, XN[:, :, :], row(B2R), ALU.add))
            with v.Fori(0, NC) as i:
                for u in range(TC):
                    t = i * TC + u
                    v.wait_ge(s["y_done"], t + (NT + 1))
                    v.tensor_tensor(Z[:, ds(t, 1), :], PS[:, 5 + u % 3:6 + u % 3, 0:D], Z[:, ds(t, 1), :],
                                    ALU.add).then_inc(s["y_kept"], 1)
            v.wait_ge(s["y_kept"], 2 * NT)
            norm(tile(Z), tile(Z))
            link(v.tensor_tensor(Z, Z, row(GAM), ALU.mult))
            link(v.tensor_tensor(Z, Z, row(BET), ALU.add))
            v.tensor_tensor(X[:, :, :], Z, X[:, :, :], ALU.add).then_inc(s["out_ready"], 1)


_INS = ["x", "src", "dst", "edge_weight", "L0_gnn_W", "L0_gnn_att_src", "L0_gnn_att_dst", "L0_gnn_bias",
        "L0_gnn_ln_gamma", "L0_gnn_ln_beta", "L0_ffn_wr", "L0_ffn_br", "L0_ffn_w1", "L0_ffn_b1", "L0_ffn_w2",
        "L0_ffn_b2", "L1_gnn_eps", "L1_gnn_W1", "L1_gnn_b1", "L1_gnn_g1", "L1_gnn_be1", "L1_gnn_W2", "L1_gnn_b2",
        "L1_gnn_g2", "L1_gnn_be2", "L1_ffn_Wr", "L1_ffn_br", "L1_ffn_W1", "L1_ffn_b1", "L1_ffn_W2", "L1_ffn_b2",
        "L1_ffn_gamma", "L1_ffn_beta"]


def kernel(**inputs):
    import numpy as _np
    import concourse.bacc as _bacc
    from concourse import mybir as _mybir
    from concourse.bass_utils import run_bass_kernel_spmd as _run

    nc = _bacc.Bacc("TRN2", target_bir_lowering=False, num_devices=1)
    arrays, args = {}, []
    for name in _INS:
        a = _np.ascontiguousarray(inputs[name])
        arrays[f"in_{name}_dram"] = a
        args.append(nc.dram_tensor(f"in_{name}_dram", a.shape, _mybir.dt.from_np(a.dtype), kind="ExternalInput").ap())
    args.append(nc.dram_tensor("out_dram", (N, D), F32, kind="ExternalOutput").ap())
    build(nc, *args)
    r = _run(nc, [arrays], core_ids=[0])
    return r.results[0]["out_dram"]
```

```python
import concourse.bass as bass
from concourse import mybir
from contextlib import ExitStack

F32 = mybir.dt.float32
I32 = mybir.dt.int32
U32 = mybir.dt.uint32
ALU = mybir.AluOpType
ACT = mybir.ActivationFunctionType
AX = mybir.AxisListType
ds = bass.ds

P = 128
N = 3125
D = 256
KD = D // P
E = 50000
NT = -(-N // P)
NPAD = NT * P
TAIL = N - (NT - 1) * P
TC = 5
NC = NT // TC
CW = TC * P
HALF = CW // 2
HEADS = 4
FH = D // HEADS
HID = 1024
MH = HID // P
EXPERTS = 8
FE = 512
SLOPE = 0.2
EPS = 1e-5
KEPT = int(0.5 * N) - 1
CAPACITY = float(-(-N * 5 // (4 * EXPERTS)))
HEADROOM = 60.0

EROWS = -(-E // P)
LAST = E - (EROWS - 1) * P
GR4 = 4
FIELDS = 4
BATCH = 4
RING = 4
NBATCH = 104
ITEMS = NBATCH * BATCH
ITEMPAD = ITEMS + RING * BATCH
BUCKETED = GR4 * P
CAP = 64.0
ROUND = 12582912.0
MSG = D + HEADS
SPARE = NPAD - 1
ROWS = NPAD + P
TABLES = BATCH
assert EROWS + NT - 1 <= ITEMS <= GR4 * P and ITEMPAD <= GR4 * P and NBATCH % RING == 0 and NT == NC * TC
assert HEADROOM < CAP


FREE = 1


class Steps:

    def __init__(self, eng, sem):
        self.eng, self.sem, self.n, self.base = eng, sem, 0, None

    def value(self):
        return self.n if self.base is None else self.base + self.n

    def __call__(self, ins):
        ins.then_inc(self.sem, 1)
        self.n += 1

    def wait(self):
        self.eng.wait_ge(self.sem, self.value())

    def begin(self, i, per):
        self.before, self.per, self.base, self.n = self.n, per, i * per + self.n, 0

    def end(self, trips):
        assert self.n == self.per, (self.n, self.per)
        self.n, self.base = self.before + trips * self.per, None


def build(nc, x, src, dst, edge_weight, g0_W, g0_as, g0_ad, g0_bias, g0_gamma, g0_beta, f0_wr, f0_br,
          f0_w1, f0_b1, f0_w2, f0_b2, g1_eps, g1_W1, g1_b1, g1_g1, g1_be1, g1_W2, g1_b2, g1_g2, g1_be2,
          f1_Wr, f1_br, f1_W1, f1_b1, f1_W2, f1_b2, f1_gamma, f1_beta, out):
    ctx = ExitStack()
    with ctx:
        def sb(name, shape, dt=F32):
            return ctx.enter_context(nc.sbuf_tensor(name, shape, dt))

        def sem(name):
            return ctx.enter_context(nc.semaphore(name))

        htab = nc.dram_tensor("htab", [NPAD, MSG], F32).ap()
        etab = nc.dram_tensor("etab", [BUCKETED + ITEMS, P * FIELDS], F32).ap()
        ttab = nc.dram_tensor("ttab", [GR4 * P], I32).ap()
        sum1 = nc.dram_tensor("sum1", [TABLES * ROWS, D], F32).ap()
        wtab = nc.dram_tensor("wtab", [NPAD], F32).ap()

        X = sb("X", [P, NT, D])
        XN = sb("XN", [P, NT, D])
        R1 = sb("R1", [P, NT * (MSG + HEADS)])
        R2 = sb("R2", [P, (NT + 1) * MSG])
        R3 = sb("R3", [P, NT * MSG])
        HN = R1[:, :].rearrange("p (t c) -> p t c", t=NT)
        A = R2[:, 0:NT * MSG].rearrange("p (t c) -> p t c", t=NT)
        B = R3[:, :].rearrange("p (t c) -> p t c", t=NT)
        H1 = R1[:, 0:KD * NPAD].rearrange("p (k n) -> p k n", k=KD)
        H2 = R3[:, 0:KD * NPAD].rearrange("p (k n) -> p k n", k=KD)
        Z = R2[:, 0:NT * D].rearrange("p (t c) -> p t c", t=NT)
        xc = sb("xc", [P, TC, D])
        xt = sb("xt", [P, KD, CW])
        ht = sb("ht", [P, MH * CW])
        w1s = sb("w1s", [P, KD, HID])
        w2s = sb("w2s", [P, MH, D])
        b1s = sb("b1s", [P, MH])
        wext = sb("wext", [P, KD, MSG + HEADS])
        gw = sb("gw", [P, 2, KD, D])
        gcol = sb("gcol", [P, 6, KD])
        wr1 = sb("wr1", [P, KD, EXPERTS])
        rows = sb("rows", [P, 8, D])
        ATS, ATD, BIAS, GAM, BET, WRR, B2R, B2B = range(8)
        small = sb("small", [P, 4])
        ident = sb("ident", [P, P])
        ones = sb("ones", [P, P])
        lower = sb("lower", [P, P])
        spare_row = sb("spare_row", [P, 1])
        table_of = sb("table_of", [P, BATCH])
        st = sb("st", [P, NT, 6])
        mean = sb("mean", [P, NT])
        var = sb("var", [P, NT])
        rstd = sb("rstd", [P, NT])
        t1 = sb("t1", [P, NT])
        t2 = sb("t2", [P, NT])
        zs = sb("zs", [P, NT, HEADS])
        zb = sb("zb", [P, NT, HEADS])
        qn = sb("qn", [P, NT, 2 * HEADS])
        exs = sb("exs", [P, NT, HEADS])
        amax = sb("amax", [P, HEADS])
        gmax = sb("gmax", [P, HEADS])
        wl = sb("wl", [P, NT])
        wm = sb("wm", [P, NT])
        wlT = sb("wlT", [NT, P])
        cnt = sb("cnt", [P, 3, NT])
        ftmp = sb("ftmp", [P, 2, D])
        bst = sb("bst", [P, KD, 7, 6])
        bmv = sb("bmv", [P, KD, 2])
        bsc = sb("bsc", [P, 3, KD])
        rt = sb("rt", [1, 12, EXPERTS])
        ri = sb("ri", [1, EXPERTS], U32)
        r1 = sb("r1", [1, 8])
        mrow = sb("mrow", [1, D])
        mcol = sb("mcol", [P, KD])
        wexp = sb("wexp", [P, 2])
        bre = sb("bre", [1, EXPERTS])

        srcT = sb("srcT", [P, ITEMPAD])
        dloc = sb("dloc", [P, ITEMPAD])
        ewT = sb("ewT", [P, ITEMPAD])
        tiles = sb("tiles", [1, GR4 * P], I32)
        iota = sb("iota", [P, P])
        number = sb("number", [P, GR4])
        first = sb("first", [P, GR4])
        f1t, f2t = sb("f1t", [P, GR4]), sb("f2t", [P, GR4])
        item_row = sb("item_row", [P, GR4])
        item_rowI = sb("item_rowI", [P, GR4], I32)
        item_tile = sb("item_tile", [P, GR4])
        item_node = sb("item_node", [P, GR4])
        tileT = sb("tileT", [GR4, P], I32)
        unsorted = sb("unsorted", [P, 2])
        unsortedI = sb("unsortedI", [1, 1], I32)
        bk = sb("bk", [P, 5, NT])
        put_at = sb("put_at", [P, 1], I32)
        put_rec = sb("put_rec", [P, FIELDS])

        def taker(of, limit):
            at = [0]

            def part(n):
                at[0] += n
                assert at[0] <= limit
                return of[:, at[0] - n:at[0]]
            return part

        part = taker(R3, NT * MSG)
        rec = part(BUCKETED * FIELDS).rearrange("p (g e f) -> p g e f", g=GR4, e=P)
        got = part(BUCKETED * FIELDS).rearrange("p (g e f) -> p g e f", g=GR4, e=P)
        dst_next = part(BUCKETED).rearrange("p (g e) -> p g e", g=GR4)
        part = taker(ht, MH * CW)
        at_least = part(GR4 * BUCKETED).rearrange("p (g i) -> p g i", g=GR4)
        items_iota = part(BUCKETED)
        tile_e, in_tile, ranks, place = (part(BUCKETED) for _ in range(4))
        part = taker(w1s[:, :, :].rearrange("p k n -> p (k n)"), KD * HID)
        srcI, dstI, dst_nextI = (part(BUCKETED).bitcast(I32).rearrange("p (g e) -> p g e", g=GR4) for _ in range(3))
        ewI = part(BUCKETED).rearrange("p (g e) -> p g e", g=GR4)
        placeI = srcI.rearrange("p g e -> p (g e)")
        part = taker(ht, MH * CW)
        G = [part(BATCH * MSG).rearrange("p (u c) -> p u c", u=BATCH) for _ in range(RING)]
        part = taker(R3, NT * MSG)
        edge_node = [part(BATCH * P).rearrange("p (u n) -> p u n", u=BATCH) for _ in range(RING)]
        node_edge = [part(BATCH * P).rearrange("p (u e) -> p u e", u=BATCH) for _ in range(2)]
        part = taker(ht, MH * CW)
        weight_node = [part(BATCH * P).rearrange("p (u n) -> p u n", u=BATCH) for _ in range(2)]
        node_src = [part(BATCH * P).rearrange("p (u e) -> p u e", u=BATCH) for _ in range(2)]
        M = [part(BATCH * D).rearrange("p (u c) -> p u c", u=BATCH) for _ in range(2)]
        xcf = xc[:, :, :].rearrange("p t c -> p (t c)")
        same = [xcf[:, j * BATCH * P:(j + 1) * BATCH * P].rearrange("p (u e) -> p u e", u=BATCH) for j in range(2)]
        earlier = xcf[:, 2 * BATCH * P:2 * BATCH * P + P]
        ez = [sb(f"ez{h}", [P, BATCH, HEADS]) for h in range(2)]
        gat = [sb(f"gat{j}", [P, BATCH], I32) for j in range(RING)]
        key = [sb(f"key{h}", [P, BATCH]) for h in range(2)]
        rowid = [sb(f"rowid{h}", [P, BATCH], I32) for h in range(2)]
        es = sb("es", [P, 3, BATCH])

        PS = ctx.enter_context(nc.psum_tensor("PS", [P, 8, 512], F32))
        PSF = PS[:, :, :].rearrange("p b c -> p (b c)")

        names = """x_in idx_clear idx_in watt_in vec_in f0w_in gw_in r1_in zero_set zeroed ones_set ident_set
            const_set iota_set dve stat var_ready std_ready norm_done xc_ready xt_read xt_ready wext_ready
            rec_ready order_max order_known flag_ready at_least_ready rows_counted item_row_ready rec_stored got_in
            dloc_ready fields_turned fields_kept tileT_done tileT_ready tiles_stored tiles_in
            bucket bucket_counted bucket_summed place_ready put_set put_done
            proj_done proj_kept amax_ready gmax_ready shift_ready exs_ready h_stored
            sums1_in table_added wlog_ready wlT_done wlT_ready wrow_stored wrow_in
            hid_done hid_kept y_done y_kept x_added h1_done h1_kept h2_done h2_kept h1n_ready h2n_ready
            bnv_ready bnstd_ready bn_ready a_ready back_done back_added mean_done mrow_ready mcol_done
            mcol_ready logit_done rexp_in rexp_out pair_ready pairw_ready wb_done expert_w1_in
            expert_w2_in expert_b2_in w2_scaled out_ready stored pool_held
            staged edge_node_ready turned node_edge_kept spread ex_in ex_out msg_ready tile_summed tile_added
            key_staged rowed weights_ready node_src_done node_src_kept row_ready summed sums_kept""".split()
        s = {n: sem(n) for n in names}
        gathered = [sem(f"gathered{j}") for j in range(RING)]
        added = [sem(f"added{u}") for u in range(TABLES)]
        block = ctx.enter_context(nc.Block())

        def nodes(ap):
            return ap.rearrange("(t p) c -> p t c", p=P)

        def on_all(ap):
            return ap.rearrange("(o c) -> o c", o=1).to_broadcast([P, ap.shape[0]])

        def batches(eng, run, step=None, per=0):
            for j in range(RING):
                run(j, j, 0)
            with eng.Fori(1, NBATCH // RING) as i:
                if step:
                    step.begin(i - 1, RING * per)
                for j in range(RING):
                    run(i * RING + j, j, i)
                if step:
                    step.end(NBATCH // RING - 1)

        def after(b, n):
            return not isinstance(b, int) or b >= n

        def items(b):
            return ds(b * BATCH, BATCH)

        @block.sync
        def _(sp):
            full, rest = (GR4 - 1) * P, EROWS - 1 - (GR4 - 1) * P
            sp.wait_ge(s["idx_clear"], 4)
            for a, t, at in ((dst, dstI, 0), (dst, dst_nextI, 1), (src, srcI, 0), (edge_weight, ewI, 0)):
                sp.dma_start(t[:, 0:GR4 - 1, :],
                             a[at:at + full * P].rearrange("(g p e) -> p g e", p=P, e=P)).then_inc(s["idx_in"], 16)
                sp.dma_start(t[0:rest, GR4 - 1, :],
                             a[at + full * P:at + (full + rest) * P].rearrange("(p e) -> p e", e=P)).then_inc(s["idx_in"], 16)
                sp.dma_start(t[rest:rest + 1, GR4 - 1, 0:LAST - at],
                             a[at + (full + rest) * P:E].rearrange("(p e) -> p e", p=1)).then_inc(s["idx_in"], 16)
            sp.wait_ge(s["dve"], 1)
            sp.dma_start(X[:, 0:NT - 1, :], nodes(x[0:(NT - 1) * P, :])).then_inc(s["x_in"], 16)
            sp.dma_start(X[0:TAIL, NT - 1, :], x[(NT - 1) * P:N, :]).then_inc(s["x_in"], 16)
            sp.dma_start(wext[:, :, 0:D], g0_W.rearrange("(k p) n -> p k n", p=P)).then_inc(s["watt_in"], 16)
            sp.dma_start(rows[:, ATS, :], on_all(g0_as.rearrange("h f -> (h f)"))).then_inc(s["watt_in"], 16)
            sp.dma_start(rows[:, ATD, :], on_all(g0_ad.rearrange("h f -> (h f)"))).then_inc(s["watt_in"], 16)
            sp.wait_ge(s["rec_ready"], 4)
            pads = ITEMS // 4
            for g in range(4):
                at = BUCKETED + g * pads
                sp.dma_start(etab[at:at + pads, :],
                             rec[P - pads:P, GR4 - 1, :, :].rearrange("p e f -> p (e f)")).then_inc(s["rec_stored"], 16)
            sp.dma_start(etab[0:BUCKETED, :].rearrange("(g p) c -> p g c", p=P),
                         rec.rearrange("p g e f -> p g (e f)")).then_inc(s["rec_stored"], 16)
            for j, v in ((BIAS, g0_bias), (GAM, g0_gamma), (BET, g0_beta), (B2R, f0_b2)):
                sp.dma_start(rows[:, j, :], on_all(v)).then_inc(s["vec_in"], 16)
            sp.dma_start(rows[:, WRR, :], on_all(f0_wr.rearrange("d o -> (d o)"))).then_inc(s["vec_in"], 16)
            sp.dma_start(small[:, 0:1], on_all(f0_br)).then_inc(s["vec_in"], 16)
            sp.dma_start(small[:, 1:2], on_all(g1_eps)).then_inc(s["vec_in"], 16)
            sp.wait_ge(s["zero_set"], 1)
            v = sum1.rearrange("(p r) c -> p (r c)", p=P)
            for r in range(0, TABLES * ROWS // P, NT + 1):
                sp.dma_start(v[:, r * D:(r + NT + 1) * D], R2[:, 0:(NT + 1) * D]).then_inc(s["zeroed"], 16)
            sp.wait_ge(s["tileT_ready"], 1)
            sp.dma_start(ttab.rearrange("(g p) -> g p", p=P), tileT[:, :]).then_inc(s["tiles_stored"], 16)
            sp.wait_ge(s["tiles_stored"], 16)
            sp.dma_start(tiles[:, :], ttab.rearrange("(o c) -> o c", o=1)).then_inc(s["tiles_in"], 16)
            sp.wait_ge(s["got_in"], 16 * GR4)
            sp.dma_start(w1s[:, :, :], f0_w1.rearrange("(k p) n -> p k n", p=P)).then_inc(s["f0w_in"], 16)
            sp.dma_start(w2s[:, :, :], f0_w2.rearrange("(k p) n -> p k n", p=P)).then_inc(s["f0w_in"], 16)
            with nc.allow_non_contiguous_dma(reason="short vectors, one feature on a partition"):
                sp.dma_start(b1s[:, :], f0_b1.rearrange("(m p) -> p m", p=P)).then_inc(s["f0w_in"], 16)
                for j, v in enumerate((g1_b1, g1_g1, g1_be1, g1_b2, g1_g2, g1_be2)):
                    sp.dma_start(gcol[:, j, :], v.rearrange("(m p) -> p m", p=P)).then_inc(s["gw_in"], 16)
            for j, w in enumerate((g1_W1, g1_W2)):
                sp.dma_start(gw[:, j, :, :], w.rearrange("(k p) n -> p k n", p=P)).then_inc(s["gw_in"], 16)
            sp.dma_start(wr1[:, :, :], f1_Wr.rearrange("(k p) n -> p k n", p=P)).then_inc(s["r1_in"], 16)
            sp.dma_start(bre[:, :], f1_br.rearrange("(o c) -> o c", o=1)).then_inc(s["r1_in"], 16)

            sp.wait_ge(s["proj_kept"], NT + FREE)
            sp.dma_start(nodes(htab), HN[:, :, 0:MSG]).then_inc(s["h_stored"], 16)

            sp.wait_ge(s["wlT_ready"], 1)
            sp.dma_start(wtab.rearrange("(t p) -> t p", p=P), wlT[:, :]).then_inc(s["wrow_stored"], 16)
            sp.wait_ge(s["wrow_stored"], 16)
            sp.dma_start(R3[:, 0:NPAD], on_all(wtab)).then_inc(s["wrow_in"], 16)

            for u in range(TABLES):
                sp.wait_ge(added[u], 16 * NBATCH)
            for u in range(TABLES):
                if u >= 2:
                    sp.wait_ge(s["table_added"], u - 1)
                dest = Z if u == 0 else R3[:, 0:NT * D].rearrange("p (t c) -> p t c", t=NT)
                sp.dma_start(dest, nodes(sum1[u * ROWS:u * ROWS + NPAD, :])).then_inc(s["sums1_in"], 16)

            sp.wait_ge(s["norm_done"], 5 * NT)
            sp.dma_start(rows[:, GAM, :], on_all(f1_gamma)).then_inc(s["expert_b2_in"], 16)
            sp.dma_start(rows[:, BET, :], on_all(f1_beta)).then_inc(s["expert_b2_in"], 16)
            sp.wait_ge(s["pair_ready"], 2)
            for j in range(2):
                e = sp.value_load(ri[0:1, j:j + 1], min_val=0, max_val=EXPERTS - 1)
                sp.dma_start(w1s[:, :, j * FE:(j + 1) * FE],
                             f1_W1.rearrange("e (k p) f -> p (e k) f", p=P)[:, ds(e * KD, KD), :]).then_inc(s["expert_w1_in"], 16)
                sp.dma_start(w2s[:, j * MH // 2:(j + 1) * MH // 2, :],
                             f1_W2.rearrange("e (k p) d -> p (e k) d", p=P)[:, ds(e * (FE // P), FE // P), :]).then_inc(s["expert_w2_in"], 16)
                with nc.allow_non_contiguous_dma(reason="a short vector, one feature on a partition"):
                    sp.dma_start(b1s[:, j * MH // 2:(j + 1) * MH // 2],
                                 f1_b1.rearrange("e (k p) -> p (e k)", p=P)[:, ds(e * (FE // P), FE // P)]).then_inc(s["expert_w1_in"], 16)
                sp.dma_start(rows[:, B2R + j, :], f1_b2[ds(e, 1), :].to_broadcast([P, D])).then_inc(s["expert_b2_in"], 16)
            sp.wait_ge(s["out_ready"], 1)
            sp.dma_start(nodes(out[0:(NT - 1) * P, :]), X[:, 0:NT - 1, :]).then_inc(s["stored"], 16)
            sp.dma_start(out[(NT - 1) * P:N, :], X[0:TAIL, NT - 1, :]).then_inc(s["stored"], 16)
            sp.wait_ge(s["stored"], 32)

        @block.gpsimd
        def _(pool):
            pool.memset(dstI[:, :, :], SPARE).then_inc(s["idx_clear"], 1)
            pool.memset(dst_nextI[:, :, :], SPARE).then_inc(s["idx_clear"], 1)
            pool.memset(srcI[:, :, :], 0).then_inc(s["idx_clear"], 1)
            pool.memset(ewI[:, :, :], 0.0).then_inc(s["idx_clear"], 1)
            pool.memset(rec[:, :, :, 3], 0.0).then_inc(s["rec_ready"], 1)
            pool.iota(items_iota, pattern=[[1, BUCKETED]], base=0, channel_multiplier=0,
                      allow_small_or_imprecise_dtypes=True).then_inc(s["iota_set"], 1)
            pool.iota(number[:, :], pattern=[[P, GR4]], base=0, channel_multiplier=1,
                      allow_small_or_imprecise_dtypes=True).then_inc(s["iota_set"], 1)
            pool.memset(ident[:, :], 1.0).then_inc(s["ones_set"], 1)
            pool.memset(lower[:, :], 1.0).then_inc(s["ones_set"], 1)
            pool.memset(ones[:, :], 1.0).then_inc(s["const_set"], 1)
            pool.wait_ge(s["ones_set"], 2)
            pool.affine_select(out=ident[:, :], in_=ident[:, :], compare_op=ALU.is_equal, fill=0.0, base=0,
                               pattern=[[-1, P]], channel_multiplier=1).then_inc(s["ident_set"], 1)
            pool.affine_select(out=lower[:, :], in_=lower[:, :], compare_op=ALU.is_gt, fill=0.0, base=0,
                               pattern=[[-1, P]], channel_multiplier=1).then_inc(s["const_set"], 1)
            pool.iota(spare_row[:, :], pattern=[[0, 1]], base=NPAD, channel_multiplier=1,
                      allow_small_or_imprecise_dtypes=True).then_inc(s["const_set"], 1)
            pool.iota(table_of[:, :], pattern=[[ROWS, BATCH]], base=0, channel_multiplier=0,
                      allow_small_or_imprecise_dtypes=True).then_inc(s["const_set"], 1)
            pool.memset(small[:, 2:3], EPS).then_inc(s["const_set"], 1)
            pool.iota(iota[:, :], pattern=[[1, P]], base=0, channel_multiplier=0,
                      allow_small_or_imprecise_dtypes=True).then_inc(s["const_set"], 1)
            pool.wait_ge(s["order_max"], 1)
            pool.partition_all_reduce(unsorted[:, 1:2], unsorted[:, 0:1], P, bass.bass_isa.ReduceOp.max).then_inc(s["order_known"], 1)

            def chunks(stage, source, kept):
                with pool.Fori(0, NC) as i:
                    pool.wait_ge(s["xt_read"], i + (NC * stage + FREE))
                    pool.wait_ge(*kept)
                    pool.tensor_copy(xc[:, :, :], source[:, ds(i * TC, TC), :]).then_inc(s["xc_ready"], 1)

            def hold():
                pool.sem_inc(s["pool_held"], 1)

            pool.wait_ge(s["rec_stored"], 16 * 5)
            pool.wait_ge(s["flag_ready"], 1)
            flag = pool.value_load(unsortedI[0:1, 0:1])
            with pool.If(flag > 0):
                pool.wait_ge(s["place_ready"], 1)
                spots = etab.rearrange("r (e f) -> (r e) f", f=FIELDS)
                recs = rec.rearrange("p g e f -> p (g e) f")
                pool.sem_inc(s["put_done"], 16)
                with pool.Fori(0, BUCKETED) as c:
                    pool.wait_ge(s["put_done"], c * 16 + 16)
                    pool.tensor_copy(put_at[:, :], placeI[:, ds(c, 1)]).then_inc(s["put_set"], 1)
                    pool.tensor_copy(put_rec[:, :].unsqueeze(1), recs[:, ds(c, 1), :]).then_inc(s["put_set"], 1)
                    pool.wait_ge(s["put_set"], c * 2 + 2)
                    hold()
                    pool.indirect_dma_start(spots, bass.IndirectOffsetOnAxis(ap=put_at[:, 0:1], axis=0),
                                            put_rec[:, :], None).then_inc(s["put_done"], 16)
                pool.wait_ge(s["put_done"], 16 * (BUCKETED + 1))
            pool.wait_ge(s["item_row_ready"], 1)
            for g in range(GR4):
                pool.indirect_dma_start(got[:, g, :, :].rearrange("p e f -> p (e f)"), None, etab,
                                        bass.IndirectOffsetOnAxis(ap=item_rowI[:, g:g + 1], axis=0)
                                        ).then_inc(s["got_in"], 16)

            chunks(0, XN, (s["norm_done"], NT))
            pool.wait_ge(s["amax_ready"], 1)
            pool.partition_all_reduce(gmax[:, :], amax[:, :], P, bass.bass_isa.ReduceOp.max).then_inc(s["gmax_ready"], 1)

            def gather(b, j, i):
                pool.wait_ge(s["staged"], b + 1)
                if after(b, RING):
                    pool.wait_ge(s["tile_summed"], (b - (RING - 1)) * BATCH)
                hold()
                for u in range(BATCH):
                    pool.indirect_dma_start(G[j][:, u, :], None, htab,
                                            bass.IndirectOffsetOnAxis(ap=gat[j][:, u:u + 1], axis=0)
                                            ).then_inc(gathered[j], 16)

            pool.wait_ge(s["h_stored"], 16)
            batches(pool, gather)

            chunks(1, XN, (s["norm_done"], 3 * NT))

            def scatter(b, j, i):
                for u in range(BATCH):
                    if after(b, 1):
                        pool.wait_ge(added[u], b * 16)
                    pool.wait_ge(s["sums_kept"], b * BATCH + (u + 1))
                    pool.wait_ge(s["row_ready"], b + 1)
                    hold()
                    pool.indirect_dma_start(sum1, bass.IndirectOffsetOnAxis(ap=rowid[j % 2][:, u:u + 1], axis=0),
                                            M[j % 2][:, u, :], None, compute_op=ALU.add).then_inc(added[u], 16)

            pool.wait_ge(s["zeroed"], 16 * TABLES)
            batches(pool, scatter)
            chunks(2, Z, (s["a_ready"], 1))
            chunks(3, XN, (s["norm_done"], 5 * NT))

        @block.scalar
        def _(act):
            stds = [0]
            HT = ht[:, :].rearrange("p (m c) -> p m c", m=MH)

            def apart():
                act.wait_ge(s["const_set"], 6)

            def std():
                stds[0] += 1
                act.wait_ge(s["const_set"], 6)
                act.wait_ge(s["var_ready"], stds[0])
                act.activation(rstd[:, :], var[:, :], ACT.Sqrt, bias=small[:, 2:3]).then_inc(s["std_ready"], 1)

            def turned(i, stage, used, before):
                act.wait_ge(s["xt_read"], i + (NC * stage + 1 + FREE))
                act.wait_ge(s[used], before + FREE)
                act.activation(xt[:, :, :].rearrange("p k c -> p (k c)"), PSF[:, 0:KD * CW],
                               ACT.Copy).then_inc(s["xt_ready"], 1)

            for q in ("xt_ready", "h1_kept", "h2_kept"):
                act.sem_inc(s[q], FREE)
            std()
            with act.Fori(0, NC) as i:
                turned(i, 0, "proj_done", i * TC)
            for f, to in enumerate((srcT, dloc, ewT)):
                act.wait_ge(s["fields_turned"], f + 1)
                act.activation(to[:, :], PS[:, f, 0:ITEMPAD], ACT.Copy).then_inc(s["fields_kept"], 1)
            act.preload_act_table(ACT.Exp)
            act.wait_ge(s["shift_ready"], 2)
            act.activation(exs[:, :, :], zb[:, :, :], ACT.Exp).then_inc(s["exs_ready"], 1)

            def stage_gather(b, j):
                act.wait_ge(s["fields_kept"], 3)
                act.activation(gat[j][:, :], srcT[:, items(b)], ACT.Copy).then_inc(s["staged"], 1)

            def keep_spread(b, h):
                act.wait_ge(s["turned"], b + 1)
                act.activation(node_edge[h], PS[:, h, :].rearrange("p (u e) -> p u e", u=BATCH),
                               ACT.Copy).then_inc(s["node_edge_kept"], 1)

            for j in range(RING):
                stage_gather(j, j)
            keep_spread(0, 0)

            def attention(b, j, i):
                act.wait_ge(s["ex_in"], b + 1)
                act.activation(G[j][:, :, D:MSG], ez[j % 2][:, :, :], ACT.Exp).then_inc(s["ex_out"], 1)
                stage_gather(b + RING, j)
                keep_spread(b + 1, 1 - j % 2)

            batches(act, attention)
            std()
            std()

            def ffn(stage, j, func, loaded):
                act.preload_act_table(func)
                act.wait_ge(*loaded)
                groups = 2 * MH
                with act.Fori(0, NC) as i:
                    turned(i, stage, "hid_done", i * groups + j * NC * groups)
                    for g in range(groups):
                        m, half = g // 2, g % 2
                        act.wait_ge(s["hid_done"], i * groups + (j * NC * groups + g + 1 + FREE))
                        act.activation(HT[:, m, half * HALF:(half + 1) * HALF], PS[:, 3 + g % 2, 0:HALF], func,
                                       bias=b1s[:, m:m + 1]).then_inc(s["hid_kept"], 1)

            ffn(1, 0, ACT.Gelu_apprx_tanh, (s["f0w_in"], 48))
            std()

            def stage_key(b, h):
                act.wait_ge(s["fields_kept"], 3)
                act.activation(key[h][:, :], srcT[:, items(b)], ACT.Copy).then_inc(s["key_staged"], 1)

            stage_key(0, 0)

            def sum_by_source(b, j, i):
                h = j % 2
                if after(b, 1):
                    act.wait_ge(s["row_ready"], b)
                stage_key(b + 1, 1 - h)
                act.wait_ge(s["node_src_done"], b + 1)
                act.activation(node_src[h], PS[:, 2 + h, :].rearrange("p (u e) -> p u e", u=BATCH),
                               ACT.Copy).then_inc(s["node_src_kept"], 1)
                for u in range(BATCH):
                    if after(b, 2):
                        act.wait_ge(added[u], (b - 1) * 16)
                    act.wait_ge(s["summed"], b * BATCH + (u + 1))
                    act.activation(M[h][:, u, :], PS[:, 4 + u, 0:D], ACT.Copy).then_inc(s["sums_kept"], 1)

            batches(act, sum_by_source)

            act.wait_ge(s["gw_in"], 16 * 8)
            with act.Fori(0, NC) as i:
                turned(i, 2, "h1_done", i * 4)
                for g in range(4):
                    m, half = g // 2, g % 2
                    act.wait_ge(s["h1_done"], i * 4 + (g + 1 + FREE))
                    apart()
                    act.activation(H1[:, m, ds(i * CW + half * HALF, HALF)], PS[:, 3 + g, 0:HALF], ACT.Identity,
                                   bias=gcol[:, 0, m:m + 1]).then_inc(s["h1_kept"], 1)

            def bn_std(n):
                act.wait_ge(s["bnv_ready"], KD * n)
                act.activation(bsc[:, 0, :], bmv[:, :, 1], ACT.Sqrt, bias=small[:, 2:3]).then_inc(s["bnstd_ready"], 1)

            def bn_relu(i, n, of, ready):
                for m in range(KD):
                    act.wait_ge(s["bn_ready"], n)
                    act.activation(xt[:, m, :], of[:, m, ds(i * CW, CW)], ACT.Relu, bias=bsc[:, 2, m:m + 1],
                                   scale=bsc[:, 1, m:m + 1]).then_inc(s[ready], 1)

            bn_std(1)
            with act.Fori(0, NC) as i:
                act.wait_ge(s["h2_done"], i * 4 + FREE)
                bn_relu(i, 1, H1, "h1n_ready")
                for g in range(4):
                    m, half = g // 2, g % 2
                    act.wait_ge(s["h2_done"], i * 4 + (g + 1 + FREE))
                    apart()
                    act.activation(H2[:, m, ds(i * CW + half * HALF, HALF)], PS[:, 3 + g, 0:HALF], ACT.Identity,
                                   bias=gcol[:, 3, m:m + 1]).then_inc(s["h2_kept"], 1)
            bn_std(2)
            with act.Fori(0, NC) as i:
                act.wait_ge(s["back_done"], i + FREE)
                bn_relu(i, 2, H2, "h2n_ready")
            std()

            act.wait_ge(s["rexp_in"], 1)
            act.activation(rt[:, 1, :], rt[:, 0, :], ACT.Exp, bias=r1[:, 1:2]).then_inc(s["rexp_out"], 1)
            act.wait_ge(s["rexp_in"], 2)
            act.activation(rt[:, 5, :], rt[:, 4, :], ACT.Exp, bias=r1[:, 1:2]).then_inc(s["rexp_out"], 1)
            act.wait_ge(s["rexp_in"], 3)
            act.activation(rt[:, 8, 0:2], rt[:, 7, 0:2], ACT.Exp, bias=r1[:, 1:2]).then_inc(s["rexp_out"], 1)
            ffn(3, 1, ACT.Gelu, (s["expert_w1_in"], 64))
            std()

        @block.tensor
        def _(pe):
            HT = ht[:, :].rearrange("p (m c) -> p m c", m=MH)

            def turn(i, stage):
                pe.wait_ge(s["xc_ready"], i + (NC * stage + 1))
                pe.wait_ge(s["xt_ready"], i + (NC * stage + FREE))
                for k in range(KD):
                    for u in range(TC):
                        c = k * CW + u * P
                        mm = pe.transpose(PSF[:, c:c + P], xc[:, u, k * P:(k + 1) * P], ident[:, :])
                mm.then_inc(s["xt_read"], 1)
                pe.wait_ge(s["xt_ready"], i + (NC * stage + 1 + FREE))

            for q in ("xt_read", "proj_done", "hid_done", "h1_done", "h2_done", "back_done"):
                pe.sem_inc(s[q], FREE)

            pe.wait_ge(s["const_set"], 6)
            pe.wait_ge(s["flag_ready"], 1)
            flag = pe.value_load(unsortedI[0:1, 0:1])
            with pe.If(flag > 0):
                pe.wait_ge(s["bucket_counted"], 1)
                pe.matmul(PS[:, 6, 0:NT], ones[:, :], bk[:, 0, :], start=True, stop=True)
                pe.matmul(PS[:, 5, 0:NT], lower[:, :], bk[:, 0, :], start=True, stop=True).then_inc(s["bucket_summed"], 1)
            pe.wait_ge(s["at_least_ready"], 1)
            for j in range(GR4):
                for g in range(GR4):
                    mm = pe.matmul(PS[:, 7, j:j + 1], at_least[:, g, j * P:(j + 1) * P], ones[:, 0:1],
                                   start=(g == 0), stop=(g == GR4 - 1))
            mm.then_inc(s["rows_counted"], 1)

            pe.wait_ge(s["ident_set"], 1)
            pe.wait_ge(s["wext_ready"], 4)
            with pe.Fori(0, NC) as i:
                turn(i, 0)
                pe.wait_ge(s["proj_kept"], i * TC + FREE)
                for u in range(TC):
                    for k in range(KD):
                        mm = pe.matmul(PS[:, 3 + u, 0:MSG + HEADS], xt[:, k, u * P:(u + 1) * P], wext[:, k, :],
                                       start=(k == 0), stop=(k == KD - 1))
                    mm.then_inc(s["proj_done"], 1)

            pe.wait_ge(s["proj_kept"], NT + FREE)
            pe.wait_ge(s["dloc_ready"], 1)
            for f in range(3):
                for g in range(GR4):
                    mm = pe.transpose(PS[:, f, g * P:(g + 1) * P], got[:, g, :, f], ident[:, :])
                mm.then_inc(s["fields_turned"], 1)
            pe.transpose(PS[0:GR4, 3, 0:P], item_tile[:, :], ident[:, :]).then_inc(s["tileT_done"], 1)

            tile_regs = [pe.alloc_register(f"pe_tile{u}") for u in range(BATCH)]

            def load_tiles(b):
                pe.load(tile_regs, tiles[0:1, items(b)])
                return [pe.snap(r, min_val=0, max_val=NT - 1) for r in tile_regs]

            def spread(b, j):
                h = j % 2
                pe.wait_ge(s["edge_node_ready"], b + 1)
                for u in range(BATCH):
                    mm = pe.transpose(PS[:, h, u * P:(u + 1) * P], edge_node[j][:, u, :], ident[:, :])
                mm.then_inc(s["turned"], 1)
                t = load_tiles(b)
                pe.wait_ge(s["node_edge_kept"], b + 1)
                for u in range(BATCH):
                    mm = pe.matmul(PS[:, 2 + h, u * 2 * HEADS:(u + 1) * 2 * HEADS], node_edge[h][:, u, :],
                                   qn[:, ds(t[u], 1), :], start=True, stop=True)
                mm.then_inc(s["spread"], 1)

            pe.wait_ge(s["fields_kept"], 3)
            pe.wait_ge(s["tiles_in"], 16)
            spread(0, 0)

            def attention(b, j, i):
                spread(b + 1, (j + 1) % RING)
                pe.wait_ge(s["msg_ready"], b + 1)
                for u in range(BATCH):
                    if after(b, 1):
                        pe.wait_ge(s["tile_added"], (b - 1) * BATCH + (u + 1))
                    pe.matmul(PS[:, 4 + u, 0:MSG], edge_node[j][:, u, :], G[j][:, u, :],
                              start=True, stop=True).then_inc(s["tile_summed"], 1)

            batches(pe, attention)

            pe.wait_ge(s["wlog_ready"], 1)
            pe.transpose(PS[0:NT, 7, 0:P], wl[:, :], ident[:, :]).then_inc(s["wlT_done"], 1)

            def ffn(stage, j, loaded):
                for q in loaded:
                    pe.wait_ge(*q)
                groups = 2 * MH
                with pe.Fori(0, NC) as i:
                    turn(i, stage)
                    for g in range(groups):
                        m, half = g // 2, g % 2
                        if g >= 2:
                            pe.wait_ge(s["hid_kept"], i * groups + (j * NC * groups + g - 1))
                        for k in range(KD):
                            mm = pe.matmul(PS[:, 3 + g % 2, 0:HALF], w1s[:, k, m * P:(m + 1) * P],
                                           xt[:, k, half * HALF:(half + 1) * HALF], start=(k == 0), stop=(k == KD - 1))
                        mm.then_inc(s["hid_done"], 1)
                    pe.wait_ge(s["hid_kept"], i * groups + (j * NC * groups + groups))
                    for u in range(TC):
                        pe.wait_ge(s["y_kept"], i * TC + (j * NT + max(0, u - 2) + FREE))
                        for m in range(MH):
                            mm = pe.matmul(PS[:, 5 + u % 3, 0:D], HT[:, m, u * P:(u + 1) * P], w2s[:, m, :],
                                           start=(m == 0), stop=(m == MH - 1))
                        mm.then_inc(s["y_done"], 1)

            pe.wait_ge(s["wlT_ready"], 1)
            ffn(1, 0, ((s["f0w_in"], 48),))

            def row_of(b, h):
                pe.wait_ge(s["key_staged"], b + 1)
                for u in range(BATCH):
                    mm = pe.matmul(PS[:, h, u * P:(u + 1) * P], key[h][:, u:u + 1].to_broadcast([P, P]),
                                   ident[:, :], start=True, stop=True)
                mm.then_inc(s["rowed"], 1)

            row_of(0, 0)

            def sum_by_source(b, j, i):
                h = j % 2
                if after(b, 1):
                    pe.wait_ge(s["weights_ready"], b)
                row_of(b + 1, 1 - h)
                pe.wait_ge(s["weights_ready"], b + 1)
                for u in range(BATCH):
                    mm = pe.matmul(PS[:, 2 + h, u * P:(u + 1) * P], weight_node[h][:, u, :], same[h][:, u, :],
                                   start=True, stop=True)
                mm.then_inc(s["node_src_done"], 1)
                t = load_tiles(b)
                pe.wait_ge(s["node_src_kept"], b + 1)
                for u in range(BATCH):
                    if after(b, 1):
                        pe.wait_ge(s["sums_kept"], (b - 1) * BATCH + (u + 1))
                    pe.matmul(PS[:, 4 + u, 0:D], node_src[h][:, u, :], XN[:, ds(t[u], 1), :],
                              start=True, stop=True).then_inc(s["summed"], 1)

            batches(pe, sum_by_source)

            def layer(i, j, done, kept):
                pe.wait_ge(s[kept], i * 4 + FREE)
                for g in range(4):
                    m, half = g // 2, g % 2
                    for k in range(KD):
                        mm = pe.matmul(PS[:, 3 + g, 0:HALF], gw[:, j, k, m * P:(m + 1) * P],
                                       xt[:, k, half * HALF:(half + 1) * HALF], start=(k == 0), stop=(k == KD - 1))
                    mm.then_inc(s[done], 1)

            pe.wait_ge(s["gw_in"], 16 * 8)
            with pe.Fori(0, NC) as i:
                turn(i, 2)
                layer(i, 0, "h1_done", "h1_kept")
            with pe.Fori(0, NC) as i:
                pe.wait_ge(s["h1n_ready"], i * KD + KD)
                layer(i, 1, "h2_done", "h2_kept")
            with pe.Fori(0, NC) as i:
                pe.wait_ge(s["h2n_ready"], i * KD + KD)
                pe.wait_ge(s["back_added"], i + FREE)
                for u in range(TC):
                    for m in range(KD):
                        c = u * D + m * P
                        mm = pe.transpose(PSF[:, c:c + P], xt[:, m, u * P:(u + 1) * P], ident[:, :])
                mm.then_inc(s["back_done"], 1)

            pe.wait_ge(s["norm_done"], 5 * NT)
            pe.wait_ge(s["const_set"], 6)
            pe.matmul(PS[0:1, 7, 0:D], ones[:, 0:1], XN[:, 0, :], start=True, stop=False)
            with pe.Fori(1, NT - 1) as t:
                pe.matmul(PS[0:1, 7, 0:D], ones[:, 0:1], XN[:, ds(t, 1), :], start=False, stop=False)
            pe.matmul(PS[0:1, 7, 0:D], ones[0:TAIL, 0:1], XN[0:TAIL, NT - 1, :],
                      start=False, stop=True).then_inc(s["mean_done"], 1)
            pe.wait_ge(s["mrow_ready"], 1)
            for k in range(KD):
                mm = pe.matmul(PS[:, 6, k:k + 1], mrow[0:1, k * P:(k + 1) * P], ones[0:1, 0:1], start=True, stop=True)
            mm.then_inc(s["mcol_done"], 1)
            pe.wait_ge(s["mcol_ready"], 1)
            pe.wait_ge(s["r1_in"], 32)
            for k in range(KD):
                mm = pe.matmul(PS[0:1, 7, 0:EXPERTS], mcol[:, k:k + 1], wr1[:, k, :], start=(k == 0), stop=(k == KD - 1))
            mm.then_inc(s["logit_done"], 1)
            pe.wait_ge(s["pairw_ready"], 1)
            pe.matmul(PS[:, 6, 0:2], ones[0:1, :], rt[0:1, 9, 0:2], start=True, stop=True).then_inc(s["wb_done"], 1)
            ffn(3, 1, ((s["expert_w1_in"], 64), (s["w2_scaled"], 2)))

        @block.vector
        def _(v):
            step = Steps(v, s["dve"])
            norms = [0]

            def link(ins):
                step(ins)
                step.wait()

            def norm(of, to):
                n = norms[0]
                with v.Fori(0, NC) as i:
                    for u in range(TC):
                        t = i * TC + u
                        v.bn_stats(st[:, ds(t, 1), :], of(t)).then_inc(s["stat"], 1)
                v.wait_ge(s["stat"], NT * (n + 1))
                step(v.tensor_tensor(mean[:, :], st[:, :, 1], st[:, :, 4], ALU.add))
                step(v.tensor_tensor(t1[:, :], st[:, :, 1], st[:, :, 4], ALU.subtract))
                step(v.tensor_tensor(t2[:, :], st[:, :, 2], st[:, :, 5], ALU.add))
                step.wait()
                step(v.tensor_scalar(mean[:, :], mean[:, :], 0.5, None, ALU.mult))
                link(v.scalar_tensor_tensor(out=t1[:, :], in0=t1[:, :], scalar=0.25, in1=t1[:, :], op0=ALU.mult, op1=ALU.mult))
                v.scalar_tensor_tensor(out=var[:, :], in0=t2[:, :], scalar=1.0 / D, in1=t1[:, :], op0=ALU.mult,
                                       op1=ALU.add).then_inc(s["var_ready"], 1)
                v.wait_ge(s["std_ready"], n + 1)
                link(v.reciprocal(rstd[:, :], rstd[:, :]))
                with v.Fori(0, NC) as i:
                    for u in range(TC):
                        t = i * TC + u
                        v.tensor_scalar(to(t), of(t), mean[:, ds(t, 1)], rstd[:, ds(t, 1)], ALU.subtract,
                                        ALU.mult).then_inc(s["norm_done"], 1)
                norms[0] += 1
                v.wait_ge(s["norm_done"], NT * norms[0])

            def tile(a):
                return lambda t: a[:, ds(t, 1), 0:D]

            def row(j, n=NT):
                return rows[:, j:j + 1, :].to_broadcast([P, n, D])

            def add_tables(a, b):
                for u in range(1, TABLES):
                    v.wait_ge(s["sums1_in"], 16 * (u + 1))
                    v.tensor_tensor(a, a, b, ALU.add).then_inc(s["table_added"], 1)
                v.wait_ge(s["table_added"], TABLES - 1)

            step(v.memset(X[:, NT - 1, :], 0.0))
            v.memset(R2[:, :], 0.0).then_inc(s["zero_set"], 1)
            v.wait_ge(s["watt_in"], 48)
            for k in range(KD):
                for j, a in ((0, ATS), (1, ATD)):
                    link(v.tensor_tensor(ftmp[:, j, :], wext[:, k, 0:D], rows[:, a, :], ALU.mult))
                    v.tensor_reduce(wext[:, k, D + j * HEADS:D + (j + 1) * HEADS],
                                    ftmp[:, j, :].rearrange("p (h f) -> p h f", h=HEADS), AX.X,
                                    ALU.add).then_inc(s["wext_ready"], 1)
            for q in ("proj_kept", "y_kept", "x_added", "back_added"):
                v.sem_inc(s[q], FREE)

            v.wait_ge(s["idx_in"], 16 * 12)
            v.tensor_copy(rec[:, :, :, 1], dstI).then_inc(s["rec_ready"], 1)
            step(v.tensor_copy(dst_next, dst_nextI))
            v.tensor_copy(rec[:, :, :, 0], srcI).then_inc(s["rec_ready"], 1)
            v.tensor_copy(rec[:, :, :, 2], ewI).then_inc(s["rec_ready"], 1)
            step.wait()
            v.wait_ge(s["rec_ready"], 4)
            link(v.tensor_tensor(dst_next, rec[:, :, :, 1], dst_next, ALU.subtract))
            v.tensor_reduce(unsorted[:, 0:1], dst_next.rearrange("p g e -> p (g e)"), AX.X, ALU.max).then_inc(s["order_max"], 1)

            def whole(to, of, scale, bias):
                link(v.tensor_scalar(to, of, scale, bias, ALU.mult, ALU.add))
                link(v.tensor_scalar(to, to, ROUND, None, ALU.add))
                link(v.tensor_scalar(to, to, -ROUND, None, ALU.add))

            v.wait_ge(s["iota_set"], 2)
            whole(f1t[:, :], rec[:, :, 0, 1], 1.0 / P, -0.498)
            step(v.tensor_tensor(f1t[:, :], f1t[:, :], number[:, :], ALU.add))
            link(v.tensor_scalar(f2t[:, :], number[:, :], 1.0, None, ALU.min))
            link(v.tensor_tensor(first[:, :], f1t[:, :], f2t[:, :], ALU.mult))
            v.tensor_tensor(at_least, items_iota.unsqueeze(1).to_broadcast([P, GR4, BUCKETED]),
                            first[:, :].unsqueeze(2).to_broadcast([P, GR4, BUCKETED]), ALU.is_ge).then_inc(s["at_least_ready"], 1)
            v.wait_ge(s["order_known"], 1)
            v.tensor_copy(unsortedI[:, :], unsorted[0:1, 1:2]).then_inc(s["flag_ready"], 1)
            v.wait_ge(s["rows_counted"], 1)
            step(v.tensor_scalar(item_row[:, :], PS[:, 7, 0:GR4], -1.0, None, ALU.add))
            step.wait()
            link(v.tensor_tensor(item_tile[:, :], number[:, :], item_row[:, :], ALU.subtract))
            v.wait_ge(s["flag_ready"], 1)
            flag = v.value_load(unsortedI[0:1, 0:1])
            with v.If(flag > 0):
                sort = Steps(v, s["bucket"])

                def then(ins):
                    sort(ins)
                    sort.wait()

                dsts = rec[:, :, :, 1]
                tiles3 = tile_e.rearrange("p (g e) -> p g e", g=GR4)
                then(v.tensor_scalar(tiles3, dsts, 1.0 / P, -0.498, ALU.mult, ALU.add))
                then(v.tensor_scalar(tile_e, tile_e, ROUND, None, ALU.add))
                then(v.tensor_scalar(tile_e, tile_e, -ROUND, None, ALU.add))
                v.wait_ge(s["const_set"], 6)
                with v.Fori(0, NT) as t:
                    sort.begin(t, 1)
                    then(v.tensor_scalar(in_tile, tile_e, iota[:, ds(t, 1)], None, ALU.is_equal, ALU.add,
                                         accum_out=bk[:, 0, ds(t, 1)]))
                    sort.end(NT)
                v.sem_inc(s["bucket_counted"], 1)
                v.wait_ge(s["bucket_summed"], 1)
                then(v.tensor_copy(bk[:, 1, :], PS[:, 6, 0:NT]))
                then(v.tensor_scalar(bk[:, 2, :], bk[:, 1, :], 1.0 / P, (P - 1.0) / P - 0.498, ALU.mult, ALU.add))
                then(v.tensor_scalar(bk[:, 2, :], bk[:, 2, :], ROUND, None, ALU.add))
                then(v.tensor_scalar(bk[:, 2, :], bk[:, 2, :], -ROUND, None, ALU.add))
                then(v.tensor_tensor_scan(bk[:, 3, :], bk[:, 2, :], bk[:, 2, :], 0.0, ALU.add, ALU.max))
                then(v.tensor_tensor(bk[:, 3, :], bk[:, 3, :], bk[:, 2, :], ALU.subtract))
                then(v.tensor_scalar(bk[:, 4, :], bk[:, 3, :], float(P), BUCKETED * P - 1.0, ALU.mult, ALU.add))
                then(v.tensor_tensor(bk[:, 4, :], bk[:, 4, :], PS[:, 5, 0:NT], ALU.add))
                then(v.memset(place, 0.0))
                with v.Fori(0, NT) as t:
                    sort.begin(t, 4)
                    then(v.tensor_scalar(in_tile, tile_e, iota[:, ds(t, 1)], None, ALU.is_equal))
                    then(v.tensor_tensor_scan(ranks, in_tile, in_tile, 0.0, ALU.add, ALU.max))
                    then(v.scalar_tensor_tensor(out=ranks, in0=ranks, scalar=bk[:, 4, ds(t, 1)], in1=in_tile,
                                                op0=ALU.add, op1=ALU.mult))
                    then(v.tensor_tensor(place, place, ranks, ALU.add))
                    sort.end(NT)
                then(v.tensor_copy(placeI, place))
                v.sem_inc(s["place_ready"], 1)
                then(v.tensor_scalar(item_row[:, :], number[:, :], float(BUCKETED), BUCKETED + ITEMS - 1.0, ALU.add, ALU.min))
                before = at_least.rearrange("p g i -> p (g i)")[:, 0:GR4 * (NT - 1)].rearrange("p (g t) -> p g t", g=GR4)
                then(v.tensor_tensor(before, number[:, :].unsqueeze(2).to_broadcast([P, GR4, NT - 1]),
                                     bk[:, 3:4, 1:NT].to_broadcast([P, GR4, NT - 1]), ALU.is_ge))
                then(v.tensor_reduce(item_tile[:, :], before, AX.X, ALU.add))
            step(v.tensor_scalar(item_node[:, :], item_tile[:, :], float(P), None, ALU.mult))
            v.tensor_copy(item_rowI[:, :], item_row[:, :]).then_inc(s["item_row_ready"], 1)

            v.wait_ge(s["x_in"], 32)
            norm(tile(X), tile(XN))

            with v.Fori(0, NC) as i:
                for u in range(TC):
                    v.wait_ge(s["proj_done"], i * TC + (u + 1 + FREE))
                    v.tensor_scalar(HN[:, ds(i * TC + u, 1), :], PS[:, 3 + u:4 + u, 0:MSG + HEADS], 0.0, None,
                                    ALU.add).then_inc(s["proj_kept"], 1)
            v.wait_ge(s["got_in"], 16 * GR4)
            v.tensor_tensor(got[:, :, :, 1], got[:, :, :, 1], item_node[:, :].unsqueeze(2).to_broadcast([P, GR4, P]),
                            ALU.subtract).then_inc(s["dloc_ready"], 1)
            v.wait_ge(s["proj_kept"], NT + FREE)
            a_src, a_dst = HN[:, :, D:MSG], HN[:, :, MSG:MSG + HEADS]
            v.tensor_reduce(amax[:, :], a_src.rearrange("p t h -> p h t"), AX.X, ALU.max).then_inc(s["amax_ready"], 1)
            step(v.tensor_copy(qn[:, :, 0:HEADS], a_dst))
            link(v.tensor_tensor(zs[:, :, :], a_src, a_dst, ALU.add))
            step(v.scalar_tensor_tensor(out=zs[:, :, :], in0=zs[:, :, :], scalar=SLOPE, in1=zs[:, :, :], op0=ALU.mult, op1=ALU.max))
            v.wait_ge(s["gmax_ready"], 1)
            link(v.tensor_tensor(zb[:, :, :], a_dst, gmax[:, :].unsqueeze(1).to_broadcast([P, NT, HEADS]), ALU.add))
            link(v.scalar_tensor_tensor(out=zb[:, :, :], in0=zb[:, :, :], scalar=SLOPE, in1=zb[:, :, :], op0=ALU.mult, op1=ALU.max))
            v.scalar_tensor_tensor(out=qn[:, :, HEADS:2 * HEADS], in0=zb[:, :, :], scalar=-HEADROOM, in1=zs[:, :, :],
                                   op0=ALU.add, op1=ALU.max).then_inc(s["shift_ready"], 1)
            v.wait_ge(s["shift_ready"], 1)
            v.tensor_tensor(zb[:, :, :], zs[:, :, :], qn[:, :, HEADS:2 * HEADS], ALU.subtract).then_inc(s["shift_ready"], 1)

            v.wait_ge(s["tileT_done"], 1)
            v.tensor_copy(tileT[:, :], PS[0:GR4, 3, 0:P]).then_inc(s["tileT_ready"], 1)

            tile_regs = [v.alloc_register(f"dve_tile{u}") for u in range(BATCH)]

            def match(b, j):
                v.tensor_tensor(edge_node[j], iota[:, :].unsqueeze(1).to_broadcast([P, BATCH, P]),
                                dloc[:, items(b)].unsqueeze(2).to_broadcast([P, BATCH, P]),
                                ALU.is_equal).then_inc(s["edge_node_ready"], 1)

            def add_to_tiles(b):
                v.load(tile_regs, tiles[0:1, items(b)])
                t = [v.snap(r, min_val=0, max_val=NT - 1) for r in tile_regs]
                for u in range(BATCH):
                    v.wait_ge(s["tile_summed"], b * BATCH + (u + 1))
                    if u or after(b, 1):
                        v.wait_ge(s["tile_added"], b * BATCH + u)
                    v.tensor_tensor(A[:, ds(t[u], 1), :], PS[:, 4 + u:5 + u, 0:MSG], A[:, ds(t[u], 1), :],
                                    ALU.add).then_inc(s["tile_added"], 1)

            def attention(b, j, i):
                h = j % 2
                v.wait_ge(gathered[j], i * (16 * BATCH) + 16 * BATCH)
                v.wait_ge(s["spread"], b + 1)
                q = PS[:, 2 + h, 0:BATCH * 2 * HEADS].rearrange("p (u c) -> p u c", u=BATCH)
                link(v.tensor_tensor(ez[h][:, :, :], G[j][:, :, D:MSG], q[:, :, 0:HEADS], ALU.add))
                link(v.scalar_tensor_tensor(out=ez[h][:, :, :], in0=ez[h][:, :, :], scalar=SLOPE,
                                            in1=ez[h][:, :, :], op0=ALU.mult, op1=ALU.max))
                link(v.tensor_tensor(ez[h][:, :, :], ez[h][:, :, :], q[:, :, HEADS:2 * HEADS], ALU.subtract))
                v.tensor_scalar(ez[h][:, :, :], ez[h][:, :, :], CAP, None, ALU.min).then_inc(s["ex_in"], 1)
                match(b + 1, (j + 1) % RING)
                if after(b, 1):
                    add_to_tiles(b - 1)
                v.wait_ge(s["ex_out"], b + 1)
                m = G[j][:, :, 0:D].rearrange("p u (h f) -> p u h f", h=HEADS)
                v.tensor_tensor(m, m, G[j][:, :, D:MSG].unsqueeze(3).to_broadcast([P, BATCH, HEADS, FH]),
                                ALU.mult).then_inc(s["msg_ready"], 1)

            v.wait_ge(s["const_set"], 6)
            v.wait_ge(s["fields_kept"], 3)
            v.wait_ge(s["tiles_in"], 16)
            v.wait_ge(s["zeroed"], 16 * TABLES)
            match(0, 0)
            batches(v, attention, step, 3)
            add_to_tiles(NBATCH - 1)
            v.wait_ge(s["tile_added"], ITEMS)
            heads = lambda a: a[:, :, 0:D].rearrange("p t (h f) -> p t h f", h=HEADS)
            of_head = lambda a: a.unsqueeze(3).to_broadcast([P, NT, HEADS, FH])
            v.wait_ge(s["h_stored"], 16)
            v.wait_ge(s["exs_ready"], 1)
            link(v.tensor_tensor(heads(HN), heads(HN), of_head(exs[:, :, :]), ALU.mult))
            den = A[:, :, D:MSG]
            step(v.tensor_tensor(A[:, :, 0:D], A[:, :, 0:D], HN[:, :, 0:D], ALU.add))
            link(v.scalar_tensor_tensor(out=den, in0=exs[:, :, :], scalar=1e-16, in1=den, op0=ALU.mult, op1=ALU.add))
            link(v.tensor_tensor(den, den, exs[:, :, :], ALU.add))
            link(v.reciprocal(den, den))
            link(v.tensor_tensor(heads(A), heads(A), of_head(den), ALU.mult))
            v.wait_ge(s["vec_in"], 16 * 7)
            link(v.tensor_tensor(A[:, :, 0:D], A[:, :, 0:D], row(BIAS), ALU.add))
            link(v.tensor_tensor(A[:, :, 0:D], A[:, :, 0:D], XN[:, :, :], ALU.add))
            norm(tile(A), tile(A))
            link(v.tensor_tensor(A[:, :, 0:D], A[:, :, 0:D], row(GAM), ALU.mult))
            link(v.tensor_tensor(A[:, :, 0:D], A[:, :, 0:D], row(BET), ALU.add))
            link(v.scalar_tensor_tensor(out=X[:, :, :], in0=A[:, :, 0:D], scalar=0.0, in1=X[:, :, :], op0=ALU.max, op1=ALU.add))

            norm(tile(X), tile(XN))
            link(v.tensor_tensor(Z, XN[:, :, :], row(WRR), ALU.mult))
            link(v.tensor_reduce(wl[:, :], Z, AX.X, ALU.add))
            v.tensor_scalar(wl[:, :], wl[:, :], small[:, 0:1], None, ALU.add).then_inc(s["wlog_ready"], 1)
            v.wait_ge(s["wlT_done"], 1)
            v.tensor_copy(wlT[:, :], PS[0:NT, 7, 0:P]).then_inc(s["wlT_ready"], 1)
            step(v.tensor_tensor(X[:, :, :], X[:, :, :], XN[:, :, :], ALU.add))
            link(v.memset(cnt[:, :, :], 0.0))
            v.wait_ge(s["wrow_in"], 16)
            wrow, scr = R3[:, 0:NPAD], R2[:, 0:NPAD]
            for t in range(NT):
                a, b = t * P, min(N, (t + 1) * P)
                w = wl[:, t:t + 1]
                if t:
                    link(v.tensor_scalar(scr[:, 0:a], wrow[:, 0:a], w, None, ALU.is_ge, ALU.add, accum_out=cnt[:, 0, t:t + 1]))
                link(v.tensor_scalar(scr[:, a:N], wrow[:, a:N], w, None, ALU.is_gt, ALU.add, accum_out=cnt[:, 1, t:t + 1]))
                link(v.scalar_tensor_tensor(out=scr[:, a:b], in0=wrow[:, a:b], scalar=w, in1=lower[:, 0:b - a],
                                            op0=ALU.is_equal, op1=ALU.mult, accum_out=cnt[:, 2, t:t + 1]))
            link(v.tensor_tensor(cnt[:, 0, :], cnt[:, 0, :], cnt[:, 1, :], ALU.add))
            link(v.tensor_tensor(cnt[:, 0, :], cnt[:, 0, :], cnt[:, 2, :], ALU.add))
            link(v.scalar_tensor_tensor(out=wm[:, :], in0=cnt[:, 0, :], scalar=float(KEPT), in1=wl[:, :],
                                        op0=ALU.is_lt, op1=ALU.mult))
            with v.Fori(0, NC) as i:
                for u in range(TC):
                    t = i * TC + u
                    v.wait_ge(s["y_done"], t + 1)
                    v.wait_ge(s["x_added"], t + FREE)
                    v.tensor_tensor(ftmp[:, u % 2, :], PS[:, 5 + u % 3, 0:D], rows[:, B2R, :], ALU.add).then_inc(s["y_kept"], 1)
                    v.wait_ge(s["y_kept"], t + (1 + FREE))
                    v.scalar_tensor_tensor(out=X[:, ds(t, 1), :], in0=ftmp[:, u % 2:u % 2 + 1, :], scalar=wm[:, ds(t, 1)],
                                           in1=X[:, ds(t, 1), :], op0=ALU.mult, op1=ALU.add).then_inc(s["x_added"], 1)
            v.wait_ge(s["x_added"], NT + FREE)

            norm(tile(X), tile(XN))

            def sum_by_source(b, j, i):
                h = j % 2
                v.wait_ge(s["rowed"], b + 1)
                if after(b, 2):
                    v.wait_ge(s["node_src_done"], b - 1)
                step(v.tensor_tensor(same[h], PS[:, h, :].rearrange("p (u e) -> p u e", u=BATCH),
                                     key[h][:, :].unsqueeze(2).to_broadcast([P, BATCH, P]), ALU.is_equal))
                for u in range(BATCH):
                    link(v.scalar_tensor_tensor(out=earlier, in0=PS[:, h, u * P:(u + 1) * P], scalar=key[h][:, u:u + 1],
                                                in1=lower[:, :], op0=ALU.is_equal, op1=ALU.mult, accum_out=es[:, 0, u:u + 1]))
                for u in range(BATCH):
                    c = ds(b * BATCH + u, 1)
                    mm = v.tensor_scalar(weight_node[h][:, u, :], iota[:, :], dloc[:, c], ewT[:, c], ALU.is_equal, ALU.mult)
                mm.then_inc(s["weights_ready"], 1)
                step(v.tensor_scalar(es[:, 1, :], key[h][:, :], -1.0, spare_row[:, 0:1], ALU.mult, ALU.add))
                link(v.tensor_tensor(es[:, 2, :], key[h][:, :], table_of[:, :], ALU.add))
                link(v.scalar_tensor_tensor(out=es[:, 1, :], in0=es[:, 0, :], scalar=1.0, in1=es[:, 1, :], op0=ALU.min, op1=ALU.mult))
                if after(b, 2):
                    for u in range(BATCH):
                        v.wait_ge(added[u], (b - 1) * 16)
                v.tensor_tensor(rowid[h][:, :], es[:, 1, :], es[:, 2, :], ALU.add).then_inc(s["row_ready"], 1)

            batches(v, sum_by_source, step, 8)
            link(v.tensor_scalar(small[:, 3:4], small[:, 1:2], 1.0, None, ALU.add))
            add_tables(Z, R3[:, 0:NT * D].rearrange("p (t c) -> p t c", t=NT))
            v.scalar_tensor_tensor(out=Z, in0=XN[:, :, :], scalar=small[:, 3:4], in1=Z, op0=ALU.mult,
                                   op1=ALU.add).then_inc(s["a_ready"], 1)

            def batch_norm(n, of, g, be):
                for m in range(KD):
                    for j in range(7):
                        step(v.bn_stats(bst[:, m, j, :], of[:, m, j * 512:min(N, (j + 1) * 512)]))
                step.wait()
                for m in range(KD):
                    v.bn_aggr(bmv[:, m, :], bst[:, m, :, :].rearrange("p j c -> p (j c)")).then_inc(s["bnv_ready"], 1)
                v.wait_ge(s["bnstd_ready"], n)
                v.wait_ge(s["bnv_ready"], KD * n)
                link(v.reciprocal(bsc[:, 0, :], bsc[:, 0, :]))
                link(v.tensor_tensor(bsc[:, 1, :], bsc[:, 0, :], gcol[:, g, :], ALU.mult))
                link(v.tensor_tensor(bsc[:, 2, :], bmv[:, :, 0], bsc[:, 1, :], ALU.mult))
                v.tensor_tensor(bsc[:, 2, :], gcol[:, be, :], bsc[:, 2, :], ALU.subtract).then_inc(s["bn_ready"], 1)

            v.wait_ge(s["gw_in"], 16 * 8)
            v.wait_ge(s["h1_kept"], 4 * NC + FREE)
            batch_norm(1, H1, 1, 2)
            v.wait_ge(s["h2_kept"], 4 * NC + FREE)
            batch_norm(2, H2, 4, 5)
            with v.Fori(0, NC) as i:
                xi = X[:, ds(i * TC, TC), :]
                v.wait_ge(s["back_done"], i + (1 + FREE))
                v.tensor_tensor(xi, xi, PSF[:, 0:KD * CW].rearrange("p (t c) -> p t c", t=TC), ALU.add).then_inc(s["back_added"], 1)
            v.wait_ge(s["back_added"], NC + FREE)

            norm(tile(X), tile(XN))
            v.wait_ge(s["mean_done"], 1)
            v.tensor_scalar(mrow[:, :], PS[0:1, 7, 0:D], 1.0 / N, None, ALU.mult).then_inc(s["mrow_ready"], 1)
            v.wait_ge(s["mcol_done"], 1)
            v.tensor_copy(mcol[:, :], PS[:, 6, 0:KD]).then_inc(s["mcol_ready"], 1)
            v.wait_ge(s["logit_done"], 1)
            v.wait_ge(s["r1_in"], 32)
            link(v.tensor_tensor(rt[:, 0, :], PS[0:1, 7, 0:EXPERTS], bre[:, :], ALU.add))

            def softmax(n, of, ex, to, w):
                link(v.tensor_reduce(r1[:, 0:1], rt[:, of, 0:w], AX.X, ALU.max))
                v.tensor_scalar(r1[:, 1:2], r1[:, 0:1], -1.0, None, ALU.mult).then_inc(s["rexp_in"], 1)
                v.wait_ge(s["rexp_out"], n)
                link(v.tensor_reduce(r1[:, 2:3], rt[:, ex, 0:w], AX.X, ALU.add))
                link(v.reciprocal(r1[:, 3:4], r1[:, 2:3]))
                return v.tensor_scalar(rt[:, to, 0:w], rt[:, ex, 0:w], r1[:, 3:4], None, ALU.mult)

            link(softmax(1, 0, 1, 2, EXPERTS))
            link(v.tensor_scalar(rt[:, 3, :], rt[:, 2, :], float(N), 1e-30, ALU.mult, ALU.max))
            link(v.reciprocal(rt[:, 3, :], rt[:, 3, :]))
            link(v.tensor_scalar(rt[:, 3, :], rt[:, 3, :], CAPACITY, 1.0, ALU.mult, ALU.min))
            link(v.tensor_tensor(rt[:, 4, :], rt[:, 2, :], rt[:, 3, :], ALU.mult))
            link(softmax(2, 4, 5, 6, EXPERTS))
            v.max(rt[:, 7, :], rt[:, 6, :]).then_inc(s["pair_ready"], 1)
            v.wait_ge(s["pair_ready"], 1)
            v.max_index(ri[:, :], rt[:, 7, :], rt[:, 6, :]).then_inc(s["pair_ready"], 1)
            softmax(3, 7, 8, 9, 2).then_inc(s["pairw_ready"], 1)
            v.wait_ge(s["wb_done"], 1)
            link(v.tensor_copy(wexp[:, :], PS[:, 6, 0:2]))
            v.wait_ge(s["expert_b2_in"], 64)
            link(v.tensor_scalar(rows[:, B2R, :], rows[:, B2R, :], wexp[:, 0:1], None, ALU.mult))
            link(v.scalar_tensor_tensor(out=rows[:, B2R, :], in0=rows[:, B2B, :], scalar=wexp[:, 1:2], in1=rows[:, B2R, :],
                                        op0=ALU.mult, op1=ALU.add))
            v.wait_ge(s["expert_w2_in"], 32)
            for j in range(2):
                wj = w2s[:, j * MH // 2:(j + 1) * MH // 2, :]
                v.tensor_scalar(wj, wj, wexp[:, j:j + 1], None, ALU.mult).then_inc(s["w2_scaled"], 1)
            link(v.tensor_tensor(Z, XN[:, :, :], row(B2R), ALU.add))
            with v.Fori(0, NC) as i:
                for u in range(TC):
                    t = i * TC + u
                    v.wait_ge(s["y_done"], t + (NT + 1))
                    v.tensor_tensor(Z[:, ds(t, 1), :], PS[:, 5 + u % 3:6 + u % 3, 0:D], Z[:, ds(t, 1), :],
                                    ALU.add).then_inc(s["y_kept"], 1)
            v.wait_ge(s["y_kept"], 2 * NT + FREE)
            norm(tile(Z), tile(Z))
            link(v.tensor_tensor(Z, Z, row(GAM), ALU.mult))
            link(v.tensor_tensor(Z, Z, row(BET), ALU.add))
            v.tensor_tensor(X[:, :, :], Z, X[:, :, :], ALU.add).then_inc(s["out_ready"], 1)


_INS = ["x", "src", "dst", "edge_weight", "L0_gnn_W", "L0_gnn_att_src", "L0_gnn_att_dst", "L0_gnn_bias",
        "L0_gnn_ln_gamma", "L0_gnn_ln_beta", "L0_ffn_wr", "L0_ffn_br", "L0_ffn_w1", "L0_ffn_b1", "L0_ffn_w2",
        "L0_ffn_b2", "L1_gnn_eps", "L1_gnn_W1", "L1_gnn_b1", "L1_gnn_g1", "L1_gnn_be1", "L1_gnn_W2", "L1_gnn_b2",
        "L1_gnn_g2", "L1_gnn_be2", "L1_ffn_Wr", "L1_ffn_br", "L1_ffn_W1", "L1_ffn_b1", "L1_ffn_W2", "L1_ffn_b2",
        "L1_ffn_gamma", "L1_ffn_beta"]


def kernel(**inputs):
    import numpy as _np
    import concourse.bacc as _bacc
    from concourse import mybir as _mybir
    from concourse.bass_utils import run_bass_kernel_spmd as _run

    nc = _bacc.Bacc("TRN2", target_bir_lowering=False, num_devices=1)
    arrays, args = {}, []
    for name in _INS:
        a = _np.ascontiguousarray(inputs[name])
        arrays[f"in_{name}_dram"] = a
        args.append(nc.dram_tensor(f"in_{name}_dram", a.shape, _mybir.dt.from_np(a.dtype), kind="ExternalInput").ap())
    args.append(nc.dram_tensor("out_dram", (N, D), F32, kind="ExternalOutput").ap())
    build(nc, *args)
    r = _run(nc, [arrays], core_ids=[0])
    return r.results[0]["out_dram"]
```

```python
import concourse.bass as bass
from concourse import mybir
from contextlib import ExitStack

F32 = mybir.dt.float32
I32 = mybir.dt.int32
U32 = mybir.dt.uint32
ALU = mybir.AluOpType
ACT = mybir.ActivationFunctionType
AX = mybir.AxisListType
ds = bass.ds

P = 128
N = 3125
D = 256
KD = D // P
E = 50000
NT = -(-N // P)
NPAD = NT * P
TAIL = N - (NT - 1) * P
TC = 5
NC = NT // TC
CW = TC * P
HALF = CW // 2
HEADS = 4
FH = D // HEADS
HID = 1024
MH = HID // P
EXPERTS = 8
FE = 512
SLOPE = 0.2
EPS = 1e-5
KEPT = int(0.5 * N) - 1
CAPACITY = float(-(-N * 5 // (4 * EXPERTS)))
HEADROOM = 60.0

EROWS = -(-E // P)
LAST = E - (EROWS - 1) * P
GROUPS = 4
FIELDS = 4
ACT_TILES = 10
BATCH = 4
RING = 4
BODY = 2 * RING
NBATCH = -(-(EROWS + NT - 1) // (BATCH * BODY)) * BODY
ITEMS = NBATCH * BATCH
ITEMPAD = ITEMS + RING * BATCH
BUCKETED = GROUPS * P
CAP = 64.0
ROUND = 12582912.0
MSG = D + HEADS
ZERO_PARTS = 26
SPARE = NPAD - 1
ROWS = NPAD + P
TABLES = BATCH
assert EROWS + NT - 1 <= ITEMS <= GROUPS * P and ITEMPAD <= GROUPS * P and NBATCH % BODY == 0 and NT == NC * TC
assert HEADROOM < CAP
FREE = 1


class Steps:

    def __init__(self, eng, sem):
        self.eng, self.sem, self.n, self.base = eng, sem, 0, None

    def value(self):
        return self.n if self.base is None else self.base + self.n

    def __call__(self, ins):
        ins.then_inc(self.sem, 1)
        self.n += 1

    def wait(self):
        self.eng.wait_ge(self.sem, self.value())

    def begin(self, i, per):
        self.before, self.per, self.base, self.n = self.n, per, i * per + self.n, 0

    def end(self, trips):
        assert self.n == self.per, (self.n, self.per)
        self.n, self.base = self.before + trips * self.per, None


def build(nc, x, src, dst, edge_weight, g0_W, g0_as, g0_ad, g0_bias, g0_gamma, g0_beta, f0_wr, f0_br,
          f0_w1, f0_b1, f0_w2, f0_b2, g1_eps, g1_W1, g1_b1, g1_g1, g1_be1, g1_W2, g1_b2, g1_g2, g1_be2,
          f1_Wr, f1_br, f1_W1, f1_b1, f1_W2, f1_b2, f1_gamma, f1_beta, out):
    ctx = ExitStack()
    with ctx:
        def sb(name, shape, dt=F32):
            return ctx.enter_context(nc.sbuf_tensor(name, shape, dt))

        def sem(name):
            return ctx.enter_context(nc.semaphore(name))

        htab = nc.dram_tensor("htab", [NPAD, MSG], F32).ap()
        etab = nc.dram_tensor("etab", [BUCKETED + ITEMS, P * FIELDS], F32).ap()
        ttab = nc.dram_tensor("ttab", [GROUPS * P], I32).ap()
        sum1 = nc.dram_tensor("sum1", [TABLES * ROWS, D], F32).ap()
        wtab = nc.dram_tensor("wtab", [NPAD], F32).ap()

        X = sb("X", [P, NT, D])
        XN = sb("XN", [P, NT, D])
        R1 = sb("R1", [P, NT * (MSG + HEADS)])
        R2 = sb("R2", [P, NT * MSG])
        R3 = sb("R3", [P, NT * MSG])
        HN = R1[:, :].rearrange("p (t c) -> p t c", t=NT)
        Y = R1[:, 0:NT * D].rearrange("p (t c) -> p t c", t=NT)
        A = R2[:, :].rearrange("p (t c) -> p t c", t=NT)
        H1 = R1[:, 0:KD * NPAD].rearrange("p (k n) -> p k n", k=KD)
        H2 = R3[:, 0:KD * NPAD].rearrange("p (k n) -> p k n", k=KD)
        Z = R2[:, 0:NT * D].rearrange("p (t c) -> p t c", t=NT)
        xc = sb("xc", [P, TC, D])
        xt = sb("xt", [P, KD, CW])
        ht = sb("ht", [P, MH * CW])
        w1s = sb("w1s", [P, KD, HID])
        w2s = sb("w2s", [P, MH, D])
        b1s = sb("b1s", [P, MH])
        wext = sb("wext", [P, KD, MSG + HEADS])
        gw = sb("gw", [P, 2, KD, D])
        gcol = sb("gcol", [P, 6, KD])
        wr1 = sb("wr1", [P, KD, EXPERTS])
        rows = sb("rows", [P, 8, D])
        ATS, ATD, BIAS, GAM, BET, WRR, B2R, B2B = range(8)
        small = sb("small", [P, 4])
        zero = sb("zero", [P, 1, D])
        ident = sb("ident", [P, P])
        ones = sb("ones", [P, P])
        lower = sb("lower", [P, P])
        spare_row = sb("spare_row", [P, 1])
        table_of = sb("table_of", [P, BATCH])
        st = sb("st", [P, NT, 6])
        mean = sb("mean", [P, NT])
        var = sb("var", [P, NT])
        rstd = sb("rstd", [P, NT])
        t1 = sb("t1", [P, NT])
        t2 = sb("t2", [P, NT])
        zs = sb("zs", [P, NT, HEADS])
        zb = sb("zb", [P, NT, HEADS])
        qn = sb("qn", [P, NT, 2 * HEADS])
        exs = sb("exs", [P, NT, HEADS])
        amax = sb("amax", [P, HEADS])
        gmax = sb("gmax", [P, HEADS])
        wl = sb("wl", [P, NT])
        wm = sb("wm", [P, NT])
        cnt = sb("cnt", [P, 3, NT])
        ftmp = sb("ftmp", [P, 2, D])
        bst = sb("bst", [P, KD, 2 * NC, 6])
        bmv = sb("bmv", [P, KD, 2])
        bsc = sb("bsc", [P, 3, KD])
        rt = sb("rt", [1, 12, EXPERTS])
        ri = sb("ri", [1, EXPERTS], U32)
        r1 = sb("r1", [1, 8])
        mrow = sb("mrow", [1, D])
        mcol = sb("mcol", [P, KD])
        wexp = sb("wexp", [P, 2])
        bre = sb("bre", [1, EXPERTS])

        srcT = sb("srcT", [P, ITEMPAD])
        dloc = sb("dloc", [P, ITEMPAD])
        ewT = sb("ewT", [P, ITEMPAD])
        tiles = sb("tiles", [1, GROUPS * P], I32)
        iota = sb("iota", [P, P])
        number = sb("number", [P, GROUPS])
        first = sb("first", [P, GROUPS])
        f1t, f2t = sb("f1t", [P, GROUPS]), sb("f2t", [P, GROUPS])
        item_row = sb("item_row", [P, GROUPS])
        item_rowI = sb("item_rowI", [P, GROUPS], I32)
        item_tile = sb("item_tile", [P, GROUPS])
        item_node = sb("item_node", [P, GROUPS])
        tileT = sb("tileT", [GROUPS, P], I32)
        unsorted = sb("unsorted", [P, 2])
        unsortedI = sb("unsortedI", [1, 1], I32)
        bk = sb("bk", [P, 5, NT])
        put_at = sb("put_at", [P, 1], I32)
        put_rec = sb("put_rec", [P, FIELDS])

        def taker(of, limit):
            at = [0]

            def part(n):
                at[0] += n
                assert at[0] <= limit
                return of[:, at[0] - n:at[0]]
            return part

        part = taker(R3, NT * MSG)
        rec = part(BUCKETED * FIELDS).rearrange("p (g e f) -> p g e f", g=GROUPS, e=P)
        got = part(BUCKETED * FIELDS).rearrange("p (g e f) -> p g e f", g=GROUPS, e=P)
        dst_next = part(BUCKETED).rearrange("p (g e) -> p g e", g=GROUPS)
        part = taker(ht, MH * CW)
        at_least = part(GROUPS * BUCKETED).rearrange("p (g i) -> p g i", g=GROUPS)
        items_iota = part(BUCKETED)
        tile_e, in_tile, ranks, place = (part(BUCKETED) for _ in range(4))
        part = taker(w1s[:, :, :].rearrange("p k n -> p (k n)"), KD * HID)
        srcI, dstI, dst_nextI = (part(BUCKETED).bitcast(I32).rearrange("p (g e) -> p g e", g=GROUPS) for _ in range(3))
        ewI = part(BUCKETED).rearrange("p (g e) -> p g e", g=GROUPS)
        placeI = srcI.rearrange("p g e -> p (g e)")
        part = taker(ht, MH * CW)
        G = [part(BATCH * MSG).rearrange("p (u c) -> p u c", u=BATCH) for _ in range(RING)]
        part = taker(R3, NT * MSG)
        edge_node = [part(BATCH * P).rearrange("p (u n) -> p u n", u=BATCH) for _ in range(RING)]
        node_edge = [part(BATCH * P).rearrange("p (u e) -> p u e", u=BATCH) for _ in range(2)]
        part = taker(ht, MH * CW)
        weight_node = [part(BATCH * P).rearrange("p (u n) -> p u n", u=BATCH) for _ in range(2)]
        node_src = [part(BATCH * P).rearrange("p (u e) -> p u e", u=BATCH) for _ in range(2)]
        M = [part(BATCH * D).rearrange("p (u c) -> p u c", u=BATCH) for _ in range(2)]
        part_sums = [of[:, 0:(TABLES - 1) * TC * D].rearrange("p (u t c) -> p u t c", u=TABLES - 1, t=TC) for of in (ht, R3)]
        back_in = [xt, ht[:, 0:KD * CW].rearrange("p (k c) -> p k c", k=KD)]
        xcf = xc[:, :, :].rearrange("p t c -> p (t c)")
        same = [xcf[:, j * BATCH * P:(j + 1) * BATCH * P].rearrange("p (u e) -> p u e", u=BATCH) for j in range(2)]
        earlier = part(BATCH * P).rearrange("p (u e) -> p u e", u=BATCH)
        ez = [sb(f"ez{h}", [P, BATCH, HEADS]) for h in range(2)]
        gat = [sb(f"gat{j}", [P, BATCH], I32) for j in range(RING)]
        key = [sb(f"key{j}", [P, BATCH]) for j in range(RING)]
        rowid = [sb(f"rowid{j}", [P, BATCH], I32) for j in range(RING)]
        es = sb("es", [P, 2, 3, BATCH])

        PS = ctx.enter_context(nc.psum_tensor("PS", [P, 8, 512], F32))
        PSF = PS[:, :, :].rearrange("p b c -> p (b c)")
        BACK = 3 * 512

        names = """x_in idx_clear idx_in watt_in vec_in f0w_in gw_in r1_in zero_set zeroed ones_set ident_set
            const_set iota_set dve stat centered var_ready std_ready norm_done norm_shift xc_ready xt_read xt_ready wext_ready
            rec_ready order_max order_known flag_ready at_least_ready rows_counted item_row_ready rec_stored got_in
            dloc_ready fields_turned fields_kept tileT_done tileT_ready tiles_stored tiles_in
            bucket bucket_counted bucket_summed place_ready put_set put_done
            proj_done proj_kept amax_ready gmax_ready shift_ready exs_ready h_stored
            table_added wlog_ready wrow_stored wrow_in node_stat y_biased gnn0_added
            hid_done hid_kept y_done y_kept x_added h1_done h1_kept h2_done h2_kept h1n_ready h2n_ready
            bnv_ready bnstd_ready bn_ready back_done back_added mean_done mrow_ready mcol_done
            mcol_ready logit_done rexp_in rexp_out pair_ready pairw_ready wb_done expert_w1_in
            expert_w2_in expert_b2_in w2_scaled out_ready stored held
            staged edge_node_ready turned node_edge_kept spread ex_in ex_out msg_ready tile_summed tile_added
            key_staged rowed weights_ready node_src_done node_src_kept row_ready summed sums_kept""".split()
        s = {n: sem(n) for n in names}
        gathered = [sem(f"gathered{j}") for j in range(RING)]
        sums_in = [sem(f"sums_in{h}") for h in range(2)]
        added = [sem(f"added{u}") for u in range(TABLES)]
        block = ctx.enter_context(nc.Block())

        def nodes(ap):
            return ap.rearrange("(t p) c -> p t c", p=P)

        def on_all(ap):
            return ap.rearrange("(o c) -> o c", o=1).to_broadcast([P, ap.shape[0]])

        def batches(eng, run, step=None, per=0):
            for j in range(BODY):
                run(j, j % RING, j // RING)
            with eng.Fori(1, NBATCH // BODY) as i:
                if step:
                    step.begin(i - 1, BODY * per)
                for j in range(BODY):
                    run(i * BODY + j, j % RING, i * (BODY // RING) + j // RING)
                if step:
                    step.end(NBATCH // BODY - 1)

        def after(b, n):
            return not isinstance(b, int) or b >= n

        def items(b):
            return ds(b * BATCH, BATCH)

        @block.sync
        def _(sp):
            full, rest = (GROUPS - 1) * P, EROWS - 1 - (GROUPS - 1) * P
            sp.wait_ge(s["idx_clear"], 4)
            for a, t, at in ((dst, dstI, 0), (dst, dst_nextI, 1), (src, srcI, 0), (edge_weight, ewI, 0)):
                sp.dma_start(t[:, 0:GROUPS - 1, :],
                             a[at:at + full * P].rearrange("(g p e) -> p g e", p=P, e=P)).then_inc(s["idx_in"], 16)
                sp.dma_start(t[0:rest, GROUPS - 1, :],
                             a[at + full * P:at + (full + rest) * P].rearrange("(p e) -> p e", e=P)).then_inc(s["idx_in"], 16)
                sp.dma_start(t[rest:rest + 1, GROUPS - 1, 0:LAST - at],
                             a[at + (full + rest) * P:E].rearrange("(p e) -> p e", p=1)).then_inc(s["idx_in"], 16)
            sp.dma_start(wext[:, :, 0:D], g0_W.rearrange("(k p) n -> p k n", p=P)).then_inc(s["watt_in"], 16)
            sp.dma_start(rows[:, ATS, :], on_all(g0_as.rearrange("h f -> (h f)"))).then_inc(s["watt_in"], 16)
            sp.dma_start(rows[:, ATD, :], on_all(g0_ad.rearrange("h f -> (h f)"))).then_inc(s["watt_in"], 16)
            sp.wait_ge(s["dve"], 1)
            sp.dma_start(X[:, 0:NT - 1, :], nodes(x[0:(NT - 1) * P, :])).then_inc(s["x_in"], 16)
            sp.dma_start(X[0:TAIL, NT - 1, :], x[(NT - 1) * P:N, :]).then_inc(s["x_in"], 16)
            sp.wait_ge(s["rec_ready"], 4)
            pads = ITEMS // 4
            for g in range(4):
                at = BUCKETED + g * pads
                sp.dma_start(etab[at:at + pads, :],
                             rec[P - pads:P, GROUPS - 1, :, :].rearrange("p e f -> p (e f)")).then_inc(s["rec_stored"], 16)
            sp.dma_start(etab[0:BUCKETED, :].rearrange("(g p) c -> p g c", p=P),
                         rec.rearrange("p g e f -> p g (e f)")).then_inc(s["rec_stored"], 16)
            for j, v in ((BIAS, g0_bias), (GAM, g0_gamma), (BET, g0_beta), (B2R, f0_b2)):
                sp.dma_start(rows[:, j, :], on_all(v)).then_inc(s["vec_in"], 16)
            sp.dma_start(rows[:, WRR, :], on_all(f0_wr.rearrange("d o -> (d o)"))).then_inc(s["vec_in"], 16)
            sp.dma_start(small[:, 0:1], on_all(f0_br)).then_inc(s["vec_in"], 16)
            sp.dma_start(small[:, 1:2], on_all(g1_eps)).then_inc(s["vec_in"], 16)
            sp.wait_ge(s["got_in"], 16 * GROUPS)
            sp.dma_start(w1s[:, :, :], f0_w1.rearrange("(k p) n -> p k n", p=P)).then_inc(s["f0w_in"], 16)
            sp.dma_start(w2s[:, :, :], f0_w2.rearrange("(k p) n -> p k n", p=P)).then_inc(s["f0w_in"], 16)
            with nc.allow_non_contiguous_dma(reason="short vectors, one feature on a partition"):
                sp.dma_start(b1s[:, :], f0_b1.rearrange("(m p) -> p m", p=P)).then_inc(s["f0w_in"], 16)
                for j, v in enumerate((g1_b1, g1_g1, g1_be1, g1_b2, g1_g2, g1_be2)):
                    sp.dma_start(gcol[:, j, :], v.rearrange("(m p) -> p m", p=P)).then_inc(s["gw_in"], 16)
            for j, w in enumerate((g1_W1, g1_W2)):
                sp.dma_start(gw[:, j, :, :], w.rearrange("(k p) n -> p k n", p=P)).then_inc(s["gw_in"], 16)
            sp.dma_start(wr1[:, :, :], f1_Wr.rearrange("(k p) n -> p k n", p=P)).then_inc(s["r1_in"], 16)
            sp.dma_start(bre[:, :], f1_br.rearrange("(o c) -> o c", o=1)).then_inc(s["r1_in"], 16)

            for c in range(NC):
                sp.wait_ge(s["proj_kept"], (c + 1) * TC + FREE)
                sp.dma_start(nodes(htab[c * CW:(c + 1) * CW, :]),
                             HN[:, c * TC:(c + 1) * TC, 0:MSG]).then_inc(s["h_stored"], 16)
            sp.wait_ge(s["tileT_ready"], 1)
            sp.dma_start(ttab.rearrange("(g p) -> g p", p=P), tileT[:, :]).then_inc(s["tiles_stored"], 16)
            sp.wait_ge(s["tiles_stored"], 16)
            sp.dma_start(tiles[:, :], ttab.rearrange("(o c) -> o c", o=1)).then_inc(s["tiles_in"], 16)
            sp.wait_ge(s["zero_set"], 1)
            v = sum1.rearrange("(p r) c -> p r c", p=P)
            each = TABLES * ROWS // P // ZERO_PARTS
            for part in range(ZERO_PARTS):
                sp.wait_ge(s["tile_summed"], ITEMS * part // ZERO_PARTS + 1)
                sp.dma_start(v[:, part * each:(part + 1) * each, :],
                             zero[:, :, :].to_broadcast([P, each, D])).then_inc(s["zeroed"], 16)

            sp.wait_ge(s["wlog_ready"], 1)
            with nc.allow_non_contiguous_dma(reason="a short vector, one node on a partition"):
                sp.dma_start(wtab.rearrange("(t p) -> p t", p=P), wl[:, :]).then_inc(s["wrow_stored"], 16)
            sp.wait_ge(s["wrow_stored"], 16)
            sp.dma_start(R3[:, 0:NPAD], on_all(wtab)).then_inc(s["wrow_in"], 16)

            for u in range(TABLES):
                sp.wait_ge(added[u], 16 * NBATCH)
            for c in range(NC):
                if c >= 2:
                    sp.wait_ge(s["table_added"], c - 1)
                for u in range(TABLES):
                    dest = Z[:, c * TC:(c + 1) * TC, :] if u == 0 else part_sums[c % 2][:, u - 1, :, :]
                    sp.dma_start(dest, nodes(sum1[u * ROWS + c * CW:u * ROWS + (c + 1) * CW, :])).then_inc(sums_in[c % 2], 16)

            sp.wait_ge(s["norm_done"], 5 * NT)
            sp.dma_start(rows[:, GAM, :], on_all(f1_gamma)).then_inc(s["expert_b2_in"], 16)
            sp.dma_start(rows[:, BET, :], on_all(f1_beta)).then_inc(s["expert_b2_in"], 16)
            sp.wait_ge(s["pair_ready"], 2)
            chosen = [sp.value_load(ri[0:1, j:j + 1], min_val=0, max_val=EXPERTS - 1) for j in range(2)]
            for j, e in enumerate(chosen):
                sp.dma_start(w1s[:, :, j * FE:(j + 1) * FE],
                             f1_W1.rearrange("e (k p) f -> p (e k) f", p=P)[:, ds(e * KD, KD), :]).then_inc(s["expert_w1_in"], 16)
                with nc.allow_non_contiguous_dma(reason="a short vector, one feature on a partition"):
                    sp.dma_start(b1s[:, j * MH // 2:(j + 1) * MH // 2],
                                 f1_b1.rearrange("e (k p) -> p (e k)", p=P)[:, ds(e * (FE // P), FE // P)]).then_inc(s["expert_w1_in"], 16)
            for j, e in enumerate(chosen):
                sp.dma_start(w2s[:, j * MH // 2:(j + 1) * MH // 2, :],
                             f1_W2.rearrange("e (k p) d -> p (e k) d", p=P)[:, ds(e * (FE // P), FE // P), :]).then_inc(s["expert_w2_in"], 16)
                sp.dma_start(rows[:, B2R + j, :], f1_b2[ds(e, 1), :].to_broadcast([P, D])).then_inc(s["expert_b2_in"], 16)
            sp.wait_ge(s["out_ready"], 1)
            early = (NC - 1) * TC
            sp.dma_start(nodes(out[0:early * P, :]), X[:, 0:early, :]).then_inc(s["stored"], 16)
            sp.wait_ge(s["out_ready"], 2)
            sp.dma_start(nodes(out[early * P:(NT - 1) * P, :]), X[:, early:NT - 1, :]).then_inc(s["stored"], 16)
            sp.dma_start(out[(NT - 1) * P:N, :], X[0:TAIL, NT - 1, :]).then_inc(s["stored"], 16)
            sp.wait_ge(s["stored"], 48)

        @block.gpsimd
        def _(pool):
            pool.memset(dstI[:, :, :], SPARE).then_inc(s["idx_clear"], 1)
            pool.memset(dst_nextI[:, :, :], SPARE).then_inc(s["idx_clear"], 1)
            pool.memset(srcI[:, :, :], 0).then_inc(s["idx_clear"], 1)
            pool.memset(ewI[:, :, :], 0.0).then_inc(s["idx_clear"], 1)
            pool.memset(rec[:, :, :, 3], 0.0).then_inc(s["rec_ready"], 1)
            pool.iota(items_iota, pattern=[[1, BUCKETED]], base=0, channel_multiplier=0,
                      allow_small_or_imprecise_dtypes=True).then_inc(s["iota_set"], 1)
            pool.iota(number[:, :], pattern=[[P, GROUPS]], base=0, channel_multiplier=1,
                      allow_small_or_imprecise_dtypes=True).then_inc(s["iota_set"], 1)
            pool.memset(ident[:, :], 1.0).then_inc(s["ones_set"], 1)
            pool.memset(lower[:, :], 1.0).then_inc(s["ones_set"], 1)
            pool.memset(ones[:, :], 1.0).then_inc(s["const_set"], 1)
            pool.wait_ge(s["ones_set"], 2)
            pool.affine_select(out=ident[:, :], in_=ident[:, :], compare_op=ALU.is_equal, fill=0.0, base=0,
                               pattern=[[-1, P]], channel_multiplier=1).then_inc(s["ident_set"], 1)
            pool.affine_select(out=lower[:, :], in_=lower[:, :], compare_op=ALU.is_gt, fill=0.0, base=0,
                               pattern=[[-1, P]], channel_multiplier=1).then_inc(s["const_set"], 1)
            pool.iota(spare_row[:, :], pattern=[[0, 1]], base=NPAD, channel_multiplier=1,
                      allow_small_or_imprecise_dtypes=True).then_inc(s["const_set"], 1)
            pool.iota(table_of[:, :], pattern=[[ROWS, BATCH]], base=0, channel_multiplier=0,
                      allow_small_or_imprecise_dtypes=True).then_inc(s["const_set"], 1)
            pool.memset(small[:, 2:3], EPS).then_inc(s["const_set"], 1)
            pool.iota(iota[:, :], pattern=[[1, P]], base=0, channel_multiplier=0,
                      allow_small_or_imprecise_dtypes=True).then_inc(s["const_set"], 1)
            pool.wait_ge(s["order_max"], 1)
            pool.partition_all_reduce(unsorted[:, 1:2], unsorted[:, 0:1], P, bass.bass_isa.ReduceOp.max).then_inc(s["order_known"], 1)

            def chunks(stage, source, before):
                with pool.Fori(1, NC) as i:
                    pool.wait_ge(s["xt_read"], i + (NC * stage + FREE))
                    pool.wait_ge(s["norm_done"], i * TC + (before + TC))
                    pool.wait_ge(s["ident_set"], 1)
                    pool.tensor_copy(xc[:, :, :], source[:, ds(i * TC, TC), :]).then_inc(s["xc_ready"], 1)

            def hold():
                pool.sem_inc(s["held"], 1)

            pool.wait_ge(s["rec_stored"], 16 * 5)
            pool.wait_ge(s["flag_ready"], 1)
            flag = pool.value_load(unsortedI[0:1, 0:1])
            with pool.If(flag > 0):
                pool.wait_ge(s["place_ready"], 1)
                spots = etab.rearrange("r (e f) -> (r e) f", f=FIELDS)
                recs = rec.rearrange("p g e f -> p (g e) f")
                with pool.Fori(0, BUCKETED) as c:
                    pool.tensor_copy(put_at[:, :], placeI[:, ds(c, 1)]).then_inc(s["put_set"], 1)
                    pool.tensor_copy(put_rec[:, :].unsqueeze(1), recs[:, ds(c, 1), :]).then_inc(s["put_set"], 1)
                    pool.wait_ge(s["put_set"], c * 2 + 2)
                    hold()
                    pool.indirect_dma_start(spots, bass.IndirectOffsetOnAxis(ap=put_at[:, 0:1], axis=0),
                                            put_rec[:, :], None).then_inc(s["put_done"], 16)
                    pool.wait_ge(s["put_done"], c * 16 + 16)
            pool.wait_ge(s["item_row_ready"], 1)
            for g in range(GROUPS):
                pool.indirect_dma_start(got[:, g, :, :].rearrange("p e f -> p (e f)"), None, etab,
                                        bass.IndirectOffsetOnAxis(ap=item_rowI[:, g:g + 1], axis=0)
                                        ).then_inc(s["got_in"], 16)

            chunks(0, XN, 0)
            pool.wait_ge(s["amax_ready"], 1)
            pool.partition_all_reduce(gmax[:, :], amax[:, :], P, bass.bass_isa.ReduceOp.max).then_inc(s["gmax_ready"], 1)

            def gather(b, j, n):
                pool.wait_ge(s["staged"], b + 1)
                if after(b, RING):
                    pool.wait_ge(s["tile_summed"], (b - (RING - 1)) * BATCH)
                hold()
                for u in range(BATCH):
                    pool.indirect_dma_start(G[j][:, u, :], None, htab,
                                            bass.IndirectOffsetOnAxis(ap=gat[j][:, u:u + 1], axis=0)
                                            ).then_inc(gathered[j], 16)

            pool.wait_ge(s["h_stored"], 16 * NC)
            batches(pool, gather)

            chunks(1, XN, 2 * NT)

            def scatter(b, j, n):
                for u in range(BATCH):
                    if after(b, 1):
                        pool.wait_ge(added[u], b * 16)
                    pool.wait_ge(s["sums_kept"], b * BATCH + (u + 1))
                    pool.wait_ge(s["row_ready"], b + 1)
                    hold()
                    pool.indirect_dma_start(sum1, bass.IndirectOffsetOnAxis(ap=rowid[j][:, u:u + 1], axis=0),
                                            M[j % 2][:, u, :], None, compute_op=ALU.add).then_inc(added[u], 16)

            pool.wait_ge(s["zeroed"], 16 * ZERO_PARTS)
            batches(pool, scatter)
            chunks(3, XN, 4 * NT)

        @block.scalar
        def _(act):
            stds = [0]
            HT = ht[:, :].rearrange("p (m c) -> p m c", m=MH)

            def apart():
                act.wait_ge(s["const_set"], 6)

            def std(lo=0, hi=NT):
                stds[0] += 1
                act.preload_act_table(ACT.Sqrt)
                act.wait_ge(s["const_set"], 6)
                act.wait_ge(s["var_ready"], stds[0])
                act.activation(rstd[:, lo:hi], var[:, lo:hi], ACT.Sqrt, bias=small[:, 2:3]).then_inc(s["std_ready"], 1)

            def first_chunk(stage, before):
                act.wait_ge(s["xt_read"], NC * stage + FREE)
                act.wait_ge(s["norm_done"], before + TC)
                act.activation(xc[:, :, :], XN[:, 0:TC, :], ACT.Copy).then_inc(s["xc_ready"], 1)

            def turned(i, stage, used, before):
                act.wait_ge(s["xt_read"], i + (NC * stage + 1 + FREE))
                act.wait_ge(s[used], before + FREE)
                act.activation(xt[:, :, :].rearrange("p k c -> p (k c)"), PSF[:, 0:KD * CW],
                               ACT.Copy).then_inc(s["xt_ready"], 1)

            for q in ("xt_ready", "h1_kept", "h2_kept"):
                act.sem_inc(s[q], FREE)
            std()
            first_chunk(0, 0)
            with act.Fori(0, NC) as i:
                turned(i, 0, "proj_done", i * TC)
            for f, to in enumerate((srcT, dloc, ewT)):
                act.wait_ge(s["fields_turned"], f + 1)
                act.activation(to[:, :], PS[:, f, 0:ITEMPAD], ACT.Copy).then_inc(s["fields_kept"], 1)
            act.preload_act_table(ACT.Exp)
            act.wait_ge(s["shift_ready"], 2)
            act.activation(exs[:, :, :], zb[:, :, :], ACT.Exp).then_inc(s["exs_ready"], 1)

            def stage_gather(b, j):
                act.wait_ge(s["fields_kept"], 3)
                act.activation(gat[j][:, :], srcT[:, items(b)], ACT.Copy).then_inc(s["staged"], 1)

            def keep_spread(b, h):
                act.wait_ge(s["turned"], b + 1)
                act.activation(node_edge[h], PS[:, h, :].rearrange("p (u e) -> p u e", u=BATCH),
                               ACT.Copy).then_inc(s["node_edge_kept"], 1)

            for j in range(RING):
                stage_gather(j, j)
            keep_spread(0, 0)
            keep_spread(1, 1)

            def attention(b, j, n):
                act.wait_ge(s["ex_in"], b + 1)
                act.activation(G[j][:, :, D:MSG], ez[j % 2][:, :, :], ACT.Exp).then_inc(s["ex_out"], 1)
                stage_gather(b + RING, j)
                keep_spread(b + 2, j % 2)

            batches(act, attention)
            std()
            std()
            first_chunk(1, 2 * NT)

            def ffn(stage, j, func, loaded, middle=None):
                act.preload_act_table(func)
                act.wait_ge(*loaded)
                groups = 2 * MH

                def chunk(i, middle=None):
                    turned(i, stage, "hid_done", i * groups + j * NC * groups)
                    for g in range(groups):
                        if g == groups // 2 and middle:
                            middle()
                        m, half = g // 2, g % 2
                        act.wait_ge(s["hid_done"], i * groups + (j * NC * groups + g + 1 + FREE))
                        act.activation(HT[:, m, half * HALF:(half + 1) * HALF], PS[:, 3 + g % 2, 0:HALF], func,
                                       bias=b1s[:, m:m + 1]).then_inc(s["hid_kept"], 1)
                    if j == 0:
                        for u in range(TC):
                            act.wait_ge(s["y_done"], i * TC + (u + 1))
                            apart()
                            act.activation(Y[:, ds(i * TC + u, 1), :], PS[:, 5 + u % 3:6 + u % 3, 0:D],
                                           ACT.Copy).then_inc(s["y_kept"], 1)

                with act.Fori(0, NC - 1) as i:
                    chunk(i)
                chunk(NC - 1, middle)

            ffn(1, 0, ACT.Gelu_apprx_tanh, (s["f0w_in"], 48))
            std()

            act.wait_ge(s["norm_shift"], 1)
            for t in range(NT - ACT_TILES, NT):
                act.activation(XN[:, t, :], X[:, t, :], ACT.Identity, bias=t1[:, t:t + 1],
                               scale=rstd[:, t:t + 1]).then_inc(s["norm_done"], 1)

            def stage_key(b, j):
                act.wait_ge(s["fields_kept"], 3)
                act.activation(key[j][:, :], srcT[:, items(b)], ACT.Copy).then_inc(s["key_staged"], 1)

            stage_key(0, 0)
            stage_key(1, 1)

            def sum_by_source(b, j, n):
                h = j % 2
                if after(b, 2):
                    act.wait_ge(s["row_ready"], b - 1)
                stage_key(b + 2, (j + 2) % RING)
                act.wait_ge(s["node_src_done"], b + 1)
                act.activation(node_src[h], PS[:, 2 + h, :].rearrange("p (u e) -> p u e", u=BATCH),
                               ACT.Copy).then_inc(s["node_src_kept"], 1)
                for u in range(BATCH):
                    if after(b, 2):
                        act.wait_ge(added[u], (b - 1) * 16)
                    act.wait_ge(s["summed"], b * BATCH + (u + 1))
                    act.activation(M[h][:, u, :], PS[:, 4 + u, 0:D], ACT.Copy).then_inc(s["sums_kept"], 1)

            batches(act, sum_by_source)

            act.wait_ge(s["gw_in"], 16 * 8)
            with act.Fori(0, NC) as i:
                turned(i, 2, "h1_done", i * 4)
                for g in range(4):
                    m, half = g // 2, g % 2
                    act.wait_ge(s["h1_done"], i * 4 + (g + 1 + FREE))
                    apart()
                    act.activation(H1[:, m, ds(i * CW + half * HALF, HALF)], PS[:, 3 + g, 0:HALF], ACT.Identity,
                                   bias=gcol[:, 0, m:m + 1]).then_inc(s["h1_kept"], 1)

            def bn_std(n):
                act.wait_ge(s["bnv_ready"], KD * n)
                act.activation(bsc[:, 0, :], bmv[:, :, 1], ACT.Sqrt, bias=small[:, 2:3]).then_inc(s["bnstd_ready"], 1)

            def bn_relu(c, n, of, to, ready):
                for m in range(KD):
                    act.wait_ge(s["bn_ready"], n)
                    act.activation(to(m), of[:, m, ds(c * CW, CW)], ACT.Relu, bias=bsc[:, 2, m:m + 1],
                                   scale=bsc[:, 1, m:m + 1]).then_inc(s[ready], 1)

            def h1_relu(c):
                bn_relu(c, 1, H1, lambda m: H1[:, m, ds(c * CW, CW)], "h1n_ready")

            def keep_h2(i):
                for g in range(4):
                    m, half = g // 2, g % 2
                    act.wait_ge(s["h2_done"], i * 4 + (g + 1 + FREE))
                    apart()
                    act.activation(H2[:, m, ds(i * CW + half * HALF, HALF)], PS[:, 3 + g, 0:HALF], ACT.Identity,
                                   bias=gcol[:, 3, m:m + 1]).then_inc(s["h2_kept"], 1)

            bn_std(1)
            h1_relu(0)
            with act.Fori(0, NC - 1) as i:
                h1_relu(i + 1)
                keep_h2(i)
            keep_h2(NC - 1)
            bn_std(2)
            for c in range(NC):
                if c >= 2:
                    act.wait_ge(s["back_done"], c - 1 + FREE)
                bn_relu(c, 2, H2, lambda m: back_in[c % 2][:, m, :], "h2n_ready")
            std()
            first_chunk(3, 4 * NT)

            act.wait_ge(s["rexp_in"], 1)
            act.activation(rt[:, 1, :], rt[:, 0, :], ACT.Exp, bias=r1[:, 1:2]).then_inc(s["rexp_out"], 1)
            act.wait_ge(s["rexp_in"], 2)
            act.activation(rt[:, 5, :], rt[:, 4, :], ACT.Exp, bias=r1[:, 1:2]).then_inc(s["rexp_out"], 1)
            act.wait_ge(s["rexp_in"], 3)
            act.activation(rt[:, 8, 0:2], rt[:, 7, 0:2], ACT.Exp, bias=r1[:, 1:2]).then_inc(s["rexp_out"], 1)
            ffn(3, 1, ACT.Gelu, (s["expert_w1_in"], 64), middle=lambda: std(0, (NC - 1) * TC))
            std((NC - 1) * TC, NT)

        @block.tensor
        def _(pe):
            HT = ht[:, :].rearrange("p (m c) -> p m c", m=MH)

            def turn(i, stage):
                pe.wait_ge(s["xc_ready"], i + (NC * stage + 1))
                pe.wait_ge(s["xt_ready"], i + (NC * stage + FREE))
                for k in range(KD):
                    for u in range(TC):
                        c = k * CW + u * P
                        mm = pe.transpose(PSF[:, c:c + P], xc[:, u, k * P:(k + 1) * P], ident[:, :])
                mm.then_inc(s["xt_read"], 1)
                pe.wait_ge(s["xt_ready"], i + (NC * stage + 1 + FREE))

            for q in ("xt_read", "proj_done", "hid_done", "h1_done", "h2_done", "back_done"):
                pe.sem_inc(s[q], FREE)

            pe.wait_ge(s["const_set"], 6)
            pe.wait_ge(s["at_least_ready"], 1)
            for j in range(GROUPS):
                for g in range(GROUPS):
                    mm = pe.matmul(PS[:, 7, j:j + 1], at_least[:, g, j * P:(j + 1) * P], ones[:, 0:1],
                                   start=(g == 0), stop=(g == GROUPS - 1))
            mm.then_inc(s["rows_counted"], 1)
            pe.wait_ge(s["flag_ready"], 1)
            flag = pe.value_load(unsortedI[0:1, 0:1])
            with pe.If(flag > 0):
                pe.wait_ge(s["bucket_counted"], 1)
                pe.matmul(PS[:, 6, 0:NT], ones[:, :], bk[:, 0, :], start=True, stop=True)
                pe.matmul(PS[:, 5, 0:NT], lower[:, :], bk[:, 0, :], start=True, stop=True).then_inc(s["bucket_summed"], 1)

            pe.wait_ge(s["ident_set"], 1)
            pe.wait_ge(s["wext_ready"], 4)
            with pe.Fori(0, NC) as i:
                turn(i, 0)
                pe.wait_ge(s["proj_kept"], i * TC + FREE)
                for u in range(TC):
                    for k in range(KD):
                        mm = pe.matmul(PS[:, 3 + u, 0:MSG + HEADS], xt[:, k, u * P:(u + 1) * P], wext[:, k, :],
                                       start=(k == 0), stop=(k == KD - 1))
                    mm.then_inc(s["proj_done"], 1)

            pe.wait_ge(s["proj_kept"], NT + FREE)
            pe.wait_ge(s["dloc_ready"], 1)
            for f in range(3):
                for g in range(GROUPS):
                    mm = pe.transpose(PS[:, f, g * P:(g + 1) * P], got[:, g, :, f], ident[:, :])
                mm.then_inc(s["fields_turned"], 1)
            pe.transpose(PS[0:GROUPS, 3, 0:P], item_tile[:, :], ident[:, :]).then_inc(s["tileT_done"], 1)

            tile_regs = [pe.alloc_register(f"pe_tile{u}") for u in range(BATCH)]

            def load_tiles(b):
                pe.load(tile_regs, tiles[0:1, items(b)])
                return [pe.snap(r, min_val=0, max_val=NT - 1) for r in tile_regs]

            def turn_match(b, j):
                pe.wait_ge(s["edge_node_ready"], (b + 1) * BATCH)
                for u in range(BATCH):
                    mm = pe.transpose(PS[:, j % 2, u * P:(u + 1) * P], edge_node[j][:, u, :], ident[:, :])
                mm.then_inc(s["turned"], 1)

            def spread(b, j):
                h = j % 2
                t = load_tiles(b)
                pe.wait_ge(s["node_edge_kept"], b + 1)
                for u in range(BATCH):
                    mm = pe.matmul(PS[:, 2 + h, u * 2 * HEADS:(u + 1) * 2 * HEADS], node_edge[h][:, u, :],
                                   qn[:, ds(t[u], 1), :], start=True, stop=True)
                mm.then_inc(s["spread"], 1)

            pe.wait_ge(s["fields_kept"], 3)
            pe.wait_ge(s["tiles_in"], 16)
            turn_match(0, 0)
            turn_match(1, 1)
            spread(0, 0)

            def attention(b, j, n):
                spread(b + 1, (j + 1) % RING)
                turn_match(b + 2, (j + 2) % RING)
                for u in range(BATCH):
                    if u % 2 == 0:
                        pe.wait_ge(s["msg_ready"], b * 2 + (u // 2 + 1))
                    if after(b, 1):
                        pe.wait_ge(s["tile_added"], (b - 1) * BATCH + (u + 1))
                    pe.matmul(PS[:, 4 + u, 0:MSG], edge_node[j][:, u, :], G[j][:, u, :],
                              start=True, stop=True).then_inc(s["tile_summed"], 1)

            batches(pe, attention)

            def ffn(stage, j, loaded, second=None):
                for q in loaded:
                    pe.wait_ge(*q)
                groups = 2 * MH
                with pe.Fori(0, NC) as i:
                    turn(i, stage)
                    for g in range(groups):
                        m, half = g // 2, g % 2
                        if g >= 2:
                            pe.wait_ge(s["hid_kept"], i * groups + (j * NC * groups + g - 1))
                        for k in range(KD):
                            mm = pe.matmul(PS[:, 3 + g % 2, 0:HALF], w1s[:, k, m * P:(m + 1) * P],
                                           xt[:, k, half * HALF:(half + 1) * HALF], start=(k == 0), stop=(k == KD - 1))
                        mm.then_inc(s["hid_done"], 1)
                    pe.wait_ge(s["hid_kept"], i * groups + (j * NC * groups + groups))
                    if second:
                        pe.wait_ge(*second)
                    for u in range(TC):
                        pe.wait_ge(s["y_kept"], i * TC + (j * NT + max(0, u - 2) + FREE))
                        for m in range(MH):
                            mm = pe.matmul(PS[:, 5 + u % 3, 0:D], HT[:, m, u * P:(u + 1) * P], w2s[:, m, :],
                                           start=(m == 0), stop=(m == MH - 1))
                        mm.then_inc(s["y_done"], 1)

            ffn(1, 0, ((s["f0w_in"], 48),))

            def row_of(b, j):
                pe.wait_ge(s["key_staged"], b + 1)
                for u in range(BATCH):
                    mm = pe.matmul(PS[:, j % 2, u * P:(u + 1) * P], key[j][:, u:u + 1].to_broadcast([P, P]),
                                   ident[:, :], start=True, stop=True)
                mm.then_inc(s["rowed"], 1)

            row_of(0, 0)

            def sum_by_source(b, j, n):
                h = j % 2
                if after(b, 1):
                    pe.wait_ge(s["weights_ready"], b)
                row_of(b + 1, (j + 1) % RING)
                pe.wait_ge(s["weights_ready"], b + 1)
                for u in range(BATCH):
                    mm = pe.matmul(PS[:, 2 + h, u * P:(u + 1) * P], weight_node[h][:, u, :], same[h][:, u, :],
                                   start=True, stop=True)
                mm.then_inc(s["node_src_done"], 1)
                t = load_tiles(b)
                pe.wait_ge(s["node_src_kept"], b + 1)
                for u in range(BATCH):
                    if after(b, 1):
                        pe.wait_ge(s["sums_kept"], (b - 1) * BATCH + (u + 1))
                    pe.matmul(PS[:, 4 + u, 0:D], node_src[h][:, u, :], XN[:, ds(t[u], 1), :],
                              start=True, stop=True).then_inc(s["summed"], 1)

            batches(pe, sum_by_source)

            def layer(i, j, done, kept, of):
                pe.wait_ge(s[kept], i * 4 + FREE)
                for g in range(4):
                    m, half = g // 2, g % 2
                    for k in range(KD):
                        mm = pe.matmul(PS[:, 3 + g, 0:HALF], gw[:, j, k, m * P:(m + 1) * P],
                                       of(k, half), start=(k == 0), stop=(k == KD - 1))
                    mm.then_inc(s[done], 1)

            pe.wait_ge(s["gw_in"], 16 * 8)
            with pe.Fori(0, NC) as i:
                turn(i, 2)
                layer(i, 0, "h1_done", "h1_kept", lambda k, half: xt[:, k, half * HALF:(half + 1) * HALF])
            with pe.Fori(0, NC) as i:
                pe.wait_ge(s["h1n_ready"], i * KD + KD)
                layer(i, 1, "h2_done", "h2_kept", lambda k, half: H1[:, k, ds(i * CW + half * HALF, HALF)])
            for c in range(NC):
                pe.wait_ge(s["h2n_ready"], c * KD + KD)
                if c >= 2:
                    pe.wait_ge(s["back_added"], c - 1 + FREE)
                for u in range(TC):
                    for m in range(KD):
                        at = c % 2 * BACK + u * D + m * P
                        mm = pe.transpose(PSF[:, at:at + P], back_in[c % 2][:, m, u * P:(u + 1) * P], ident[:, :])
                mm.then_inc(s["back_done"], 1)

            pe.wait_ge(s["const_set"], 6)
            pe.wait_ge(s["norm_done"], 4 * NT + 1)
            pe.matmul(PS[0:1, 7, 0:D], ones[:, 0:1], XN[:, 0, :], start=True, stop=False)
            with pe.Fori(1, NT - 1) as t:
                pe.wait_ge(s["norm_done"], t + (4 * NT + 1))
                pe.matmul(PS[0:1, 7, 0:D], ones[:, 0:1], XN[:, ds(t, 1), :], start=False, stop=False)
            pe.wait_ge(s["norm_done"], 5 * NT)
            pe.matmul(PS[0:1, 7, 0:D], ones[0:TAIL, 0:1], XN[0:TAIL, NT - 1, :],
                      start=False, stop=True).then_inc(s["mean_done"], 1)
            pe.wait_ge(s["mrow_ready"], 1)
            for k in range(KD):
                mm = pe.matmul(PS[:, 6, k:k + 1], mrow[0:1, k * P:(k + 1) * P], ones[0:1, 0:1], start=True, stop=True)
            mm.then_inc(s["mcol_done"], 1)
            pe.wait_ge(s["mcol_ready"], 1)
            pe.wait_ge(s["r1_in"], 32)
            for k in range(KD):
                mm = pe.matmul(PS[0:1, 7, 0:EXPERTS], mcol[:, k:k + 1], wr1[:, k, :], start=(k == 0), stop=(k == KD - 1))
            mm.then_inc(s["logit_done"], 1)
            pe.wait_ge(s["pairw_ready"], 1)
            pe.matmul(PS[:, 6, 0:2], ones[0:1, :], rt[0:1, 9, 0:2], start=True, stop=True).then_inc(s["wb_done"], 1)
            ffn(3, 1, ((s["expert_w1_in"], 64),), (s["w2_scaled"], 2))

        @block.vector
        def _(v):
            step = Steps(v, s["dve"])
            norms, stat_count, norm_tiles, centered = [0], [0], [0], [0]

            def link(ins):
                step(ins)
                step.wait()

            def each_tile(run, lo=0, hi=NT):
                with v.Fori(lo // TC, hi // TC) as i:
                    for u in range(TC):
                        run(i * TC + u)

            def stats(of, t):
                v.bn_stats(st[:, ds(t, 1), :], of(t)).then_inc(s["stat"], 1)

            def scales(lo=0, hi=NT):
                stat_count[0] += hi - lo
                norms[0] += 1
                a = lambda x: x[:, lo:hi]
                v.wait_ge(s["stat"], stat_count[0])
                step(v.tensor_tensor(a(mean), st[:, lo:hi, 1], st[:, lo:hi, 4], ALU.add))
                step(v.tensor_tensor(a(t1), st[:, lo:hi, 1], st[:, lo:hi, 4], ALU.subtract))
                step(v.tensor_tensor(a(t2), st[:, lo:hi, 2], st[:, lo:hi, 5], ALU.add))
                step.wait()
                step(v.tensor_scalar(a(mean), a(mean), 0.5, None, ALU.mult))
                link(v.scalar_tensor_tensor(out=a(t1), in0=a(t1), scalar=0.25, in1=a(t1), op0=ALU.mult, op1=ALU.mult))
                v.scalar_tensor_tensor(out=a(var), in0=a(t2), scalar=1.0 / D, in1=a(t1), op0=ALU.mult,
                                       op1=ALU.add).then_inc(s["var_ready"], 1)
                v.wait_ge(s["std_ready"], norms[0])
                link(v.reciprocal(a(rstd), a(rstd)))

            def apply(of, to):
                each_tile(lambda t: v.tensor_scalar(to(t), of(t), mean[:, ds(t, 1)], rstd[:, ds(t, 1)], ALU.subtract,
                                                    ALU.mult).then_inc(s["norm_done"], 1))
                norm_tiles[0] += NT
                v.wait_ge(s["norm_done"], norm_tiles[0])

            def norm(of, to):
                each_tile(lambda t: stats(of, t))
                scales()
                apply(of, to)

            def apply_affine(i, a):
                for u in range(TC):
                    t = i * TC + u
                    v.scalar_tensor_tensor(out=a(t), in0=a(t), scalar=mean[:, ds(t, 1)], in1=rows[:, GAM:GAM + 1, :],
                                           op0=ALU.subtract, op1=ALU.mult).then_inc(s["centered"], 1)
                for u in range(TC):
                    t = i * TC + u
                    v.wait_ge(s["centered"], t + (centered[0] + 1))
                    v.scalar_tensor_tensor(out=a(t), in0=a(t), scalar=rstd[:, ds(t, 1)], in1=rows[:, BET:BET + 1, :],
                                           op0=ALU.mult, op1=ALU.add).then_inc(s["norm_done"], 1)
                v.wait_ge(s["norm_done"], i * TC + (norm_tiles[0] + TC))

            def tile(a):
                return lambda t: a[:, ds(t, 1), 0:D]

            def row(j, n=NT):
                return rows[:, j:j + 1, :].to_broadcast([P, n, D])

            step(v.memset(X[:, NT - 1, :], 0.0))
            v.memset(zero[:, :, :], 0.0).then_inc(s["zero_set"], 1)
            for q in ("proj_kept", "y_kept", "back_added"):
                v.sem_inc(s[q], FREE)

            v.wait_ge(s["idx_in"], 16 * 12)
            v.tensor_copy(rec[:, :, :, 1], dstI).then_inc(s["rec_ready"], 1)
            step(v.tensor_copy(dst_next, dst_nextI))
            v.tensor_copy(rec[:, :, :, 0], srcI).then_inc(s["rec_ready"], 1)
            v.tensor_copy(rec[:, :, :, 2], ewI).then_inc(s["rec_ready"], 1)
            step.wait()
            v.wait_ge(s["rec_ready"], 4)
            link(v.tensor_tensor(dst_next, rec[:, :, :, 1], dst_next, ALU.subtract))
            v.tensor_reduce(unsorted[:, 0:1], dst_next.rearrange("p g e -> p (g e)"), AX.X, ALU.max).then_inc(s["order_max"], 1)

            def whole(to, of, scale, bias):
                link(v.tensor_scalar(to, of, scale, bias, ALU.mult, ALU.add))
                link(v.tensor_scalar(to, to, ROUND, None, ALU.add))
                link(v.tensor_scalar(to, to, -ROUND, None, ALU.add))

            v.wait_ge(s["iota_set"], 2)
            whole(f1t[:, :], rec[:, :, 0, 1], 1.0 / P, -0.498)
            step(v.tensor_tensor(f1t[:, :], f1t[:, :], number[:, :], ALU.add))
            link(v.tensor_scalar(f2t[:, :], number[:, :], 1.0, None, ALU.min))
            link(v.tensor_tensor(first[:, :], f1t[:, :], f2t[:, :], ALU.mult))
            v.tensor_tensor(at_least, items_iota.unsqueeze(1).to_broadcast([P, GROUPS, BUCKETED]),
                            first[:, :].unsqueeze(2).to_broadcast([P, GROUPS, BUCKETED]), ALU.is_ge).then_inc(s["at_least_ready"], 1)
            v.wait_ge(s["watt_in"], 48)
            for k in range(KD):
                for j, a in ((0, ATS), (1, ATD)):
                    link(v.tensor_tensor(ftmp[:, j, :], wext[:, k, 0:D], rows[:, a, :], ALU.mult))
                    v.tensor_reduce(wext[:, k, D + j * HEADS:D + (j + 1) * HEADS],
                                    ftmp[:, j, :].rearrange("p (h f) -> p h f", h=HEADS), AX.X,
                                    ALU.add).then_inc(s["wext_ready"], 1)
            v.wait_ge(s["x_in"], 32)
            each_tile(lambda t: stats(tile(X), t))
            v.wait_ge(s["order_known"], 1)
            v.tensor_copy(unsortedI[:, :], unsorted[0:1, 1:2]).then_inc(s["flag_ready"], 1)
            v.wait_ge(s["rows_counted"], 1)
            step(v.tensor_scalar(item_row[:, :], PS[:, 7, 0:GROUPS], -1.0, None, ALU.add))
            step.wait()
            link(v.tensor_tensor(item_tile[:, :], number[:, :], item_row[:, :], ALU.subtract))
            v.wait_ge(s["flag_ready"], 1)
            flag = v.value_load(unsortedI[0:1, 0:1])
            with v.If(flag > 0):
                sort = Steps(v, s["bucket"])

                def then(ins):
                    sort(ins)
                    sort.wait()

                dsts = rec[:, :, :, 1]
                tiles3 = tile_e.rearrange("p (g e) -> p g e", g=GROUPS)
                then(v.tensor_scalar(tiles3, dsts, 1.0 / P, -0.498, ALU.mult, ALU.add))
                then(v.tensor_scalar(tile_e, tile_e, ROUND, None, ALU.add))
                then(v.tensor_scalar(tile_e, tile_e, -ROUND, None, ALU.add))
                then(v.scalar_tensor_tensor(out=tiles3, in0=dsts, scalar=float(N), in1=tiles3, op0=ALU.is_ge, op1=ALU.add))
                v.wait_ge(s["const_set"], 6)
                with v.Fori(0, NT) as t:
                    sort.begin(t, 1)
                    then(v.tensor_scalar(in_tile, tile_e, iota[:, ds(t, 1)], None, ALU.is_equal, ALU.add,
                                         accum_out=bk[:, 0, ds(t, 1)]))
                    sort.end(NT)
                v.sem_inc(s["bucket_counted"], 1)
                v.wait_ge(s["bucket_summed"], 1)
                then(v.tensor_copy(bk[:, 1, :], PS[:, 6, 0:NT]))
                then(v.tensor_scalar(bk[:, 2, :], bk[:, 1, :], 1.0 / P, (P - 1.0) / P - 0.498, ALU.mult, ALU.add))
                then(v.tensor_scalar(bk[:, 2, :], bk[:, 2, :], ROUND, None, ALU.add))
                then(v.tensor_scalar(bk[:, 2, :], bk[:, 2, :], -ROUND, None, ALU.add))
                then(v.tensor_tensor_scan(bk[:, 3, :], bk[:, 2, :], bk[:, 2, :], 0.0, ALU.add, ALU.max))
                then(v.tensor_tensor(bk[:, 3, :], bk[:, 3, :], bk[:, 2, :], ALU.subtract))
                then(v.tensor_scalar(bk[:, 4, :], bk[:, 3, :], float(P), BUCKETED * P - 1.0, ALU.mult, ALU.add))
                then(v.tensor_tensor(bk[:, 4, :], bk[:, 4, :], PS[:, 5, 0:NT], ALU.add))
                then(v.memset(place, 0.0))
                with v.Fori(0, NT) as t:
                    sort.begin(t, 4)
                    then(v.tensor_scalar(in_tile, tile_e, iota[:, ds(t, 1)], None, ALU.is_equal))
                    then(v.tensor_tensor_scan(ranks, in_tile, in_tile, 0.0, ALU.add, ALU.max))
                    then(v.scalar_tensor_tensor(out=ranks, in0=ranks, scalar=bk[:, 4, ds(t, 1)], in1=in_tile,
                                                op0=ALU.add, op1=ALU.mult))
                    then(v.tensor_tensor(place, place, ranks, ALU.add))
                    sort.end(NT)
                then(v.tensor_copy(placeI, place))
                v.sem_inc(s["place_ready"], 1)
                then(v.tensor_scalar(item_row[:, :], number[:, :], float(BUCKETED), BUCKETED + ITEMS - 1.0, ALU.add, ALU.min))
                before = at_least.rearrange("p g i -> p (g i)")[:, 0:GROUPS * (NT - 1)].rearrange("p (g t) -> p g t", g=GROUPS)
                then(v.tensor_tensor(before, number[:, :].unsqueeze(2).to_broadcast([P, GROUPS, NT - 1]),
                                     bk[:, 3:4, 1:NT].to_broadcast([P, GROUPS, NT - 1]), ALU.is_ge))
                then(v.tensor_reduce(item_tile[:, :], before, AX.X, ALU.add))
            step(v.tensor_scalar(item_node[:, :], item_tile[:, :], float(P), None, ALU.mult))
            v.tensor_copy(item_rowI[:, :], item_row[:, :]).then_inc(s["item_row_ready"], 1)

            scales()
            apply(tile(X), tile(XN))

            v.wait_ge(s["vec_in"], 16 * 7)
            with v.Fori(0, NC) as i:
                step.begin(i, 1)
                xi = XN[:, ds(i * TC, TC), :]
                v.wait_ge(s["xc_ready"], i + 1)
                step(v.tensor_tensor(xi, xi, row(BIAS, TC), ALU.add))
                step.end(NC)
                for u in range(TC):
                    v.wait_ge(s["proj_done"], i * TC + (u + 1 + FREE))
                    v.tensor_scalar(HN[:, ds(i * TC + u, 1), :], PS[:, 3 + u:4 + u, 0:MSG + HEADS], 0.0, None,
                                    ALU.add).then_inc(s["proj_kept"], 1)
            v.wait_ge(s["got_in"], 16 * GROUPS)
            v.tensor_tensor(got[:, :, :, 1], got[:, :, :, 1], item_node[:, :].unsqueeze(2).to_broadcast([P, GROUPS, P]),
                            ALU.subtract).then_inc(s["dloc_ready"], 1)
            v.wait_ge(s["proj_kept"], NT + FREE)
            a_src, a_dst = HN[:, :, D:MSG], HN[:, :, MSG:MSG + HEADS]
            v.tensor_reduce(amax[:, :], a_src.rearrange("p t h -> p h t"), AX.X, ALU.max).then_inc(s["amax_ready"], 1)
            step(v.tensor_copy(qn[:, :, 0:HEADS], a_dst))
            link(v.tensor_tensor(zs[:, :, :], a_src, a_dst, ALU.add))
            step(v.scalar_tensor_tensor(out=zs[:, :, :], in0=zs[:, :, :], scalar=SLOPE, in1=zs[:, :, :], op0=ALU.mult, op1=ALU.max))
            v.wait_ge(s["gmax_ready"], 1)
            link(v.tensor_tensor(zb[:, :, :], a_dst, gmax[:, :].unsqueeze(1).to_broadcast([P, NT, HEADS]), ALU.add))
            link(v.scalar_tensor_tensor(out=zb[:, :, :], in0=zb[:, :, :], scalar=SLOPE, in1=zb[:, :, :], op0=ALU.mult, op1=ALU.max))
            v.scalar_tensor_tensor(out=qn[:, :, HEADS:2 * HEADS], in0=zb[:, :, :], scalar=-HEADROOM, in1=zs[:, :, :],
                                   op0=ALU.add, op1=ALU.max).then_inc(s["shift_ready"], 1)
            v.wait_ge(s["shift_ready"], 1)
            v.tensor_tensor(zb[:, :, :], zs[:, :, :], qn[:, :, HEADS:2 * HEADS], ALU.subtract).then_inc(s["shift_ready"], 1)

            v.wait_ge(s["tileT_done"], 1)
            v.tensor_copy(tileT[:, :], PS[0:GROUPS, 3, 0:P]).then_inc(s["tileT_ready"], 1)

            heads = lambda a: a[:, :, 0:D].rearrange("p t (h f) -> p t h f", h=HEADS)
            of_head = lambda a: a.unsqueeze(3).to_broadcast([P, NT, HEADS, FH])
            den = A[:, :, D:MSG]
            v.wait_ge(s["exs_ready"], 1)
            step(v.tensor_tensor(heads(A), heads(HN), of_head(exs[:, :, :]), ALU.mult))
            link(v.tensor_copy(den, exs[:, :, :]))

            tile_regs = [v.alloc_register(f"dve_tile{u}") for u in range(BATCH)]

            def match(b, j, u):
                v.tensor_scalar(edge_node[j][:, u, :], iota[:, :], dloc[:, ds(b * BATCH + u, 1)], None,
                                ALU.is_equal).then_inc(s["edge_node_ready"], 1)

            def load_tiles(b):
                v.load(tile_regs, tiles[0:1, items(b)])
                return [v.snap(r, min_val=0, max_val=NT - 1) for r in tile_regs]

            def add_to_tile(b, u, t):
                v.wait_ge(s["tile_summed"], b * BATCH + (u + 1))
                if u or after(b, 1):
                    v.wait_ge(s["tile_added"], b * BATCH + u)
                v.tensor_tensor(A[:, ds(t[u], 1), :], PS[:, 4 + u:5 + u, 0:MSG], A[:, ds(t[u], 1), :],
                                ALU.add).then_inc(s["tile_added"], 1)

            def attention(b, j, n):
                h = j % 2
                v.wait_ge(gathered[j], n * (16 * BATCH) + 16 * BATCH)
                v.wait_ge(s["spread"], b + 1)
                e = ez[h][:, :, :]
                q = PS[:, 2 + h, 0:BATCH * 2 * HEADS].rearrange("p (u c) -> p u c", u=BATCH)
                t = load_tiles(b - 1) if after(b, 1) else None
                scores = (lambda: v.tensor_tensor(e, G[j][:, :, D:MSG], q[:, :, 0:HEADS], ALU.add),
                          lambda: v.scalar_tensor_tensor(out=e, in0=e, scalar=SLOPE, in1=e, op0=ALU.mult, op1=ALU.max),
                          lambda: v.tensor_tensor(e, e, q[:, :, HEADS:2 * HEADS], ALU.subtract),
                          lambda: v.tensor_scalar(e, e, CAP, None, ALU.min))
                for u in range(BATCH):
                    if u:
                        step.wait()
                    if u < BATCH - 1:
                        step(scores[u]())
                    else:
                        scores[u]().then_inc(s["ex_in"], 1)
                    for w in ((0, 1), (2,), (3,), ())[u]:
                        match(b + 2, (j + 2) % RING, w)
                    if t:
                        add_to_tile(b - 1, u, t)
                v.wait_ge(s["ex_out"], b + 1)
                for u in (0, 2):
                    m = G[j][:, u:u + 2, 0:D].rearrange("p u (h f) -> p u h f", h=HEADS)
                    v.tensor_tensor(m, m, G[j][:, u:u + 2, D:MSG].unsqueeze(3).to_broadcast([P, 2, HEADS, FH]),
                                    ALU.mult).then_inc(s["msg_ready"], 1)

            v.wait_ge(s["const_set"], 6)
            v.wait_ge(s["fields_kept"], 3)
            v.wait_ge(s["tiles_in"], 16)
            for b in range(2):
                for u in range(BATCH):
                    match(b, b, u)
            batches(v, attention, step, 3)
            t = load_tiles(NBATCH - 1)
            for u in range(BATCH):
                add_to_tile(NBATCH - 1, u, t)
            v.wait_ge(s["tile_added"], ITEMS)
            link(v.scalar_tensor_tensor(out=den, in0=exs[:, :, :], scalar=1e-16, in1=den, op0=ALU.mult, op1=ALU.add))
            link(v.reciprocal(den, den))
            link(v.tensor_tensor(heads(A), heads(A), of_head(den), ALU.mult))
            link(v.tensor_tensor(A[:, :, 0:D], A[:, :, 0:D], XN[:, :, :], ALU.add))
            each_tile(lambda t: stats(tile(A), t))
            scales()
            with v.Fori(0, NC) as i:
                apply_affine(i, tile(A))
                xi = X[:, ds(i * TC, TC), :]
                v.scalar_tensor_tensor(out=xi, in0=A[:, ds(i * TC, TC), 0:D], scalar=0.0, in1=xi, op0=ALU.max,
                                       op1=ALU.add).then_inc(s["gnn0_added"], 1)
                v.wait_ge(s["gnn0_added"], i + 1)
                for u in range(TC):
                    stats(tile(X), i * TC + u)
            norm_tiles[0] += NT
            centered[0] += NT

            scales()
            apply(tile(X), tile(XN))
            with v.Fori(0, NC) as i:
                step.begin(i, TC)
                for u in range(TC):
                    t = i * TC + u
                    step(v.scalar_tensor_tensor(out=Z[:, ds(t, 1), :], in0=XN[:, ds(t, 1), :], scalar=1.0,
                                                in1=rows[:, WRR:WRR + 1, :], op0=ALU.mult, op1=ALU.mult,
                                                accum_out=wl[:, ds(t, 1)]))
                step.end(NC)
            step.wait()
            v.tensor_scalar(wl[:, :], wl[:, :], small[:, 0:1], None, ALU.add).then_inc(s["wlog_ready"], 1)
            step(v.tensor_tensor(X[:, :, :], X[:, :, :], XN[:, :, :], ALU.add))
            link(v.memset(cnt[:, :, :], 0.0))
            v.wait_ge(s["wrow_in"], 16)
            wrow, scr = R3[:, 0:NPAD], R2[:, 0:NPAD]
            for t in range(NT):
                a, b = t * P, min(N, (t + 1) * P)
                w = wl[:, t:t + 1]
                if t:
                    link(v.tensor_scalar(scr[:, 0:a], wrow[:, 0:a], w, None, ALU.is_ge, ALU.add, accum_out=cnt[:, 0, t:t + 1]))
                link(v.tensor_scalar(scr[:, a:N], wrow[:, a:N], w, None, ALU.is_gt, ALU.add, accum_out=cnt[:, 1, t:t + 1]))
                link(v.scalar_tensor_tensor(out=scr[:, a:b], in0=wrow[:, a:b], scalar=w, in1=lower[:, 0:b - a],
                                            op0=ALU.is_equal, op1=ALU.mult, accum_out=cnt[:, 2, t:t + 1]))
            link(v.tensor_tensor(cnt[:, 0, :], cnt[:, 0, :], cnt[:, 1, :], ALU.add))
            link(v.tensor_tensor(cnt[:, 0, :], cnt[:, 0, :], cnt[:, 2, :], ALU.add))
            link(v.scalar_tensor_tensor(out=wm[:, :], in0=cnt[:, 0, :], scalar=float(KEPT), in1=wl[:, :],
                                        op0=ALU.is_lt, op1=ALU.mult))

            def stats_after(t):
                v.wait_ge(s["x_added"], t + 1)
                stats(tile(X), t)

            with v.Fori(0, NC) as i:
                for u in range(TC):
                    t = i * TC + u
                    yt = Y[:, ds(t, 1), :]
                    v.wait_ge(s["y_kept"], t + (1 + FREE))
                    v.tensor_tensor(yt, yt, rows[:, B2R:B2R + 1, :], ALU.add).then_inc(s["y_biased"], 1)
                    if u:
                        stats_after(t - 1)
                    v.wait_ge(s["y_biased"], t + 1)
                    v.scalar_tensor_tensor(out=X[:, ds(t, 1), :], in0=yt, scalar=wm[:, ds(t, 1)],
                                           in1=X[:, ds(t, 1), :], op0=ALU.mult, op1=ALU.add).then_inc(s["x_added"], 1)
                stats_after(i * TC + (TC - 1))
            v.wait_ge(s["x_added"], NT)

            scales()
            v.scalar_tensor_tensor(out=t1[:, :], in0=mean[:, :], scalar=-1.0, in1=rstd[:, :], op0=ALU.mult,
                                   op1=ALU.mult).then_inc(s["norm_shift"], 1)
            each_tile(lambda t: v.tensor_scalar(XN[:, ds(t, 1), :], X[:, ds(t, 1), :], mean[:, ds(t, 1)],
                                                rstd[:, ds(t, 1)], ALU.subtract, ALU.mult).then_inc(s["norm_done"], 1),
                      0, NT - ACT_TILES)
            v.wait_ge(s["norm_done"], 4 * NT)
            norm_tiles[0] += NT

            def sum_by_source(b, j, n):
                h = j % 2
                v.wait_ge(s["rowed"], b + 1)
                if after(b, 2):
                    v.wait_ge(s["node_src_done"], b - 1)
                    v.wait_ge(s["row_ready"], b - 1)
                step(v.tensor_tensor(same[h], PS[:, h, :].rearrange("p (u e) -> p u e", u=BATCH),
                                     key[j][:, :].unsqueeze(2).to_broadcast([P, BATCH, P]), ALU.is_equal))
                for u in range(BATCH):
                    step(v.scalar_tensor_tensor(out=earlier[:, u, :], in0=PS[:, h, u * P:(u + 1) * P], scalar=key[j][:, u:u + 1],
                                                in1=lower[:, :], op0=ALU.is_equal, op1=ALU.mult, accum_out=es[:, h, 0, u:u + 1]))
                for u in range(BATCH):
                    c = ds(b * BATCH + u, 1)
                    mm = v.tensor_scalar(weight_node[h][:, u, :], iota[:, :], dloc[:, c], ewT[:, c], ALU.is_equal, ALU.mult)
                mm.then_inc(s["weights_ready"], 1)
                step(v.tensor_scalar(es[:, h, 1, :], key[j][:, :], -1.0, spare_row[:, 0:1], ALU.mult, ALU.add))
                link(v.tensor_tensor(es[:, h, 2, :], key[j][:, :], table_of[:, :], ALU.add))
                link(v.scalar_tensor_tensor(out=es[:, h, 1, :], in0=es[:, h, 0, :], scalar=1.0, in1=es[:, h, 1, :], op0=ALU.min, op1=ALU.mult))
                if after(b, RING):
                    for u in range(BATCH):
                        v.wait_ge(added[u], (b - (RING - 1)) * 16)
                v.tensor_tensor(rowid[j][:, :], es[:, h, 1, :], es[:, h, 2, :], ALU.add).then_inc(s["row_ready"], 1)

            batches(v, sum_by_source, step, 8)
            link(v.tensor_scalar(small[:, 3:4], small[:, 1:2], 1.0, None, ALU.add))
            for c in range(NC):
                z = Z[:, c * TC:(c + 1) * TC, :]
                v.wait_ge(sums_in[c % 2], 16 * TABLES * (c // 2 + 1))
                for u in range(TABLES - 1):
                    ins = v.tensor_tensor(z, z, part_sums[c % 2][:, u, :, :], ALU.add)
                    if u < TABLES - 2:
                        link(ins)
                ins.then_inc(s["table_added"], 1)
                v.wait_ge(s["table_added"], c + 1)
                v.wait_ge(s["xt_read"], NC * 2 + c + FREE)
                v.scalar_tensor_tensor(out=xc[:, :, :], in0=XN[:, c * TC:(c + 1) * TC, :], scalar=small[:, 3:4], in1=z,
                                       op0=ALU.mult, op1=ALU.add).then_inc(s["xc_ready"], 1)

            def node_stats(of, kept):
                def part(i, g, width):
                    m, half = g // 2, g % 2
                    v.wait_ge(s[kept], i * 4 + (g + 1 + FREE))
                    v.bn_stats(bst[:, m, ds(i * 2 + half, 1), :],
                               of[:, m:m + 1, ds(i * CW + half * HALF, width)]).then_inc(s["node_stat"], 1)

                with v.Fori(0, NC - 1) as i:
                    for g in range(4):
                        part(i, g, HALF)
                for g in range(4):
                    part(NC - 1, g, min(HALF, N - (NC - 1) * CW - g % 2 * HALF))

            def batch_norm(n, g, be):
                v.wait_ge(s["node_stat"], n * 4 * NC)
                for m in range(KD):
                    v.bn_aggr(bmv[:, m, :], bst[:, m, :, :].rearrange("p j c -> p (j c)")).then_inc(s["bnv_ready"], 1)
                v.wait_ge(s["bnstd_ready"], n)
                v.wait_ge(s["bnv_ready"], KD * n)
                link(v.reciprocal(bsc[:, 0, :], bsc[:, 0, :]))
                link(v.tensor_tensor(bsc[:, 1, :], bsc[:, 0, :], gcol[:, g, :], ALU.mult))
                link(v.tensor_tensor(bsc[:, 2, :], bmv[:, :, 0], bsc[:, 1, :], ALU.mult))
                v.tensor_tensor(bsc[:, 2, :], gcol[:, be, :], bsc[:, 2, :], ALU.subtract).then_inc(s["bn_ready"], 1)

            v.wait_ge(s["gw_in"], 16 * 8)
            node_stats(H1, "h1_kept")
            batch_norm(1, 1, 2)
            node_stats(H2, "h2_kept")
            batch_norm(2, 4, 5)
            for c in range(NC):
                xi = X[:, c * TC:(c + 1) * TC, :]
                v.wait_ge(s["back_done"], c + 1 + FREE)
                v.tensor_tensor(xi, xi, PSF[:, c % 2 * BACK:c % 2 * BACK + TC * D].rearrange("p (t c) -> p t c", t=TC),
                                ALU.add).then_inc(s["back_added"], 1)
                v.wait_ge(s["back_added"], c + 1 + FREE)
                for u in range(TC):
                    stats(tile(X), c * TC + u)

            scales()
            apply(tile(X), tile(XN))
            v.wait_ge(s["mean_done"], 1)
            v.tensor_scalar(mrow[:, :], PS[0:1, 7, 0:D], 1.0 / N, None, ALU.mult).then_inc(s["mrow_ready"], 1)
            v.wait_ge(s["mcol_done"], 1)
            v.tensor_copy(mcol[:, :], PS[:, 6, 0:KD]).then_inc(s["mcol_ready"], 1)
            v.wait_ge(s["logit_done"], 1)
            v.wait_ge(s["r1_in"], 32)
            link(v.tensor_tensor(rt[:, 0, :], PS[0:1, 7, 0:EXPERTS], bre[:, :], ALU.add))

            def softmax(n, of, ex, to, w):
                link(v.tensor_reduce(r1[:, 0:1], rt[:, of, 0:w], AX.X, ALU.max))
                v.tensor_scalar(r1[:, 1:2], r1[:, 0:1], -1.0, None, ALU.mult).then_inc(s["rexp_in"], 1)
                v.wait_ge(s["rexp_out"], n)
                link(v.tensor_reduce(r1[:, 2:3], rt[:, ex, 0:w], AX.X, ALU.add))
                link(v.reciprocal(r1[:, 3:4], r1[:, 2:3]))
                return v.tensor_scalar(rt[:, to, 0:w], rt[:, ex, 0:w], r1[:, 3:4], None, ALU.mult)

            link(softmax(1, 0, 1, 2, EXPERTS))
            link(v.tensor_scalar(rt[:, 3, :], rt[:, 2, :], float(N), 1e-30, ALU.mult, ALU.max))
            link(v.reciprocal(rt[:, 3, :], rt[:, 3, :]))
            link(v.tensor_scalar(rt[:, 3, :], rt[:, 3, :], CAPACITY, 1.0, ALU.mult, ALU.min))
            link(v.tensor_tensor(rt[:, 4, :], rt[:, 2, :], rt[:, 3, :], ALU.mult))
            link(softmax(2, 4, 5, 6, EXPERTS))
            v.max(rt[:, 7, :], rt[:, 6, :]).then_inc(s["pair_ready"], 1)
            v.wait_ge(s["pair_ready"], 1)
            v.max_index(ri[:, :], rt[:, 7, :], rt[:, 6, :]).then_inc(s["pair_ready"], 1)
            softmax(3, 7, 8, 9, 2).then_inc(s["pairw_ready"], 1)
            v.wait_ge(s["wb_done"], 1)
            link(v.tensor_copy(wexp[:, :], PS[:, 6, 0:2]))
            v.wait_ge(s["expert_b2_in"], 64)
            link(v.tensor_scalar(rows[:, B2R, :], rows[:, B2R, :], wexp[:, 0:1], None, ALU.mult))
            link(v.scalar_tensor_tensor(out=rows[:, B2R, :], in0=rows[:, B2B, :], scalar=wexp[:, 1:2], in1=rows[:, B2R, :],
                                        op0=ALU.mult, op1=ALU.add))
            v.wait_ge(s["expert_w2_in"], 32)
            for j in range(2):
                wj = w2s[:, j * MH // 2:(j + 1) * MH // 2, :]
                v.tensor_scalar(wj, wj, wexp[:, j:j + 1], None, ALU.mult).then_inc(s["w2_scaled"], 1)
            link(v.tensor_tensor(Z, XN[:, :, :], row(B2R), ALU.add))

            def add_y(i):
                for u in range(TC):
                    t = i * TC + u
                    v.wait_ge(s["y_done"], t + (NT + 1))
                    v.tensor_tensor(Z[:, ds(t, 1), :], PS[:, 5 + u % 3:6 + u % 3, 0:D], Z[:, ds(t, 1), :],
                                    ALU.add).then_inc(s["y_kept"], 1)
                for u in range(TC):
                    t = i * TC + u
                    v.wait_ge(s["y_kept"], t + (NT + 1 + FREE))
                    stats(tile(Z), t)

            def finish(lo, hi):
                scales(lo, hi)
                with v.Fori(lo // TC, hi // TC) as i:
                    apply_affine(i, tile(Z))
                v.tensor_tensor(X[:, lo:hi, :], Z[:, lo:hi, :], X[:, lo:hi, :], ALU.add).then_inc(s["out_ready"], 1)

            with v.Fori(0, NC - 1) as i:
                add_y(i)
            finish(0, (NC - 1) * TC)
            add_y(NC - 1)
            finish((NC - 1) * TC, NT)


_INS = ["x", "src", "dst", "edge_weight", "L0_gnn_W", "L0_gnn_att_src", "L0_gnn_att_dst", "L0_gnn_bias",
        "L0_gnn_ln_gamma", "L0_gnn_ln_beta", "L0_ffn_wr", "L0_ffn_br", "L0_ffn_w1", "L0_ffn_b1", "L0_ffn_w2",
        "L0_ffn_b2", "L1_gnn_eps", "L1_gnn_W1", "L1_gnn_b1", "L1_gnn_g1", "L1_gnn_be1", "L1_gnn_W2", "L1_gnn_b2",
        "L1_gnn_g2", "L1_gnn_be2", "L1_ffn_Wr", "L1_ffn_br", "L1_ffn_W1", "L1_ffn_b1", "L1_ffn_W2", "L1_ffn_b2",
        "L1_ffn_gamma", "L1_ffn_beta"]


def kernel(**inputs):
    import numpy as _np
    import concourse.bacc as _bacc
    from concourse import mybir as _mybir
    from concourse.bass_utils import run_bass_kernel_spmd as _run

    nc = _bacc.Bacc("TRN2", target_bir_lowering=False, num_devices=1)
    arrays, args = {}, []
    for name in _INS:
        a = _np.ascontiguousarray(inputs[name])
        arrays[f"in_{name}_dram"] = a
        args.append(nc.dram_tensor(f"in_{name}_dram", a.shape, _mybir.dt.from_np(a.dtype), kind="ExternalInput").ap())
    args.append(nc.dram_tensor("out_dram", (N, D), F32, kind="ExternalOutput").ap())
    build(nc, *args)
    r = _run(nc, [arrays], core_ids=[0])
    return r.results[0]["out_dram"]
```
